# Optimizing a Trainium2 kernel written in Bass

```python
import numpy as np
import jax
import jax.numpy as jnp

def _softmax(x, axis=-1):
    return jax.nn.softmax(x, axis=axis)

def _gelu(x):
    return jax.nn.gelu(x, approximate=True)

def _silu(x):
    return jax.nn.silu(x)

def _sigmoid(x):
    return jax.nn.sigmoid(x)

def _layernorm(x, axis=-1, eps=1e-05):
    m = jnp.mean(x, axis=axis, keepdims=True)
    v = jnp.var(x, axis=axis, keepdims=True)
    return (x - m) / jnp.sqrt(v + eps)

def _scatter_add(tgt, idx, src, axis=0):
    return tgt.at[idx].add(src)

def _segment_sum(src, seg, n):
    return jax.ops.segment_sum(src, seg, n)
kernel_name = 'mk_xattn_ffn_d4_seqx_r8_f13c59'

def setup_inputs(seed: int=0):
    np.random.seed(seed)
    _w = jnp.asarray

    def _rec_inputs():
        import jax
        import jax.numpy as jnp
        _rk = jax.random.key(seed)
        x = -0.0002928 + 1 * jax.random.normal(jax.random.fold_in(_rk, 1), (8, 256, 128), jnp.float32)
        _lenS = 256 - jax.random.randint(jax.random.fold_in(_rk, 7), (8,), 0, max(1, 256 // 4) + 1, jnp.int32)
        _lenS2 = 256 - jax.random.randint(jax.random.fold_in(_rk, 8), (8,), 0, max(1, 256 // 4) + 1, jnp.int32)
        _ctx_1024P = jax.random.normal(jax.random.fold_in(_rk, 11), (8, 16, 128), jnp.float32)
        _ctx_1024c = jax.random.dirichlet(jax.random.fold_in(_rk, 511), 0.3 * jnp.ones((16,), jnp.float32), (8, 256))
        _ctx_1024t = jnp.einsum('bsk,bkd->bsd', _ctx_1024c, _ctx_1024P)
        _ctx_1024t = _ctx_1024t * jax.lax.rsqrt(jnp.mean(jnp.square(_ctx_1024t)) + 1e-12) * 0.953939
        ctx_1024 = -1.39393e-06 + 0.999914 * (_ctx_1024t + 0.3 * jax.random.normal(jax.random.fold_in(_rk, 611), (8, 256, 128), jnp.float32))
        _validS = jnp.arange(256)[None, :] < _lenS[:, None]
        _validS2 = jnp.arange(256)[None, :] < _lenS2[:, None]
        _causal = jnp.tril(jnp.ones((256, 256), dtype=bool))
        mask_BxS2_ik0 = jnp.where(jnp.broadcast_to(_validS2[:, :], (8, 256)), 0, 1).astype(jnp.int32)
        mask_BxS2_bk0 = jnp.logical_not(jnp.broadcast_to(_validS2[:, :], (8, 256)))
        return (x, ctx_1024, mask_BxS2_ik0, mask_BxS2_bk0)
    x, ctx_1024, mask_BxS2_ik0, mask_BxS2_bk0 = _rec_inputs()

    def _L0_xattn_setup():
        import jax, jax.numpy as jnp
        import numpy as np
        SCALE_BASE = 512.0
        GN_EPS = 1e-05

        def _xpos(x, downscale):
            L, D = (x.shape[-2], x.shape[-1])
            half = D // 2
            base = (jnp.arange(0, D, 2, dtype=jnp.float32) + 0.4 * D) / (1.4 * D)
            min_pos = -(L // 2)
            power = (jnp.arange(min_pos, min_pos + L, dtype=jnp.float32) / SCALE_BASE)[:, None]
            scale = base[None, :] ** power
            inv_freq = 1.0 / 10000.0 ** (jnp.arange(half, dtype=jnp.float32) / half)
            ang = jnp.arange(L, dtype=jnp.float32)[:, None] * inv_freq[None, :]
            sin, cos = (jnp.sin(ang), jnp.cos(ang))
            if downscale:
                scale = 1.0 / scale
            sin_s = jnp.repeat(sin * scale, 2, axis=-1)
            cos_s = jnp.repeat(cos * scale, 2, axis=-1)
            x1, x2 = (x[..., ::2], x[..., 1::2])
            rot = jnp.stack((-x2, x1), axis=-1).reshape(x.shape)
            return x * cos_s + rot * sin_s

        def _decay_mask(L, H):
            gammas = 1.0 - jnp.exp(jnp.linspace(np.log(1.0 / 32.0), np.log(1.0 / 512.0), H)).astype(jnp.float32)
            idx = jnp.arange(L)
            dist = idx[:, None] - idx[None, :]
            causal = dist >= 0
            d = jnp.maximum(dist, 0).astype(jnp.float32)
            return jnp.where(causal[None], gammas[:, None, None] ** d[None], 0.0)
        key = jax.random.key(seed)
        ks = jax.random.split(key, 9)
        B, L, D, H = (2, 256, 128, 16)
        hd = D // H
        return {'query': jax.random.normal(ks[0], (B, L, D), jnp.float32), 'key': jax.random.normal(ks[1], (B, L, D), jnp.float32), 'value': jax.random.normal(ks[2], (B, L, D), jnp.float32), 'W_Q': jax.random.normal(ks[3], (H, D, hd), jnp.float32) / D, 'W_K': jax.random.normal(ks[4], (H, D, hd), jnp.float32) / D, 'W_V': jax.random.normal(ks[5], (H, D, hd), jnp.float32) / D, 'g_w': jax.random.normal(ks[6], (D, D), jnp.float32) * (2.0 / (D + D)) ** 0.5, 'g_b': jnp.zeros((D,), jnp.float32), 'out_w': jax.random.normal(ks[7], (D, D), jnp.float32) * (2.0 / (D + D)) ** 0.5, 'out_b': jnp.zeros((D,), jnp.float32)}
    _L0_xattn_all = _L0_xattn_setup()
    _L0_xattn_in = {k: v for k, v in _L0_xattn_all.items() if k in ('W_Q', 'W_K', 'W_V', 'g_w', 'g_b', 'out_w', 'out_b')}
    del _L0_xattn_all

    def _L0_ffn_setup():
        import jax, jax.numpy as jnp
        import numpy as np
        D_MODEL = 128
        FF_DIM = 4 * D_MODEL
        NUM_EXPERTS = 8
        TOP_K = 2
        B, L = (4, 256)
        key = jax.random.key(seed)
        ks = jax.random.split(key, 7)
        s_in = 1.0 / np.sqrt(D_MODEL)
        s_ff = 1.0 / np.sqrt(FF_DIM)
        return {'x': jax.random.normal(ks[0], (B, L, D_MODEL), dtype=jnp.float32), 'router_w': jax.random.uniform(ks[1], (NUM_EXPERTS, D_MODEL), jnp.float32, -s_in, s_in), 'router_b': jax.random.uniform(ks[2], (NUM_EXPERTS,), jnp.float32, -s_in, s_in), 'w1': jax.random.uniform(ks[3], (NUM_EXPERTS, FF_DIM, D_MODEL), jnp.float32, -s_in, s_in), 'b1': jax.random.uniform(ks[4], (NUM_EXPERTS, FF_DIM), jnp.float32, -s_in, s_in), 'w2': jax.random.uniform(ks[5], (NUM_EXPERTS, D_MODEL, FF_DIM), jnp.float32, -s_ff, s_ff), 'b2': jax.random.uniform(ks[6], (NUM_EXPERTS, D_MODEL), jnp.float32, -s_ff, s_ff)}
    _L0_ffn_all = _L0_ffn_setup()
    _L0_ffn_in = {k: v for k, v in _L0_ffn_all.items() if k in ('router_w', 'router_b', 'w1', 'b1', 'w2', 'b2')}
    del _L0_ffn_all

    def _L1_xattn_setup():
        import jax, jax.numpy as jnp
        import numpy as np
        B, C_LEN, Q_LEN, D = (8, 256, 64, 128)
        key = jax.random.key(seed)
        ks = jax.random.split(key, 10)
        scale = 1.0 / np.sqrt(D)
        return {'c': jax.random.normal(ks[0], (B, C_LEN, D), dtype=jnp.float32), 'q': jax.random.normal(ks[1], (B, Q_LEN, D), dtype=jnp.float32), 'w_cq': jax.random.normal(ks[2], (D,), dtype=jnp.float32) * scale, 'b_cq': jax.random.normal(ks[3], (), dtype=jnp.float32) * scale, 'w_c': jax.random.normal(ks[4], (D,), dtype=jnp.float32) * scale, 'b_c': jax.random.normal(ks[5], (), dtype=jnp.float32) * scale, 'w_q': jax.random.normal(ks[6], (D,), dtype=jnp.float32) * scale, 'b_q': jax.random.normal(ks[7], (), dtype=jnp.float32) * scale, 'W_l': jax.random.normal(ks[8], (D, 4 * D), dtype=jnp.float32) * (1.0 / np.sqrt(4 * D)), 'b_l': jax.random.normal(ks[9], (D,), dtype=jnp.float32) * (1.0 / np.sqrt(4 * D))}
    _L1_xattn_all = _L1_xattn_setup()
    _L1_xattn_in = {k: v for k, v in _L1_xattn_all.items() if k in ('w_cq', 'b_cq', 'w_c', 'b_c', 'w_q', 'b_q', 'W_l', 'b_l')}
    del _L1_xattn_all

    def _L1_ffn_setup():
        import jax, jax.numpy as jnp
        import numpy as np
        DIM = 128
        HID = 512
        NUM_EXPERTS = 8
        TOP_K = 2
        ALPHA = 2.0
        B, S = (4, 256)

        def _swiglu(x, wu, wg, wd):
            up = x @ wu
            g = x @ wg
            gate = jax.nn.sigmoid(g) * g
            return up * gate @ wd
        key = jax.random.key(seed)
        ks = jax.random.split(key, 8)
        x = jax.random.normal(ks[0], (B, S, DIM), dtype=jnp.float32)
        Wr = jax.random.normal(ks[1], (DIM, NUM_EXPERTS), dtype=jnp.float32) * 0.02
        Wu = jax.random.normal(ks[2], (NUM_EXPERTS - 1, DIM, HID), dtype=jnp.float32) * 0.02
        Wg = jax.random.normal(ks[3], (NUM_EXPERTS - 1, DIM, HID), dtype=jnp.float32) * 0.02
        Wd = jax.random.normal(ks[4], (NUM_EXPERTS - 1, HID, DIM), dtype=jnp.float32) * 0.002
        Wu_s = jax.random.normal(ks[5], (DIM, HID), dtype=jnp.float32) * 0.02
        Wg_s = jax.random.normal(ks[6], (DIM, HID), dtype=jnp.float32) * 0.02
        Wd_s = jax.random.normal(ks[7], (HID, DIM), dtype=jnp.float32) * 0.002
        return {'x': x, 'Wr': Wr, 'Wu': Wu, 'Wg': Wg, 'Wd': Wd, 'Wu_s': Wu_s, 'Wg_s': Wg_s, 'Wd_s': Wd_s}
    _L1_ffn_all = _L1_ffn_setup()
    _L1_ffn_in = {k: v for k, v in _L1_ffn_all.items() if k in ('Wr', 'Wu', 'Wg', 'Wd', 'Wu_s', 'Wg_s', 'Wd_s')}
    del _L1_ffn_all

    def _L2_xattn_setup():
        import jax, jax.numpy as jnp
        import numpy as np
        D_MODEL = 128
        NUM_HEADS = 16
        D_K = D_MODEL // NUM_HEADS
        key = jax.random.key(seed)
        ks = jax.random.split(key, 13)
        B, S = (2, 256)
        s = 1.0 / np.sqrt(D_MODEL)
        inp = {'q': jax.random.normal(ks[0], (B, S, D_MODEL), jnp.float32), 'k': jax.random.normal(ks[1], (B, S, D_MODEL), jnp.float32), 'v': jax.random.normal(ks[2], (B, S, D_MODEL), jnp.float32), 'mask': jax.random.randint(ks[3], (B, S), 0, 2, jnp.int32), 'Wq': jax.random.normal(ks[4], (D_MODEL, D_MODEL), jnp.float32) * s, 'bq': jax.random.normal(ks[5], (D_MODEL,), jnp.float32) * s, 'Wk': jax.random.normal(ks[6], (D_MODEL, D_MODEL), jnp.float32) * s, 'bk': jax.random.normal(ks[7], (D_MODEL,), jnp.float32) * s, 'Wv': jax.random.normal(ks[8], (D_MODEL, D_MODEL), jnp.float32) * s, 'bv': jax.random.normal(ks[9], (D_MODEL,), jnp.float32) * s, 'Wo': jax.random.normal(ks[10], (D_MODEL, D_MODEL), jnp.float32) * s, 'bo': jax.random.normal(ks[11], (D_MODEL,), jnp.float32) * s}
        return inp
    _L2_xattn_all = _L2_xattn_setup()
    _L2_xattn_in = {k: v for k, v in _L2_xattn_all.items() if k in ('Wq', 'bq', 'Wk', 'bk', 'Wv', 'bv', 'Wo', 'bo')}
    del _L2_xattn_all

    def _L2_ffn_setup():
        import jax, jax.numpy as jnp
        import numpy as np
        B, S, D_MODEL, D_HIDDEN = (4, 256, 128, 512)

        def act_quant(x):
            scale = 127.0 / jnp.clip(jnp.max(jnp.abs(x), axis=-1, keepdims=True), 1e-05)
            return jnp.clip(jnp.round(x * scale), -128, 127) / scale

        def weight_quant(w):
            scale = 1.0 / jnp.clip(jnp.mean(jnp.abs(w)), 1e-05)
            return jnp.clip(jnp.round(w * scale), -1, 1) / scale

        def bit_linear(x, w):
            xq = x + jax.lax.stop_gradient(act_quant(x) - x)
            wq = w + jax.lax.stop_gradient(weight_quant(w) - w)
            return jnp.einsum('bsd,hd->bsh', xq, wq)

        def depthwise_conv1d(x_bcl, w, b):
            y = jax.lax.conv_general_dilated(x_bcl, w, window_strides=(1,), padding=[(1, 1)], dimension_numbers=('NCH', 'OIH', 'NCH'), feature_group_count=x_bcl.shape[1])
            return y + b[None, :, None]
        key = jax.random.key(seed)
        ks = jax.random.split(key, 5)
        lim1 = 1.0 / np.sqrt(D_MODEL)
        lim2 = 1.0 / np.sqrt(D_HIDDEN)
        limc = 1.0 / np.sqrt(3.0)
        return {'x': jax.random.normal(ks[0], (B, S, D_MODEL), dtype=jnp.float32), 'w1': jax.random.uniform(ks[1], (D_HIDDEN, D_MODEL), jnp.float32, -lim1, lim1), 'conv_w': jax.random.uniform(ks[2], (D_HIDDEN, 1, 3), jnp.float32, -limc, limc), 'conv_b': jax.random.uniform(ks[3], (D_HIDDEN,), jnp.float32, -limc, limc), 'w2': jax.random.uniform(ks[4], (D_MODEL, D_HIDDEN), jnp.float32, -lim2, lim2)}
    _L2_ffn_all = _L2_ffn_setup()
    _L2_ffn_in = {k: v for k, v in _L2_ffn_all.items() if k in ('w1', 'conv_w', 'conv_b', 'w2')}
    del _L2_ffn_all

    def _L3_xattn_setup():
        import jax, jax.numpy as jnp
        import numpy as np
        DIM, DIM_HEAD, HEADS, SCALE = (128, 64, 8, 8.0)
        INNER = DIM_HEAD * HEADS
        LN_EPS = 1e-05
        L2_EPS = 1e-12

        def layer_norm(x, w, b):
            mu = jnp.mean(x, axis=-1, keepdims=True)
            var = jnp.mean(jnp.square(x - mu), axis=-1, keepdims=True)
            return (x - mu) * jax.lax.rsqrt(var + LN_EPS) * w + b

        def l2norm(t):
            n = jnp.sqrt(jnp.sum(jnp.square(t), axis=-1, keepdims=True))
            return t / jnp.maximum(n, L2_EPS)
        key = jax.random.key(seed)
        ks = jax.random.split(key, 8)
        b, n, m = (8, 1024, 64)
        x = jax.random.normal(ks[0], (b, n, DIM), dtype=jnp.float32)
        latents = jax.random.normal(ks[1], (b, m, DIM), dtype=jnp.float32)
        mask = jax.random.randint(ks[2], (b, n), 0, 2) > 0
        Wq = jax.random.normal(ks[3], (DIM, INNER), dtype=jnp.float32) * DIM ** (-0.5)
        Wkv = jax.random.normal(ks[4], (DIM, 2 * INNER), dtype=jnp.float32) * DIM ** (-0.5)
        Wo = jax.random.normal(ks[5], (INNER, DIM), dtype=jnp.float32) * INNER ** (-0.5)
        return {'x': x, 'latents': latents, 'mask': mask, 'ln_x_w': jnp.ones((DIM,)), 'ln_x_b': jnp.zeros((DIM,)), 'ln_l_w': jnp.ones((DIM,)), 'ln_l_b': jnp.zeros((DIM,)), 'Wq': Wq, 'Wkv': Wkv, 'q_scale': jnp.ones((DIM_HEAD,)), 'k_scale': jnp.ones((DIM_HEAD,)), 'Wo': Wo, 'ln_o_w': jnp.ones((DIM,)), 'ln_o_b': jnp.zeros((DIM,))}
    _L3_xattn_all = _L3_xattn_setup()
    _L3_xattn_in = {k: v for k, v in _L3_xattn_all.items() if k in ('ln_x_w', 'ln_x_b', 'ln_l_w', 'ln_l_b', 'Wq', 'Wkv', 'q_scale', 'k_scale', 'Wo', 'ln_o_w', 'ln_o_b')}
    del _L3_xattn_all

    def _L3_ffn_setup():
        import jax, jax.numpy as jnp
        from jax import lax
        import numpy as np
        D_MODEL = 128
        HIDDEN = 64
        N_EXPERTS = 32
        TOP_K = 2
        B, S = (1, 512)

        def _moe_group(x2, router_w, wg, wu, wd, top_k):
            T = x2.shape[0]
            n_experts = router_w.shape[1]
            logits = x2 @ router_w
            scores = jax.nn.softmax(logits, axis=-1)
            expert_weights, expert_indices = lax.top_k(scores, top_k)
            flat_e = expert_indices.reshape(-1)
            flat_w = expert_weights.reshape(-1)
            flat_t = jnp.repeat(jnp.arange(T), top_k)
            order = jnp.argsort(flat_e)
            tok = flat_t[order]
            xs = x2[tok]
            group_sizes = jnp.bincount(flat_e, length=n_experts).astype(jnp.int32)
            gate = lax.ragged_dot(xs, wg, group_sizes)
            up = lax.ragged_dot(xs, wu, group_sizes)
            ys = lax.ragged_dot(jax.nn.silu(gate) * up, wd, group_sizes)
            ys = ys * flat_w[order][:, None]
            return jnp.zeros_like(x2).at[tok].add(ys)
        key = jax.random.key(seed)
        ks = jax.random.split(key, 9)
        w = lambda k, shape: jax.random.normal(k, shape, dtype=jnp.float32) * 0.02
        return {'x': jax.random.normal(ks[0], (B, S, D_MODEL), dtype=jnp.float32), 'router_w0': w(ks[1], (D_MODEL, N_EXPERTS)), 'wg0': w(ks[2], (N_EXPERTS, D_MODEL, HIDDEN)), 'wu0': w(ks[3], (N_EXPERTS, D_MODEL, HIDDEN)), 'wd0': w(ks[4], (N_EXPERTS, HIDDEN, D_MODEL)), 'router_w1': w(ks[5], (D_MODEL, N_EXPERTS)), 'wg1': w(ks[6], (N_EXPERTS, D_MODEL, HIDDEN)), 'wu1': w(ks[7], (N_EXPERTS, D_MODEL, HIDDEN)), 'wd1': w(ks[8], (N_EXPERTS, HIDDEN, D_MODEL))}
    _L3_ffn_all = _L3_ffn_setup()
    _L3_ffn_in = {k: v for k, v in _L3_ffn_all.items() if k in ('router_w0', 'wg0', 'wu0', 'wd0', 'router_w1', 'wg1', 'wu1', 'wd1')}
    del _L3_ffn_all
    return {'x': x, 'ctx_1024': ctx_1024, 'mask_BxS2_ik0': mask_BxS2_ik0, 'mask_BxS2_bk0': mask_BxS2_bk0, 'L0_xattn_W_Q': _L0_xattn_in['W_Q'], 'L0_xattn_W_K': _L0_xattn_in['W_K'], 'L0_xattn_W_V': _L0_xattn_in['W_V'], 'L0_xattn_g_w': _L0_xattn_in['g_w'], 'L0_xattn_g_b': _L0_xattn_in['g_b'], 'L0_xattn_out_w': _L0_xattn_in['out_w'], 'L0_xattn_out_b': _L0_xattn_in['out_b'], 'L0_ffn_router_w': _L0_ffn_in['router_w'], 'L0_ffn_router_b': _L0_ffn_in['router_b'], 'L0_ffn_w1': _L0_ffn_in['w1'], 'L0_ffn_b1': _L0_ffn_in['b1'], 'L0_ffn_w2': _L0_ffn_in['w2'], 'L0_ffn_b2': _L0_ffn_in['b2'], 'L1_xattn_w_cq': _L1_xattn_in['w_cq'], 'L1_xattn_b_cq': _L1_xattn_in['b_cq'], 'L1_xattn_w_c': _L1_xattn_in['w_c'], 'L1_xattn_b_c': _L1_xattn_in['b_c'], 'L1_xattn_w_q': _L1_xattn_in['w_q'], 'L1_xattn_b_q': _L1_xattn_in['b_q'], 'L1_xattn_W_l': _L1_xattn_in['W_l'], 'L1_xattn_b_l': _L1_xattn_in['b_l'], 'L1_ffn_Wr': _L1_ffn_in['Wr'], 'L1_ffn_Wu': _L1_ffn_in['Wu'], 'L1_ffn_Wg': _L1_ffn_in['Wg'], 'L1_ffn_Wd': _L1_ffn_in['Wd'], 'L1_ffn_Wu_s': _L1_ffn_in['Wu_s'], 'L1_ffn_Wg_s': _L1_ffn_in['Wg_s'], 'L1_ffn_Wd_s': _L1_ffn_in['Wd_s'], 'L2_xattn_Wq': _L2_xattn_in['Wq'], 'L2_xattn_bq': _L2_xattn_in['bq'], 'L2_xattn_Wk': _L2_xattn_in['Wk'], 'L2_xattn_bk': _L2_xattn_in['bk'], 'L2_xattn_Wv': _L2_xattn_in['Wv'], 'L2_xattn_bv': _L2_xattn_in['bv'], 'L2_xattn_Wo': _L2_xattn_in['Wo'], 'L2_xattn_bo': _L2_xattn_in['bo'], 'L2_ffn_w1': _L2_ffn_in['w1'], 'L2_ffn_conv_w': _L2_ffn_in['conv_w'], 'L2_ffn_conv_b': _L2_ffn_in['conv_b'], 'L2_ffn_w2': _L2_ffn_in['w2'], 'L3_xattn_ln_x_w': _L3_xattn_in['ln_x_w'], 'L3_xattn_ln_x_b': _L3_xattn_in['ln_x_b'], 'L3_xattn_ln_l_w': _L3_xattn_in['ln_l_w'], 'L3_xattn_ln_l_b': _L3_xattn_in['ln_l_b'], 'L3_xattn_Wq': _L3_xattn_in['Wq'], 'L3_xattn_Wkv': _L3_xattn_in['Wkv'], 'L3_xattn_q_scale': _L3_xattn_in['q_scale'], 'L3_xattn_k_scale': _L3_xattn_in['k_scale'], 'L3_xattn_Wo': _L3_xattn_in['Wo'], 'L3_xattn_ln_o_w': _L3_xattn_in['ln_o_w'], 'L3_xattn_ln_o_b': _L3_xattn_in['ln_o_b'], 'L3_ffn_router_w0': _L3_ffn_in['router_w0'], 'L3_ffn_wg0': _L3_ffn_in['wg0'], 'L3_ffn_wu0': _L3_ffn_in['wu0'], 'L3_ffn_wd0': _L3_ffn_in['wd0'], 'L3_ffn_router_w1': _L3_ffn_in['router_w1'], 'L3_ffn_wg1': _L3_ffn_in['wg1'], 'L3_ffn_wu1': _L3_ffn_in['wu1'], 'L3_ffn_wd1': _L3_ffn_in['wd1']}

def reference(x, ctx_1024, mask_BxS2_ik0, mask_BxS2_bk0, L0_xattn_W_Q, L0_xattn_W_K, L0_xattn_W_V, L0_xattn_g_w, L0_xattn_g_b, L0_xattn_out_w, L0_xattn_out_b, L0_ffn_router_w, L0_ffn_router_b, L0_ffn_w1, L0_ffn_b1, L0_ffn_w2, L0_ffn_b2, L1_xattn_w_cq, L1_xattn_b_cq, L1_xattn_w_c, L1_xattn_b_c, L1_xattn_w_q, L1_xattn_b_q, L1_xattn_W_l, L1_xattn_b_l, L1_ffn_Wr, L1_ffn_Wu, L1_ffn_Wg, L1_ffn_Wd, L1_ffn_Wu_s, L1_ffn_Wg_s, L1_ffn_Wd_s, L2_xattn_Wq, L2_xattn_bq, L2_xattn_Wk, L2_xattn_bk, L2_xattn_Wv, L2_xattn_bv, L2_xattn_Wo, L2_xattn_bo, L2_ffn_w1, L2_ffn_conv_w, L2_ffn_conv_b, L2_ffn_w2, L3_xattn_ln_x_w, L3_xattn_ln_x_b, L3_xattn_ln_l_w, L3_xattn_ln_l_b, L3_xattn_Wq, L3_xattn_Wkv, L3_xattn_q_scale, L3_xattn_k_scale, L3_xattn_Wo, L3_xattn_ln_o_w, L3_xattn_ln_o_b, L3_ffn_router_w0, L3_ffn_wg0, L3_ffn_wu0, L3_ffn_wd0, L3_ffn_router_w1, L3_ffn_wg1, L3_ffn_wu1, L3_ffn_wd1):
    import jax
    import jax.numpy as jnp

    def _L0_xattn_ref(query, key, value, W_Q, W_K, W_V, g_w, g_b, out_w, out_b):
        import jax, jax.numpy as jnp
        import numpy as np
        SCALE_BASE = 512.0
        GN_EPS = 1e-05

        def _xpos(x, downscale):
            L, D = (x.shape[-2], x.shape[-1])
            half = D // 2
            base = (jnp.arange(0, D, 2, dtype=jnp.float32) + 0.4 * D) / (1.4 * D)
            min_pos = -(L // 2)
            power = (jnp.arange(min_pos, min_pos + L, dtype=jnp.float32) / SCALE_BASE)[:, None]
            scale = base[None, :] ** power
            inv_freq = 1.0 / 10000.0 ** (jnp.arange(half, dtype=jnp.float32) / half)
            ang = jnp.arange(L, dtype=jnp.float32)[:, None] * inv_freq[None, :]
            sin, cos = (jnp.sin(ang), jnp.cos(ang))
            if downscale:
                scale = 1.0 / scale
            sin_s = jnp.repeat(sin * scale, 2, axis=-1)
            cos_s = jnp.repeat(cos * scale, 2, axis=-1)
            x1, x2 = (x[..., ::2], x[..., 1::2])
            rot = jnp.stack((-x2, x1), axis=-1).reshape(x.shape)
            return x * cos_s + rot * sin_s

        def _decay_mask(L, H):
            gammas = 1.0 - jnp.exp(jnp.linspace(np.log(1.0 / 32.0), np.log(1.0 / 512.0), H)).astype(jnp.float32)
            idx = jnp.arange(L)
            dist = idx[:, None] - idx[None, :]
            causal = dist >= 0
            d = jnp.maximum(dist, 0).astype(jnp.float32)
            return jnp.where(causal[None], gammas[:, None, None] ** d[None], 0.0)
        B, L, D = query.shape
        H = W_Q.shape[0]
        q = jnp.einsum('bld,hde->bhle', query, W_Q)
        k = jnp.einsum('bld,hde->bhle', key, W_K)
        v = jnp.einsum('bld,hde->bhle', value, W_V)
        q = _xpos(q, downscale=False)
        k = _xpos(k, downscale=True)
        sim = jnp.einsum('bhnd,bhsd->bhns', q, k) * _decay_mask(L, H)[None]
        ret = jnp.einsum('bhns,bhsd->bhnd', sim, v)
        mu = ret.mean(axis=-1, keepdims=True)
        var = ret.var(axis=-1, keepdims=True)
        ret = (ret - mu) / jnp.sqrt(var + GN_EPS)
        ret = ret.transpose(0, 2, 1, 3).reshape(B, L, D)
        gate = jax.nn.silu(query @ g_w.T + g_b)
        return ret * gate @ out_w.T + out_b

    def _L0_ffn_ref(x, router_w, router_b, w1, b1, w2, b2):
        import jax, jax.numpy as jnp
        import numpy as np
        D_MODEL = 128
        FF_DIM = 4 * D_MODEL
        NUM_EXPERTS = 8
        TOP_K = 2
        B, L = (4, 256)
        Bq, Lq, D = x.shape
        x_flat = x.reshape(-1, D)
        logits = x_flat @ router_w.T + router_b
        probs = jax.nn.softmax(logits, axis=-1)
        topk_w, topk_idx = jax.lax.top_k(probs, TOP_K)
        topk_w = topk_w / jnp.sum(topk_w, axis=-1, keepdims=True)
        onehot = jax.nn.one_hot(topk_idx, NUM_EXPERTS, dtype=x.dtype)
        coef = jnp.einsum('tk,tke->te', topk_w, onehot)
        h = jnp.einsum('td,efd->tef', x_flat, w1) + b1[None]
        h = jax.nn.gelu(h, approximate=False)
        y = jnp.einsum('tef,edf->ted', h, w2) + b2[None]
        out = jnp.einsum('ted,te->td', y, coef)
        return out.reshape(Bq, Lq, D)

    def _L1_xattn_ref(c, q, w_cq, b_cq, w_c, b_c, w_q, b_q, W_l, b_l):
        import jax, jax.numpy as jnp
        import numpy as np
        B, C_LEN, Q_LEN, D = (8, 256, 64, 128)
        cq = jnp.einsum('bcd,bqd,d->bcq', c, q, w_cq) + b_cq
        s = (c @ w_c + b_c)[:, :, None] + (q @ w_q + b_q)[:, None, :] + cq
        a = jax.nn.softmax(s, axis=2)
        c2q_att = jnp.einsum('bcq,bqd->bcd', a, q)
        b_att = jax.nn.softmax(jnp.max(s, axis=2), axis=1)
        q2c_att = jnp.einsum('bc,bcd->bd', b_att, c)[:, None, :]
        x = jnp.concatenate([c, c2q_att, c * c2q_att, c * q2c_att], axis=-1)
        z = x @ W_l.T + b_l
        return z

    def _L1_ffn_ref(x, Wr, Wu, Wg, Wd, Wu_s, Wg_s, Wd_s):
        import jax, jax.numpy as jnp
        import numpy as np
        DIM = 128
        HID = 512
        NUM_EXPERTS = 8
        TOP_K = 2
        ALPHA = 2.0
        B, S = (4, 256)

        def _swiglu(x, wu, wg, wd):
            up = x @ wu
            g = x @ wg
            gate = jax.nn.sigmoid(g) * g
            return up * gate @ wd
        logits = x @ Wr
        probs = jax.nn.softmax(logits, axis=-1)
        topk_vals, topk_idx = jax.lax.top_k(probs, TOP_K)
        out = jnp.zeros_like(x)
        for i in range(TOP_K - 1):
            p = topk_vals[..., i:i + 1]
            ind = topk_idx[..., i]
            acc = jnp.zeros_like(x)
            for j in range(NUM_EXPERTS - 1):
                mask = (ind == j).astype(x.dtype)[..., None]
                acc = acc + _swiglu(x, Wu[j], Wg[j], Wd[j]) * mask
            out = out + ALPHA * p * acc
        out = out + _swiglu(x, Wu_s, Wg_s, Wd_s)
        return out

    def _L2_xattn_ref(q, k, v, mask, Wq, bq, Wk, bk, Wv, bv, Wo, bo):
        import jax, jax.numpy as jnp
        import numpy as np
        D_MODEL = 128
        NUM_HEADS = 16
        D_K = D_MODEL // NUM_HEADS
        B, S, _ = q.shape

        def split(x):
            return x.reshape(B, -1, NUM_HEADS, D_K).transpose(0, 2, 1, 3)
        qh = split(q @ Wq.T + bq)
        kh = split(k @ Wk.T + bk)
        vh = split(v @ Wv.T + bv)
        scores = jnp.einsum('bhqd,bhkd->bhqk', qh, kh) / jnp.sqrt(jnp.float32(D_K))
        scores = jnp.where(mask[:, None, None, :] == 0, jnp.float32(-1000000000.0), scores)
        attn = jax.nn.softmax(scores, axis=-1)
        out = jnp.einsum('bhqk,bhkd->bhqd', attn, vh)
        out = out.transpose(0, 2, 1, 3).reshape(B, S, NUM_HEADS * D_K)
        return out @ Wo.T + bo

    def _L2_ffn_ref(x, w1, conv_w, conv_b, w2):
        import jax, jax.numpy as jnp
        import numpy as np
        B, S, D_MODEL, D_HIDDEN = (4, 256, 128, 512)

        def act_quant(x):
            scale = 127.0 / jnp.clip(jnp.max(jnp.abs(x), axis=-1, keepdims=True), 1e-05)
            return jnp.clip(jnp.round(x * scale), -128, 127) / scale

        def weight_quant(w):
            scale = 1.0 / jnp.clip(jnp.mean(jnp.abs(w)), 1e-05)
            return jnp.clip(jnp.round(w * scale), -1, 1) / scale

        def bit_linear(x, w):
            xq = x + jax.lax.stop_gradient(act_quant(x) - x)
            wq = w + jax.lax.stop_gradient(weight_quant(w) - w)
            return jnp.einsum('bsd,hd->bsh', xq, wq)

        def depthwise_conv1d(x_bcl, w, b):
            y = jax.lax.conv_general_dilated(x_bcl, w, window_strides=(1,), padding=[(1, 1)], dimension_numbers=('NCH', 'OIH', 'NCH'), feature_group_count=x_bcl.shape[1])
            return y + b[None, :, None]
        h = bit_linear(x, w1)
        h = depthwise_conv1d(h.transpose(0, 2, 1), conv_w, conv_b)
        h = h.transpose(0, 2, 1)
        h = jax.nn.silu(h)
        return bit_linear(h, w2)

    def _L3_xattn_ref(x, latents, mask, ln_x_w, ln_x_b, ln_l_w, ln_l_b, Wq, Wkv, q_scale, k_scale, Wo, ln_o_w, ln_o_b):
        import jax, jax.numpy as jnp
        import numpy as np
        DIM, DIM_HEAD, HEADS, SCALE = (128, 64, 8, 8.0)
        INNER = DIM_HEAD * HEADS
        LN_EPS = 1e-05
        L2_EPS = 1e-12

        def layer_norm(x, w, b):
            mu = jnp.mean(x, axis=-1, keepdims=True)
            var = jnp.mean(jnp.square(x - mu), axis=-1, keepdims=True)
            return (x - mu) * jax.lax.rsqrt(var + LN_EPS) * w + b

        def l2norm(t):
            n = jnp.sqrt(jnp.sum(jnp.square(t), axis=-1, keepdims=True))
            return t / jnp.maximum(n, L2_EPS)
        b, n, _ = x.shape
        m = latents.shape[1]
        x = layer_norm(x, ln_x_w, ln_x_b)
        latents = layer_norm(latents, ln_l_w, ln_l_b)
        q = latents @ Wq
        kv_input = jnp.concatenate([x, latents], axis=1)
        kv = kv_input @ Wkv
        k, v = jnp.split(kv, 2, axis=-1)

        def to_heads(t):
            return t.reshape(t.shape[0], t.shape[1], HEADS, DIM_HEAD).transpose(0, 2, 1, 3)
        q, k, v = map(to_heads, (q, k, v))
        q = l2norm(q) * q_scale
        k = l2norm(k) * k_scale
        sim = jnp.einsum('bhid,bhjd->bhij', q, k) * SCALE
        full_mask = jnp.concatenate([mask, jnp.ones((b, m), dtype=bool)], axis=1)[:, None, None, :]
        max_neg = -jnp.finfo(sim.dtype).max
        sim = jnp.where(full_mask, sim, max_neg)
        attn = jax.nn.softmax(sim.astype(jnp.float32), axis=-1).astype(sim.dtype)
        out = jnp.einsum('bhij,bhjd->bhid', attn, v)
        out = out.transpose(0, 2, 1, 3).reshape(b, m, INNER)
        return layer_norm(out @ Wo, ln_o_w, ln_o_b)

    def _L3_ffn_ref(x, router_w0, wg0, wu0, wd0, router_w1, wg1, wu1, wd1):
        import jax, jax.numpy as jnp
        from jax import lax
        import numpy as np
        D_MODEL = 128
        HIDDEN = 64
        N_EXPERTS = 32
        TOP_K = 2
        B, S = (1, 512)

        def _moe_group(x2, router_w, wg, wu, wd, top_k):
            T = x2.shape[0]
            n_experts = router_w.shape[1]
            logits = x2 @ router_w
            scores = jax.nn.softmax(logits, axis=-1)
            expert_weights, expert_indices = lax.top_k(scores, top_k)
            flat_e = expert_indices.reshape(-1)
            flat_w = expert_weights.reshape(-1)
            flat_t = jnp.repeat(jnp.arange(T), top_k)
            order = jnp.argsort(flat_e)
            tok = flat_t[order]
            xs = x2[tok]
            group_sizes = jnp.bincount(flat_e, length=n_experts).astype(jnp.int32)
            gate = lax.ragged_dot(xs, wg, group_sizes)
            up = lax.ragged_dot(xs, wu, group_sizes)
            ys = lax.ragged_dot(jax.nn.silu(gate) * up, wd, group_sizes)
            ys = ys * flat_w[order][:, None]
            return jnp.zeros_like(x2).at[tok].add(ys)
        b, s, d = x.shape
        x2 = x.reshape(-1, d)
        out0 = _moe_group(x2, router_w0, wg0, wu0, wd0, TOP_K)
        out1 = _moe_group(x2, router_w1, wg1, wu1, wd1, TOP_K)
        out = (out0 * TOP_K + out1 * TOP_K) / (TOP_K + TOP_K)
        return out.reshape(b, s, d)
    x = x + _L0_xattn_ref(_layernorm(x, axis=-1), ctx_1024, ctx_1024, L0_xattn_W_Q, L0_xattn_W_K, L0_xattn_W_V, L0_xattn_g_w, L0_xattn_g_b, L0_xattn_out_w, L0_xattn_out_b)
    x = x + _L0_ffn_ref(_layernorm(x, axis=-1), L0_ffn_router_w, L0_ffn_router_b, L0_ffn_w1, L0_ffn_b1, L0_ffn_w2, L0_ffn_b2)
    x = x + _L1_xattn_ref(_layernorm(x, axis=-1), ctx_1024, L1_xattn_w_cq, L1_xattn_b_cq, L1_xattn_w_c, L1_xattn_b_c, L1_xattn_w_q, L1_xattn_b_q, L1_xattn_W_l, L1_xattn_b_l)
    x = x + _L1_ffn_ref(_layernorm(x, axis=-1), L1_ffn_Wr, L1_ffn_Wu, L1_ffn_Wg, L1_ffn_Wd, L1_ffn_Wu_s, L1_ffn_Wg_s, L1_ffn_Wd_s)
    x = x + _L2_xattn_ref(_layernorm(x, axis=-1), ctx_1024, ctx_1024, mask_BxS2_ik0, L2_xattn_Wq, L2_xattn_bq, L2_xattn_Wk, L2_xattn_bk, L2_xattn_Wv, L2_xattn_bv, L2_xattn_Wo, L2_xattn_bo)
    x = x + _L2_ffn_ref(_layernorm(x, axis=-1), L2_ffn_w1, L2_ffn_conv_w, L2_ffn_conv_b, L2_ffn_w2)
    x = x + _L3_xattn_ref(ctx_1024, _layernorm(x, axis=-1), mask_BxS2_bk0, L3_xattn_ln_x_w, L3_xattn_ln_x_b, L3_xattn_ln_l_w, L3_xattn_ln_l_b, L3_xattn_Wq, L3_xattn_Wkv, L3_xattn_q_scale, L3_xattn_k_scale, L3_xattn_Wo, L3_xattn_ln_o_w, L3_xattn_ln_o_b)
    x = x + _L3_ffn_ref(_layernorm(x, axis=-1), L3_ffn_router_w0, L3_ffn_wg0, L3_ffn_wu0, L3_ffn_wd0, L3_ffn_router_w1, L3_ffn_wg1, L3_ffn_wu1, L3_ffn_wd1)
    return x

_drawn_inputs = setup_inputs


def setup_inputs(seed=0):
    import zlib

    import numpy as np

    out = dict(_drawn_inputs(seed))
    spreads = {'L0_xattn_g_b': (0.0, 0.1),
     'L0_xattn_out_b': (0.0, 0.1),
     'L3_xattn_ln_x_w': (1.0, 0.6),
     'L3_xattn_ln_x_b': (0.0, 0.375),
     'L3_xattn_ln_l_w': (1.0, 0.2),
     'L3_xattn_ln_l_b': (0.0, 0.1),
     'L3_xattn_q_scale': (1.0, 0.2),
     'L3_xattn_k_scale': (1.0, 0.2),
     'L3_xattn_ln_o_w': (1.0, 0.2),
     'L3_xattn_ln_o_b': (0.0, 0.1)}
    factors = {'L0_ffn_b1': 5.342,
     'L0_ffn_b2': 3.534,
     'L1_ffn_Wr': 8.0,
     'L1_ffn_Wu': 8.0,
     'L1_ffn_Wg': 8.0,
     'L1_ffn_Wd': 8.0,
     'L1_ffn_Wu_s': 8.0,
     'L1_ffn_Wg_s': 8.0,
     'L1_ffn_Wd_s': 8.0,
     'L2_xattn_bk': 8.0,
     'L3_ffn_router_w0': 8.0,
     'L3_ffn_wg0': 8.0,
     'L3_ffn_wu0': 8.0,
     'L3_ffn_wd0': 8.0,
     'L3_ffn_router_w1': 8.0,
     'L3_ffn_wg1': 8.0,
     'L3_ffn_wu1': 8.0,
     'L3_ffn_wd1': 8.0}
    for name, (base, spread) in spreads.items():
        noise = np.random.default_rng([zlib.crc32(name.encode()), seed]).standard_normal(out[name].shape)
        drawn = base * np.exp(spread * noise) if base else spread * noise
        out[name] = jnp.asarray(drawn.astype(out[name].dtype))
    for name, factor in factors.items():
        out[name] = (out[name] * factor).astype(out[name].dtype)
    return out
```

```python
from contextlib import ExitStack

import numpy as np
import concourse.bass as bass
from concourse import mybir

F32, BF16, I32, U8 = mybir.dt.float32, mybir.dt.bfloat16, mybir.dt.int32, mybir.dt.uint8
ALU = mybir.AluOpType
ACT = mybir.ActivationFunctionType
AX = mybir.AxisListType

P = 128
B, S, D = 8, 256, 128
TILES = B * S // P
GROUPS = 4
GT = TILES // GROUPS
GN = GT * P
EPS = 1e-5
ROUND = 1.5 * 2.0 ** 23
NEG = -1e9
LAYERS = ("L0x", "L0f", "L1x", "L1f", "L2x", "L2f", "L3x", "L3f")


class Queue:

    def __init__(self, eng, sem):
        self.eng, self.sem, self.done, self.waited = eng, sem, 0, {}

    def wait(self, *tickets):
        for t in tickets:
            if t is None:
                continue
            if isinstance(t, list):
                self.wait(*t)
                continue
            sem, count = t
            if self.waited.get(sem.name, 0) < count:
                self.waited[sem.name] = count
                self.eng.wait_ge(sem, count)

    def run(self, issue, *after):
        self.wait(*after)
        self.done += 1
        issue(self.eng).then_inc(self.sem, 1)
        return (self.sem, self.done)

    def chain(self, issue, *after):
        return self.run(issue, self.last(), *after)

    def quiet(self, issue, *after):
        self.wait(*after)
        issue(self.eng)

    def last(self):
        return (self.sem, self.done) if self.done else None


class Buffer:

    def __init__(self, ap):
        self.ap, self.free = ap, []


class Ring:
    def __init__(self, aps):
        self.buffers, self.at = [Buffer(a) for a in aps], 0

    def take(self):
        b = self.buffers[self.at % len(self.buffers)]
        self.at += 1
        return b


def build(nc, ins, out):
    ctx = ExitStack()
    with ctx:
        def sem(name):
            return ctx.enter_context(nc.semaphore(name))

        PE, VEC, SCA, POOL = (Queue(eng, sem(n)) for eng, n in (
            (nc.tensor, "pe_done"), (nc.vector, "vec_done"), (nc.scalar, "sca_done"), (nc.gpsimd, "pool_done")))
        SYNC = Queue(nc.sync, None)

        def sb(name, shape, dt=F32, where=None):
            return (where or ctx).enter_context(nc.sbuf_tensor(name, shape, dt))

        def load_group(name, pairs, *after):
            s = sem("in_" + name)
            SYNC.wait(*after)
            for dst, src in pairs:
                SYNC.eng.dma_start(dst, src).then_inc(s, 16)
            return (s, 16 * len(pairs))

        x = sb("x", [P, TILES, D])
        xn = sb("xn", [P, TILES, D])
        xnT = sb("xnT", [P, TILES * P])
        ctxt = sb("ctxt", [P, TILES, D])
        ctxT = sb("ctxT", [P, TILES * P])
        ident = sb("ident", [P, P])
        identb = sb("identb", [P, P], BF16)
        ones = sb("ones", [P, P])
        onesb = sb("onesb", [P, P], BF16)
        stats = sb("stats", [P, GT, 6])
        meanvar = sb("meanvar", [P, GT, 2])
        rsq_v = sb("rsq_v", [P, 64])
        rsq_i = sb("rsq_i", [P, 64], I32)
        rsq_y = sb("rsq_y", [P, 64])
        rsq_t = sb("rsq_t", [P, 64])
        psum = [ctx.enter_context(nc.psum_tensor(f"bank{i}", [P, 512], F32)) for i in range(8)]
        banks = Ring([b[:, :] for b in psum[0:6]])
        accs = Ring([b[:, :] for b in psum[6:8]])

        x_v = ins["x"].rearrange("b (u p) d -> p (b u) d", p=P)
        c_v = ins["ctx_1024"].rearrange("b (u p) d -> p (b u) d", p=P)
        x_in = load_group("x", [(x[:, :, :], x_v)])
        const_in = load_group("const", [(ident[:, :], ins["c_ident"])])
        ctx_in = load_group("ctx", [(ctxT[:, :], ins["ctxT"]), (ctxt[:, :, :], c_v)])
        ones_set = VEC.run(lambda e: e.memset(ones[:, :], 1.0))
        onesb_set = VEC.run(lambda e: e.memset(onesb[:, :], 1.0))
        identb_set = VEC.run(lambda e: e.tensor_copy(identb[:, :], ident[:, :]), const_in)
        PE.wait(const_in, ones_set, onesb_set, identb_set)
        x_ready = [[x_in] for _ in range(GROUPS)]

        def mm(dst, lhsT, rhs, start, stop, *after, tell=False):
            f = lambda e: e.matmul(dst, lhsT, rhs, start=start, stop=stop, skip_group_check=True)
            return PE.run(f, *after) if tell else PE.quiet(f, *after)

        def transpose(dst, src, idt, *after, tell=False):
            f = lambda e: e.transpose(dst, src, idt)
            return PE.run(f, *after) if tell else PE.quiet(f, *after)

        def rsqrt(n, *after):
            v, i, y, t = rsq_v[:, 0:n], rsq_i[:, 0:n], rsq_y[:, 0:n], rsq_t[:, 0:n]
            VEC.chain(lambda e: e.tensor_scalar(i, v.bitcast(I32), 1, None, ALU.logical_shift_right), *after)
            VEC.chain(lambda e: e.tensor_scalar(y.bitcast(I32), i, -1.0, float(0x5F3759DF), ALU.mult, ALU.add))
            for _ in range(3):
                VEC.chain(lambda e: e.tensor_tensor(t, y, y, ALU.mult))
                VEC.chain(lambda e: e.tensor_tensor(t, t, v, ALU.mult))
                VEC.chain(lambda e: e.tensor_scalar(t, t, -0.5, 1.5, ALU.mult, ALU.add))
                VEC.chain(lambda e: e.tensor_tensor(y, y, t, ALU.mult))
            return VEC.last()

        def normalise(src, dst, n, *after):
            VEC.wait(*after)
            VEC.wait(VEC.last())
            for k in range(n):
                VEC.run(lambda e, k=k: e.bn_stats(stats[:, k, :], src[:, k, :]))
            VEC.wait(VEC.last())
            for k in range(n):
                VEC.run(lambda e, k=k: e.bn_aggr(meanvar[:, k, :], stats[:, k, :]))
            VEC.chain(lambda e: e.tensor_scalar(rsq_v[:, 0:n], meanvar[:, 0:n, 1], EPS, None, ALU.add))
            rsqrt(n)
            VEC.wait(VEC.last())
            for k in range(n):
                done = VEC.run(lambda e, k=k: e.tensor_scalar(dst[:, k, :], src[:, k, :], meanvar[:, k, 0:1],
                                                              rsq_y[:, k:k + 1], ALU.subtract, ALU.mult))
            return done

        def turn(src, dst, n, ready, dst_free=(), scale=None, bias=None):
            b = banks.take()
            for k in range(n):
                t = transpose(b.ap[:, k * P:(k + 1) * P], src[:, k, :], ident[:, :], b.free, ready, tell=(k == n - 1))
            if scale is None:
                done = SCA.run(lambda e: e.activation(dst, b.ap[:, 0:n * P], ACT.Copy), t, *dst_free)
            else:
                done = SCA.run(lambda e: e.activation(dst, b.ap[:, 0:n * P], ACT.Identity, scale=scale, bias=bias),
                               t, *dst_free)
            b.free = [done]
            return done

        def xgroup(g):
            return x[:, g * GT:(g + 1) * GT, :]

        def norm_x(g, *free):
            n = normalise(xgroup(g), xn[:, g * GT:(g + 1) * GT, :], GT, x_ready[g], *free)
            t = turn(xn[:, g * GT:(g + 1) * GT, :], xnT[:, g * GN:(g + 1) * GN], GT, n, free)
            return n, t

        def add_to_x(g, bank, ready):
            t = VEC.run(lambda e: e.tensor_tensor(x[:, g * GT:(g + 1) * GT, :],
                                                  bank.ap.rearrange("p (t d) -> p t d", t=GT),
                                                  x[:, g * GT:(g + 1) * GT, :], ALU.add), ready, x_ready[g])
            bank.free = [t]
            x_ready[g] = [t]

        def project_tokens(bank, lhs_of, weights, bias_row, ready, *after):
            for t in range(GT):
                o = bank.ap[:, t * P:(t + 1) * P]
                if bias_row is not None:
                    mm(o, ones[0:1, :], bias_row, True, False, bank.free, ready, *after)
                for k, w in enumerate(weights):
                    done = mm(o, lhs_of(t, k), w, bias_row is None and k == 0, k == len(weights) - 1,
                              bank.free, ready, *after, tell=(k == len(weights) - 1))
            return done

        WA = sb("WA", [P, 3 * 4096])
        WB = sb("WB", [P, 3 * 4096])
        region_free = {"A": [], "B": []}

        def fence():
            ends = [q.last() for q in (PE, VEC, SCA, POOL)]
            for q in (PE, VEC, SCA, POOL, SYNC):
                q.wait(*ends)

        def all_last():
            return [q.last() for q in (PE, VEC, SCA, POOL)]

        def retention(work):
            H, HD = 16, 8
            w = sb("w_ret", [P, 7, P], where=work)
            rows = sb("rows_ret", [1, 2, P], where=work)
            tab = sb("tab_ret", [P, 4, S], where=work)
            masks = sb("mask_ret", [P, 4 + P + 512], where=work)
            win = load_group("ret", [(w[:, :, :], ins["w_ret"]), (rows[0:1, :, :], ins["rows_ret"]),
                                     (tab[:, :, :], ins["c_xpos"]), (masks[:, :], ins["c_retmask"])])
            head4, blockdiag, causal = masks[:, 0:4], masks[:, 4:4 + P], masks[:, 4 + P:]
            QT = sb("QT", [P, GN], where=work)
            KT = sb("KT", [P, GN], where=work)
            rot = sb("rot", [P, 2, GN], where=work)
            QM = sb("QM", [P, 4, GN], where=work)
            V = sb("V", [P, GT, P], where=work)
            Ktok = sb("Ktok", [P, 2, P], where=work)
            state = sb("state", [P, 2, P], where=work)
            probs = Ring([sb(f"prob{i}", [P, 512], where=work)[:, :] for i in range(3)])
            mu = sb("mu", [P, 64], where=work)
            cen = sb("cen", [P, 512], where=work)
            sq = sb("sq", [P, 512], where=work)
            gate = sb("gate", [P, 512], where=work)
            yT = sb("yT", [P, GN], where=work)
            group_end = []
            for g in range(GROUPS):
                _, xT = norm_x(g)
                cols = slice(g * GN, (g + 1) * GN)

                def rotated(dst, k, src, t0, ready):
                    made = []
                    for j in range(2):
                        b = banks.take()
                        m = mm(b.ap, w[:, k + j, :], src[:, cols], True, True, b.free, ready, win, tell=True)
                        v = VEC.run(lambda e, j=j, b=b: e.tensor_tensor(
                            rot[:, j, :].rearrange("p (b s) -> p b s", b=2), b.ap.rearrange("p (b s) -> p b s", b=2),
                            tab[:, t0 + j:t0 + j + 1, :].to_broadcast([P, 2, S]), ALU.mult), m, win, *group_end)
                        b.free = [v]
                        made.append(v)
                    return VEC.chain(lambda e: e.tensor_tensor(dst, rot[:, 0, :], rot[:, 1, :], ALU.add), made)

                q_ready = rotated(QT[:, :], 0, xnT, 0, xT)
                VEC.wait(q_ready)
                for j in range(4):
                    qm = VEC.run(lambda e, j=j: e.tensor_scalar(QM[:, j, :], QT[:, :], head4[:, j:j + 1], None,
                                                                ALU.mult))
                k_ready = rotated(KT[:, :], 2, ctxT, 2, ctx_in)
                b = banks.take()
                v_mm = project_tokens(b, lambda t, k: ctxT[:, (g * GT + t) * P:(g * GT + t + 1) * P],
                                      [w[:, 4, :]], None, win, ctx_in)
                v_ready = SCA.run(lambda e, b=b: e.activation(V[:, :, :], b.ap.rearrange("p (t d) -> p t d", t=GT),
                                                              ACT.Copy), v_mm, *group_end)
                b.free = [v_ready]
                b = banks.take()
                for u in range(2):
                    t = transpose(b.ap[:, u * P:(u + 1) * P], KT[:, 2 * u * P:(2 * u + 1) * P], ident[:, :],
                                  b.free, k_ready, tell=(u == 1))
                ktok = SCA.run(lambda e, b=b: e.activation(Ktok[:, :, :], b.ap[:, 0:2 * P].rearrange(
                    "p (t d) -> p t d", t=2), ACT.Copy), t, *group_end)
                b.free = [ktok]
                b = banks.take()
                for u in range(2):
                    t = mm(b.ap[:, u * P:(u + 1) * P], Ktok[:, u, :], V[:, 2 * u, :], True, True, b.free, ktok,
                           v_ready, tell=(u == 1))
                st = VEC.run(lambda e, b=b: e.tensor_tensor(
                    state[:, :, :], b.ap[:, 0:2 * P].rearrange("p (t d) -> p t d", t=2),
                    blockdiag.unsqueeze(1).to_broadcast([P, 2, P]), ALU.mult), t, *group_end)
                b.free = [st]
                ret = accs.take()
                for t in range(GT):
                    tile = slice(t * P, (t + 1) * P)
                    if t % 2:
                        mm(ret.ap[:, tile], QT[:, tile], state[:, t // 2, :], True, False, ret.free, st, q_ready)
                    for c in range(4):
                        rows32 = slice(32 * c, 32 * c + 32)
                        b = banks.take()
                        s_mm = mm(b.ap, KT[rows32, tile], QM[rows32, :, tile], True, True, b.free, qm, k_ready,
                                  tell=True)
                        p = probs.take()
                        pr = VEC.run(lambda e, p=p, b=b: e.tensor_tensor(p.ap, b.ap, causal, ALU.mult), s_mm, p.free)
                        b.free = [pr]
                        for j in range(4):
                            h = 4 * c + j
                            av = mm(ret.ap[:, t * P + h * HD:t * P + (h + 1) * HD], p.ap[:, j * P:(j + 1) * P],
                                    V[:, t, h * HD:(h + 1) * HD], h == 0 and t % 2 == 0, True, ret.free, pr, v_ready,
                                    tell=(j == 3))
                        p.free = [av]
                heads = lambda a: a.rearrange("p (h e) -> p h e", e=HD)
                wide = lambda a: a.unsqueeze(2).to_broadcast([P, 64, HD])
                VEC.run(lambda e: e.reduce_sum(mu[:, :], heads(ret.ap), AX.X), av, VEC.last())
                VEC.chain(lambda e: e.tensor_scalar(mu[:, :], mu[:, :], 1.0 / HD, None, ALU.mult))
                c_ready = VEC.chain(lambda e: e.tensor_tensor(heads(cen[:, :]), heads(ret.ap), wide(mu[:, :]),
                                                              ALU.subtract))
                ret.free = [c_ready]
                sq_ready = SCA.run(lambda e: e.activation(sq[:, :], cen[:, :], ACT.Square), c_ready, *group_end)
                VEC.chain(lambda e: e.reduce_sum(rsq_v[:, :], heads(sq[:, :]), AX.X), sq_ready)
                VEC.chain(lambda e: e.tensor_scalar(rsq_v[:, :], rsq_v[:, :], 1.0 / HD, EPS, ALU.mult, ALU.add))
                rsqrt(64)
                n_ready = VEC.chain(lambda e: e.tensor_tensor(heads(cen[:, :]), heads(cen[:, :]), wide(rsq_y[:, :]),
                                                              ALU.mult))
                b = banks.take()
                g_mm = project_tokens(b, lambda t, k: xnT[:, (g * GT + t) * P:(g * GT + t + 1) * P], [w[:, 5, :]],
                                      rows[0:1, 0, :], xT, win)
                gate_ready = SCA.run(lambda e, b=b: e.activation(gate[:, :], b.ap, ACT.Silu), g_mm, *group_end)
                b.free = [gate_ready]
                y_ready = VEC.run(lambda e: e.tensor_tensor(cen[:, :], cen[:, :], gate[:, :], ALU.mult), n_ready,
                                  gate_ready)
                yt = turn(cen[:, :].rearrange("p (t d) -> p t d", t=GT), yT[:, :], GT, y_ready, group_end)
                b = banks.take()
                o_mm = project_tokens(b, lambda t, k: yT[:, t * P:(t + 1) * P], [w[:, 6, :]], rows[0:1, 1, :], yt)
                add_to_x(g, b, o_mm)
                group_end = all_last()

        def router(g, E, w_r, bias_row, kind, coef, tmp, ready, xT, *free):
            logits, top, ex, ssum = tmp
            b = banks.take()
            for t in range(GT):
                tok = slice((g * GT + t) * P, (g * GT + t + 1) * P)
                o = b.ap[:, t * E:(t + 1) * E]
                if bias_row is not None:
                    mm(o, ones[0:1, :], bias_row, True, False, b.free, xT, ready)
                m = mm(o, xnT[:, tok], w_r, bias_row is None, True, b.free, xT, ready, tell=(t == GT - 1))
            lg = VEC.run(lambda e: e.tensor_copy(logits, b.ap[:, 0:GT * E].rearrange("p (t e) -> p t e", t=GT)), m,
                         VEC.last(), *free)
            b.free = [lg]
            VEC.wait(lg)
            for t in range(GT):
                VEC.run(lambda e, t=t: e.max(top[:, t, :], logits[:, t, :]))
            sub = VEC.chain(lambda e: e.tensor_tensor(ex, logits, top[:, :, 0:1].to_broadcast([P, GT, E]),
                                                      ALU.subtract))
            exd = SCA.run(lambda e: e.activation(ex, ex, ACT.Exp), sub)
            if kind != "pair":
                VEC.run(lambda e: e.reduce_sum(ssum, ex, AX.X), exd)
            k = 0 if kind == "first" else 1
            VEC.chain(lambda e: e.tensor_tensor(logits, logits, top[:, :, k:k + 1].to_broadcast([P, GT, E]),
                                                ALU.is_ge), exd)
            VEC.chain(lambda e: e.tensor_tensor(ex, ex, logits, ALU.mult))
            if kind == "pair":
                VEC.chain(lambda e: e.reduce_sum(ssum, ex, AX.X))
            VEC.chain(lambda e: e.reciprocal(ssum, ssum))
            if kind == "first":
                VEC.chain(lambda e: e.tensor_scalar(ssum, ssum, 2.0, None, ALU.mult))
            if kind == "half":
                VEC.chain(lambda e: e.tensor_scalar(ssum, ssum, 0.5, None, ALU.mult))
            return VEC.chain(lambda e: e.tensor_tensor(coef, ex, ssum.unsqueeze(2).to_broadcast([P, GT, E]),
                                                       ALU.mult))

        def moe_gelu(work):
            E, F = 8, 512
            FB = F // P
            w1 = WA[:, 0:E * F]
            w2 = WA[:, E * F:2 * E * F].rearrange("p (e k d) -> p e k d", e=E, k=FB)
            b1 = sb("b1", [P, E * FB], where=work)
            b2 = sb("b2", [E, D], where=work)
            wr = sb("wr0", [P, E], where=work)
            br = sb("br0", [1, E], where=work)
            win = load_group("moe0", [(wr[:, :], ins["r0_w"]), (br[0:1, :], ins["r0_b"]), (b1[:, :], ins["e0_b1"]),
                                      (b2[:, :], ins["e0_b2"]), (w1, ins["e0_w1"]),
                                      (WA[:, E * F:2 * E * F], ins["e0_w2"])], *region_free["A"])
            coef = sb("coef0", [P, GROUPS * GT, E], where=work)
            tmp = (sb("lg0", [P, GT, E], where=work)[:, :, :], sb("top0", [P, GT, 8], where=work),
                   sb("ex0", [P, GT, E], where=work)[:, :, :], sb("ss0", [P, GT], where=work)[:, :])
            coefT = sb("coefT0", [E, GN], where=work)
            hT = Ring([sb(f"hT0_{i}", [P, FB, GN], where=work)[:, :, :] for i in range(2)])
            b2_done = []
            for g in range(GROUPS):
                _, xT = norm_x(g)
                cf = coef[:, g * GT:(g + 1) * GT, :]
                c_ready = router(g, E, wr[:, :], br[0:1, :], "pair", cf, tmp, win, xT)
                b = banks.take()
                for t in range(GT):
                    m = transpose(b.ap[0:E, t * P:(t + 1) * P], cf[:, t, :], ident[:, :], b.free, c_ready,
                                  tell=(t == GT - 1))
                ct = SCA.run(lambda e, b=b: e.activation(coefT[:, :], b.ap[0:E, :], ACT.Copy), m, *b2_done)
                b.free = [ct]
                b = banks.take()
                for t in range(GT):
                    m = mm(b.ap[:, t * P:(t + 1) * P], coefT[:, t * P:(t + 1) * P], b2[:, :], True, True, b.free, ct,
                           win, tell=(t == GT - 1))
                b2_done = [m]
                add_to_x(g, b, m)
                for ex in range(E):
                    h = hT.take()
                    for k in range(FB):
                        b = banks.take()
                        c0 = ex * F + k * P
                        m = mm(b.ap, w1[:, c0:c0 + P], xnT[:, g * GN:(g + 1) * GN], True, True, b.free, xT, win,
                               tell=True)
                        hd = SCA.run(lambda e, b=b, h=h, k=k, ex=ex: e.activation(
                            h.ap[:, k, :], b.ap, ACT.Gelu, bias=b1[:, ex * FB + k:ex * FB + k + 1]), m, h.free, win)
                        b.free = [hd]
                    b = accs.take()
                    m = project_tokens(b, lambda t, k: h.ap[:, k, t * P:(t + 1) * P],
                                       [w2[:, ex, k, :] for k in range(FB)], None, hd, win)
                    h.free = [m]
                    VEC.wait(x_ready[g])
                    for t in range(GT):
                        n = g * GT + t
                        v = VEC.run(lambda e, n=n, t=t, b=b, ex=ex: e.scalar_tensor_tensor(
                            x[:, n, :], b.ap[:, t * P:(t + 1) * P], coef[:, n, ex:ex + 1], x[:, n, :], ALU.mult,
                            ALU.add), m, c_ready)
                    b.free = [v]
                    x_ready[g] = [v]
            region_free["A"] = [PE.last()]

        def bidaf(work):
            Wl = sb("Wl", [P, 4, D], where=work)
            cols = sb("cols1", [P, 3], where=work)
            bias3 = sb("bias3", [P, 3], where=work)
            row = sb("row1", [1, D], where=work)
            win = load_group("bidaf", [(Wl[:, :, :], ins["l1_W"]), (cols[:, :], ins["l1_cols"]),
                                       (bias3[:, :], ins["l1_bias"]), (row[0:1, :], ins["l1_row"])])
            cw = sb("cw", [P, S], where=work)
            attn = sb("attn", [P, 2, S], where=work)
            aT = sb("aT", [P, 2, S], where=work)
            c2q = sb("c2q", [P, 2, S], where=work)
            mx = sb("mx", [P, 4], where=work)
            nm = sb("nm", [P, 2], where=work)
            sm = sb("sm", [P, 2], where=work)
            rs = sb("rs", [P, 2], where=work)
            bsum = sb("bsum", [P, 1], where=work)
            mrow = sb("mrow", [1, S], where=work)
            mtop = sb("mtop", [1, 1], where=work)
            eb = sb("eb", [P, 2], where=work)
            rb = sb("rb", [P, 1], where=work)
            q2c = sb("q2c", [P, 1], where=work)
            W14 = sb("W14", [P, D], where=work)
            VEC.run(lambda e: e.reduce_sum(bsum[:, :], bias3[:, :], AX.X), win)
            end = []
            for g in range(GROUPS):
                xnr, xT = norm_x(g)
                zb = accs.take()
                for u in range(2):
                    bt = 2 * g + u
                    tok = slice(bt * S, (bt + 1) * S)
                    tile = lambda i: slice(bt * S + i * P, bt * S + (i + 1) * P)
                    cwr = VEC.run(lambda e: e.tensor_scalar(cw[:, :], xnT[:, tok], cols[:, 0:1], cols[:, 1:2],
                                                            ALU.mult, ALU.add), xT, win, *end)
                    b = banks.take()
                    for i in range(2):
                        s_mm = mm(b.ap[:, i * S:(i + 1) * S], cw[:, i * P:(i + 1) * P], ctxT[:, tok], True, True,
                                  b.free, cwr, ctx_in, tell=(i == 1))
                    bc = banks.take()
                    for i in range(2):
                        c_mm = mm(bc.ap[:, i:i + 1], xnT[:, tile(i)], cols[:, 2:3], True, True, bc.free, xT, win,
                                  tell=(i == 1))
                    VEC.wait(VEC.last())
                    VEC.run(lambda e, b=b: e.reduce_max(mx[:, 0:2], b.ap.rearrange("p (i s) -> p i s", i=2), AX.X),
                            s_mm)
                    nmr = VEC.chain(lambda e: e.tensor_scalar(nm[:, :], mx[:, 0:2], -1.0, None, ALU.mult))
                    for i in range(2):
                        ex = SCA.run(lambda e, b=b, i=i: e.activation(attn[:, i, :], b.ap[:, i * S:(i + 1) * S],
                                                                      ACT.Exp, bias=nm[:, i:i + 1],
                                                                      accum_out=sm[:, i:i + 1]), nmr, *end)
                    b.free = [ex, VEC.last()]
                    mr = VEC.chain(lambda e, bc=bc: e.scalar_tensor_tensor(mx[:, 2:4], bc.ap[:, 0:2], bsum[:, 0:1],
                                                                           mx[:, 0:2], ALU.add, ALU.add), c_mm)
                    bc.free = [mr]
                    VEC.chain(lambda e: e.reciprocal(rs[:, :], sm[:, :]), ex)
                    VEC.wait(VEC.last())
                    for i in range(2):
                        ar = VEC.run(lambda e, i=i: e.tensor_scalar(attn[:, i, :], attn[:, i, :], rs[:, i:i + 1],
                                                                    None, ALU.mult))
                    b = banks.take()
                    for i in range(2):
                        for j in range(2):
                            t = transpose(b.ap[:, j * S + i * P:j * S + (i + 1) * P], attn[:, i, j * P:(j + 1) * P],
                                          ident[:, :], b.free, ar, tell=(i + j == 2))
                    at = SCA.run(lambda e, b=b: e.activation(aT[:, :, :], b.ap.rearrange("p (j s) -> p j s", j=2),
                                                             ACT.Copy), t, *end)
                    b.free = [at]
                    b = banks.take()
                    for j in range(2):
                        t = mm(b.ap[:, 0:S], ctxt[:, 2 * bt + j, :], aT[:, j, :], j == 0, j == 1, b.free, at, ctx_in,
                               tell=(j == 1))
                    c1 = SCA.run(lambda e, b=b: e.activation(c2q[:, 0, :], b.ap[:, 0:S], ACT.Copy), t, *end)
                    c2 = VEC.run(lambda e: e.tensor_tensor(c2q[:, 1, :], c2q[:, 0, :], xnT[:, tok], ALU.mult), c1)
                    b.free = [c1]
                    b = banks.take()
                    for i in range(2):
                        t = mm(b.ap[0:1, i * P:(i + 1) * P], mx[:, 2 + i:3 + i], ident[:, :], True, True, b.free, mr,
                               tell=(i == 1))
                    VEC.run(lambda e, b=b: e.reduce_max(mtop[0:1, :], b.ap[0:1, 0:S], AX.X), t, VEC.last())
                    mt = VEC.chain(lambda e: e.tensor_scalar(mtop[0:1, :], mtop[0:1, :], -1.0, None, ALU.mult))
                    b.free = [mt]
                    b = banks.take()
                    t = mm(b.ap[:, 0:1], ones[0:1, :], mtop[0:1, :], True, True, b.free, mt, tell=True)
                    nb = VEC.run(lambda e, b=b: e.tensor_copy(q2c[:, :], b.ap[:, 0:1]), t)
                    b.free = [nb]
                    er = SCA.run(lambda e: e.activation(eb[:, :], mx[:, 2:4], ACT.Exp, bias=q2c[:, 0:1]), nb)
                    b = banks.take()
                    for i in range(2):
                        mm(b.ap[:, 0:1], xn[:, 2 * bt + i, :], eb[:, i:i + 1], i == 0, i == 1, b.free, er, xnr)
                    for i in range(2):
                        t = mm(b.ap[:, 1:2], ones[:, :], eb[:, i:i + 1], i == 0, i == 1, tell=(i == 1))
                    VEC.run(lambda e, b=b: e.reciprocal(rb[:, :], b.ap[:, 1:2]), t)
                    q2 = VEC.chain(lambda e, b=b: e.tensor_scalar(q2c[:, :], b.ap[:, 0:1], rb[:, 0:1], None,
                                                                  ALU.mult), er)
                    b.free = [q2]
                    w14 = VEC.chain(lambda e: e.scalar_tensor_tensor(W14[:, :], Wl[:, 3, :], q2c[:, 0:1], Wl[:, 0, :],
                                                                     ALU.mult, ALU.add))
                    for i in range(2):
                        o = zb.ap[:, (2 * u + i) * P:(2 * u + i + 1) * P]
                        mm(o, ones[0:1, :], row[0:1, :], True, False, zb.free, w14, c2)
                        mm(o, xnT[:, tile(i)], W14[:, :], False, False)
                        mm(o, c2q[:, 0, i * P:(i + 1) * P], Wl[:, 1, :], False, False)
                        z = mm(o, c2q[:, 1, i * P:(i + 1) * P], Wl[:, 2, :], False, True, tell=(i == 1))
                    end = [z, er, w14]
                add_to_x(g, zb, z)

        def moe_swiglu(work):
            E, F, NX = 8, 512, 8
            FB = F // P
            wg, wu = WB[:, 0:4096], WB[:, 4096:8192]
            wd = WB[:, 8192:12288].rearrange("p (e k d) -> p e k d", e=NX, k=FB)
            wr = sb("wr1", [P, E], where=work)
            win = load_group("moe1", [(wr[:, :], ins["r1_w"]), (wg, ins["e1_g"]), (wu, ins["e1_u"]),
                                      (WB[:, 8192:12288], ins["e1_d"])], *region_free["B"])
            coef = sb("coef1", [P, TILES, E], where=work)
            tmp = (sb("lg1", [P, GT, E], where=work)[:, :, :], sb("top1", [P, GT, 8], where=work),
                   sb("ex1", [P, GT, E], where=work)[:, :, :], sb("ss1", [P, GT], where=work)[:, :])
            sg = Ring([sb(f"sg{i}", [P, GN], where=work)[:, :] for i in range(3)])
            hT = Ring([sb(f"hT1_{i}", [P, FB, GN], where=work)[:, :, :] for i in range(2)])
            for g in range(GROUPS):
                _, xT = norm_x(g)
                cf = coef[:, g * GT:(g + 1) * GT, :]
                c_ready = router(g, E, wr[:, :], None, "first", cf, tmp, win, xT)
                for ex in range(NX):
                    h = hT.take()
                    for k in range(FB):
                        c0 = ex * F + k * P
                        bg, bu, s = banks.take(), banks.take(), sg.take()
                        m1 = mm(bg.ap, wg[:, c0:c0 + P], xnT[:, g * GN:(g + 1) * GN], True, True, bg.free, xT, win,
                                tell=True)
                        m2 = mm(bu.ap, wu[:, c0:c0 + P], xnT[:, g * GN:(g + 1) * GN], True, True, bu.free, tell=True)
                        a = SCA.run(lambda e, s=s, bg=bg: e.activation(s.ap, bg.ap, ACT.Silu), m1, s.free)
                        bg.free = [a]
                        hd = VEC.run(lambda e, s=s, bu=bu, h=h, k=k: e.tensor_tensor(h.ap[:, k, :], bu.ap, s.ap,
                                                                                     ALU.mult), m2, a, h.free)
                        bu.free = s.free = [hd]
                    b = accs.take()
                    m = project_tokens(b, lambda t, k: h.ap[:, k, t * P:(t + 1) * P],
                                       [wd[:, ex, k, :] for k in range(FB)], None, hd, win)
                    h.free = [m]
                    if ex == NX - 1:
                        add_to_x(g, b, m)
                        continue
                    VEC.wait(x_ready[g])
                    for t in range(GT):
                        n = g * GT + t
                        v = VEC.run(lambda e, n=n, t=t, b=b, ex=ex: e.scalar_tensor_tensor(
                            x[:, n, :], b.ap[:, t * P:(t + 1) * P], coef[:, n, ex:ex + 1], x[:, n, :], ALU.mult,
                            ALU.add), m, c_ready)
                    b.free = [v]
                    x_ready[g] = [v]
            region_free["B"] = [PE.last()]

        def attention16(work):
            H, HD = 16, 8
            w = sb("w2", [P, 4, P], where=work)
            bcols = sb("bcols2", [P, 2], where=work)
            rows = sb("rows2", [1, 2, P], where=work)
            head4 = sb("head4", [P, 4], where=work)
            sel = sb("sel2", [P, 4 * P], where=work)
            selb = sb("selb2", [P, 4, P], BF16, where=work)
            mki = sb("mki", [P, TILES], I32, where=work)
            mri = sb("mri", [P, TILES * P], I32, where=work)
            keepr = sb("keepr", [P, TILES * P], where=work)
            flag = sb("flag", [P, 2, B], where=work)
            negc = sb("negc", [P, TILES], where=work)
            negr = sb("negr", [P, TILES * P], BF16, where=work)
            win = load_group("att16", [(w[:, :, :], ins["l2_w"]), (bcols[:, :], ins["l2_cols"]),
                                       (rows[0:1, :, :], ins["l2_rows"]), (head4[:, :], ins["c_retmask"][:, 0:4]),
                                       (sel[:, :], ins["c_sel16"]), (mki[:, :], ins["mask_cols"]),
                                       (mri[:, :], ins["mask_row"])])
            VEC.run(lambda e: e.tensor_copy(selb[:, :, :], sel[:, :].rearrange("p (h s) -> p h s", h=4)), win)
            VEC.run(lambda e: e.tensor_scalar(keepr[:, :], mri[:, :], 0.0, None, ALU.not_equal), win)
            VEC.chain(lambda e: e.reduce_max(flag[:, 0, :], keepr[:, :].rearrange("p (b s) -> p b s", b=B), AX.X))
            fl = VEC.chain(lambda e: e.tensor_scalar(flag[:, 1, :], flag[:, 0, :], float(HD) ** -0.5, None,
                                                     ALU.mult))
            VEC.run(lambda e: e.tensor_scalar(negc[:, :], mki[:, :], 0.0, NEG, ALU.is_equal, ALU.mult))
            VEC.chain(lambda e: e.tensor_tensor(
                negc[:, :].rearrange("p (b u) -> p b u", b=B), negc[:, :].rearrange("p (b u) -> p b u", b=B),
                flag[:, 0, :].unsqueeze(2).to_broadcast([P, B, 2]), ALU.mult))
            VEC.run(lambda e: e.tensor_scalar(keepr[:, :], keepr[:, :], -NEG, NEG, ALU.mult, ALU.add))
            VEC.chain(lambda e: e.tensor_tensor(
                negr[:, :].rearrange("p (b s) -> p b s", b=B), keepr[:, :].rearrange("p (b s) -> p b s", b=B),
                flag[:, 0, :].unsqueeze(2).to_broadcast([P, B, S]), ALU.mult))
            mask_ready = VEC.last()

            QT = sb("QT2", [P, S], where=work)
            KT = sb("KT2", [P, S], where=work)
            QTb = sb("QTb2", [P, S], BF16, where=work)
            QM = sb("QM2", [P, 4, S], where=work)
            KMb = sb("KMb2", [P, 4, S], BF16, where=work)
            V = sb("V2", [P, 2, H, HD + 1], where=work)
            nmx = sb("nmx2", [P, 2, 4, 32], where=work)
            nmT = sb("nmT2", [P, S], BF16, where=work)
            probs = Ring([sb(f"pr2_{i}", [P, 512], where=work)[:, :] for i in range(4)])
            rs = sb("rs2", [P, 2, H], where=work)
            att = sb("att2", [P, 2, P], where=work)
            attT = sb("attT2", [P, 2 * P], where=work)
            VEC.run(lambda e: e.memset(nmx[:, :, :, :], 0.0))
            v1 = VEC.run(lambda e: e.memset(V[:, :, :, HD:HD + 1], 1.0))
            end = [v1]
            for g in range(GROUPS):
                _, xT = norm_x(g)
                for u in range(2):
                    bt = 2 * g + u
                    tok = slice(bt * S, (bt + 1) * S)
                    b = banks.take()
                    qm = mm(b.ap[:, 0:S], w[:, 0, :], xnT[:, tok], True, True, b.free, xT, win, tell=True)
                    qr = VEC.run(lambda e, b=b: e.tensor_scalar(QT[:, :], b.ap[:, 0:S], bcols[:, 0:1],
                                                                flag[:, 1, bt:bt + 1], ALU.add, ALU.mult), qm, fl,
                                 *end)
                    b.free = [qr]
                    b = banks.take()
                    km = mm(b.ap[:, 0:S], w[:, 1, :], ctxT[:, tok], True, True, b.free, ctx_in, win, tell=True)
                    kr = SCA.run(lambda e, b=b: e.activation(KT[:, :], b.ap[:, 0:S], ACT.Identity,
                                                             bias=bcols[:, 1:2]), km, *end)
                    b.free = [kr]
                    qb = POOL.run(lambda e: e.tensor_copy(QTb[:, :], QT[:, :]), qr, *end)
                    for j in range(4):
                        kb = POOL.run(lambda e, j=j: e.tensor_scalar(KMb[:, j, :], KT[:, :], head4[:, j:j + 1], None,
                                                                     ALU.mult), kr, *end)
                    VEC.wait(qr)
                    for j in range(4):
                        qmr = VEC.run(lambda e, j=j: e.tensor_scalar(QM[:, j, :], QT[:, :], head4[:, j:j + 1], None,
                                                                     ALU.mult))
                    b = banks.take()
                    for i in range(2):
                        o = b.ap[:, i * P:(i + 1) * P]
                        mm(o, ones[0:1, :], rows[0:1, 0, :], True, False, b.free, win)
                        vm = mm(o, ctxT[:, bt * S + i * P:bt * S + (i + 1) * P], w[:, 2, :], False, True,
                                tell=(i == 1))
                    vr = SCA.run(lambda e, b=b: e.activation(
                        V[:, :, :, 0:HD], b.ap[:, 0:S].rearrange("p (u h e) -> p u h e", u=2, e=HD), ACT.Copy), vm,
                        v1, *end)
                    b.free = [vr]
                    for i in range(2):
                        for c in range(4):
                            for half in range(2):
                                r = slice(32 * c, 32 * c + 32)
                                b = banks.take()
                                mm(b.ap, QTb[r, i * P:(i + 1) * P], KMb[r, 2 * half:2 * half + 2, :], True, False,
                                   b.free, qb, kb)
                                m = mm(b.ap.rearrange("p (h s) -> p h s", h=2), onesb[32 * c:32 * c + 1, 0:P],
                                       negr[32 * c:32 * c + 1, tok].unsqueeze(1).to_broadcast([1, 2, S]), False, True,
                                       mask_ready, tell=True)
                                mr = VEC.run(lambda e, b=b, i=i: e.tensor_reduce(
                                    nmx[:, i, c, 2 * half:2 * half + 2], b.ap.rearrange("p (h s) -> p h s", h=2), AX.X, ALU.max,
                                    negate=True), m, *end)
                                b.free = [mr]
                    b = banks.take()
                    for i in range(2):
                        t = transpose(b.ap[:, i * P:(i + 1) * P], nmx[:, i, :, :].rearrange("p c j -> p (c j)"),
                                      ident[:, :], b.free, mr, tell=(i == 1))
                    nt = SCA.run(lambda e, b=b: e.activation(nmT[:, :], b.ap[:, 0:S], ACT.Copy), t, *end)
                    b.free = [nt]
                    av_banks = [accs.take(), accs.take()]
                    for c in range(4):
                        for half in range(2):
                            r = slice(32 * c, 32 * c + 32)
                            h0 = 4 * c + 2 * half
                            ps = []
                            for kt in range(2):
                                b = banks.take()
                                mm(b.ap, KT[r, kt * P:(kt + 1) * P], QM[r, 2 * half:2 * half + 2, :], True, False,
                                   b.free, kr, qmr)
                                for hh in range(2):
                                    m = mm(b.ap[:, hh * S:(hh + 1) * S], selb[r, 2 * half + hh, :], nmT[r, :], False, True,
                                           nt, tell=(hh == 1))
                                p = probs.take()
                                er = SCA.run(lambda e, p=p, b=b, kt=kt: e.activation(
                                    p.ap, b.ap, ACT.Exp, bias=negc[:, 2 * bt + kt:2 * bt + kt + 1]), m, p.free,
                                    mask_ready)
                                b.free = [er]
                                ps.append((p, er))
                            for hh in range(2):
                                for i in range(2):
                                    for kt in range(2):
                                        h = h0 + hh
                                        av = mm(av_banks[i].ap[:, h * 9:(h + 1) * 9],
                                                ps[kt][0].ap[:, hh * S + i * P:hh * S + (i + 1) * P],
                                                V[:, kt, h, :], kt == 0, kt == 1, av_banks[i].free, ps[kt][1], vr,
                                                tell=True)
                            for p, _ in ps:
                                p.free = [av]
                    for i in range(2):
                        o = av_banks[i].ap[:, 0:H * 9].rearrange("p (h e) -> p h e", e=9)
                        VEC.run(lambda e, o=o, i=i: e.reciprocal(rs[:, i, :], o[:, :, HD]), av, *end)
                        ar = VEC.chain(lambda e, o=o, i=i: e.tensor_tensor(
                            att[:, i, :].rearrange("p (h e) -> p h e", e=HD), o[:, :, 0:HD],
                            rs[:, i, :].unsqueeze(2).to_broadcast([P, H, HD]), ALU.mult))
                        av_banks[i].free = [ar]
                    tt = turn(att[:, :, :], attT[:, :], 2, ar, end)
                    b = banks.take()
                    for i in range(2):
                        o = b.ap[:, i * P:(i + 1) * P]
                        mm(o, ones[0:1, :], rows[0:1, 1, :], True, False, b.free, tt)
                        z = mm(o, attT[:, i * P:(i + 1) * P], w[:, 3, :], False, True, tell=(i == 1))
                    xr = VEC.run(lambda e: e.tensor_tensor(
                        x[:, 2 * bt:2 * bt + 2, :], b.ap[:, 0:2 * P].rearrange("p (t d) -> p t d", t=2),
                        x[:, 2 * bt:2 * bt + 2, :], ALU.add), z, x_ready[g])
                    b.free = [xr]
                    end = [z, tt, ar, er, kb]
                x_ready[g] = [xr]

        def bitnet(work):
            F = 512
            FB = F // P
            wf = sb("wf4", [P, 2, F], where=work)
            cv = sb("cv4", [P, FB, 4], where=work)
            win = load_group("bit", [(wf[:, :, :], ins["b_w"]), (cv[:, :, :], ins["b_conv"])])
            wq = sb("wq4", [P, 2, F], BF16, where=work)
            asum = sb("asum", [P, 2], where=work)
            wmean = sb("wmean", [P, 2], where=work)
            wsc = sb("wsc", [P, 2], where=work)
            VEC.run(lambda e: e.tensor_reduce(asum[:, :], wf[:, :, :], AX.X, ALU.add, apply_absolute_value=True), win)
            b = banks.take()
            t = mm(b.ap[:, 0:2], ones[:, :], asum[:, :], True, True, b.free, VEC.last(), tell=True)
            VEC.run(lambda e, b=b: e.tensor_scalar(wmean[:, :], b.ap[:, 0:2], 1.0 / (F * D), EPS, ALU.mult, ALU.max),
                    t)
            b.free = [VEC.last()]
            VEC.chain(lambda e: e.reciprocal(wsc[:, :], wmean[:, :]))
            VEC.wait(VEC.last())
            for k in range(2):
                VEC.run(lambda e, k=k: e.tensor_scalar(wf[:, k, :], wf[:, k, :], wsc[:, k:k + 1], ROUND, ALU.mult,
                                                       ALU.add))
            VEC.chain(lambda e: e.tensor_scalar(wf[:, :, :], wf[:, :, :], ROUND, 1.0, ALU.subtract, ALU.min))
            wr = VEC.chain(lambda e: e.tensor_scalar(wq[:, :, :], wf[:, :, :], -1.0, None, ALU.max))
            amax = sb("amax", [P, GT], where=work)
            qs = sb("qs", [P, GT], where=work)
            deq = sb("deq", [P, GT], where=work)
            rnd = sb("rnd", [P, GT, D], where=work)
            diag = sb("diag", [P, GT, P], where=work)
            xiT = sb("xiT", [P, GN], BF16, where=work)
            dq = sb("dq", [P, GN], where=work)
            hT = sb("hT4", [P, FB, GN], where=work)
            cT = sb("cT4", [P, FB, GN], where=work)
            sT = sb("sT4", [P, FB, GN], where=work)
            hr = sb("hr4", [P, FB, P], where=work)
            hi = sb("hi4", [P, F], BF16, where=work)
            hiT = sb("hiT4", [P, F], BF16, where=work)

            def scales(n, k, *after):
                a, q, d = amax[:, 0:n], qs[:, 0:n], deq[:, 0:n]
                VEC.chain(lambda e: e.tensor_scalar(a, a, EPS, None, ALU.max), *after)
                VEC.chain(lambda e: e.reciprocal(q, a))
                VEC.chain(lambda e: e.tensor_scalar(q, q, 127.0, None, ALU.mult))
                return VEC.chain(lambda e: e.tensor_scalar(d, a, 1.0 / 127.0, wmean[:, k:k + 1], ALU.mult, ALU.mult))

            end = []
            for g in range(GROUPS):
                xnr, xT = norm_x(g, *end)
                xg = xn[:, g * GT:(g + 1) * GT, :]
                VEC.chain(lambda e: e.tensor_reduce(amax[:, :], xg, AX.X, ALU.max, apply_absolute_value=True), *end)
                scales(GT, 0)
                VEC.wait(VEC.last())
                for t in range(GT):
                    VEC.run(lambda e, t=t: e.tensor_scalar(rnd[:, t, :], xg[:, t, :], qs[:, t:t + 1], ROUND, ALU.mult,
                                                           ALU.add))
                    VEC.run(lambda e, t=t: e.tensor_scalar(diag[:, t, :], ident[:, :], deq[:, t:t + 1], None,
                                                           ALU.mult))
                xi = VEC.chain(lambda e: e.tensor_scalar(rnd[:, :, :], rnd[:, :, :], ROUND, None, ALU.subtract))
                xt = turn(rnd[:, :, :], xiT[:, :], GT, xi, end)
                b = banks.take()
                for t in range(GT):
                    m = mm(b.ap[:, t * P:(t + 1) * P], ones[:, :], diag[:, t, :], True, True, b.free, xi,
                           tell=(t == GT - 1))
                dr = SCA.run(lambda e, b=b: e.activation(dq[:, :], b.ap, ACT.Copy), m, *end)
                b.free = [dr]
                for k in range(FB):
                    b = banks.take()
                    m = mm(b.ap, wq[:, 0, k * P:(k + 1) * P], xiT[:, :], True, True, b.free, xt, wr, tell=True)
                    h = VEC.run(lambda e, b=b, k=k: e.tensor_tensor(hT[:, k, :], b.ap, dq[:, :], ALU.mult), m, dr,
                                *end)
                    b.free = [h]
                    c = SCA.run(lambda e, k=k: e.activation(cT[:, k, :], hT[:, k, :], ACT.Identity,
                                                            scale=cv[:, k, 1:2], bias=cv[:, k, 3:4]), h, win, *end)
                    hb = hT[:, k, :].rearrange("p (b s) -> p b s", b=2)
                    cb = cT[:, k, :].rearrange("p (b s) -> p b s", b=2)
                    v = VEC.run(lambda e, hb=hb, cb=cb, k=k: e.scalar_tensor_tensor(
                        cb[:, :, 1:S], hb[:, :, 0:S - 1], cv[:, k, 0:1], cb[:, :, 1:S], ALU.mult, ALU.add), c)
                    v = VEC.chain(lambda e, hb=hb, cb=cb, k=k: e.scalar_tensor_tensor(
                        cb[:, :, 0:S - 1], hb[:, :, 1:S], cv[:, k, 2:3], cb[:, :, 0:S - 1], ALU.mult, ALU.add))
                    sr = SCA.run(lambda e, k=k: e.activation(sT[:, k, :], cT[:, k, :], ACT.Silu), v, *end)
                yb = accs.take()
                for t in range(GT):
                    b = banks.take()
                    for k in range(FB):
                        m = transpose(b.ap[:, k * P:(k + 1) * P], sT[:, k, t * P:(t + 1) * P], ident[:, :], b.free,
                                      sr, tell=(k == FB - 1))
                    VEC.chain(lambda e, b=b: e.tensor_reduce(amax[:, 0:1], b.ap, AX.X, ALU.max,
                                                             apply_absolute_value=True), m)
                    scales(1, 1)
                    r = VEC.chain(lambda e, b=b: e.tensor_scalar(hr[:, :, :].rearrange("p k d -> p (k d)"), b.ap,
                                                                 qs[:, 0:1], ROUND, ALU.mult, ALU.add))
                    b.free = [r]
                    r = VEC.chain(lambda e: e.tensor_scalar(hi[:, :], hr[:, :, :].rearrange("p k d -> p (k d)"),
                                                            ROUND, None, ALU.subtract), *end)
                    b = banks.take()
                    bb = b.ap.bitcast(BF16)
                    for k in range(FB):
                        m = transpose(bb[:, k * P:(k + 1) * P], hi[:, k * P:(k + 1) * P], identb[:, :], b.free, r,
                                      tell=(k == FB - 1))
                    ht = SCA.run(lambda e, bb=bb: e.activation(hiT[:, :], bb[:, 0:F], ACT.Copy), m, *end)
                    b.free = [ht]
                    for k in range(FB):
                        m = mm(yb.ap[:, t * P:(t + 1) * P], hiT[:, k * P:(k + 1) * P], wq[:, 1, k * P:(k + 1) * P],
                               k == 0, k == FB - 1, yb.free, ht, tell=(k == FB - 1))
                    n = g * GT + t
                    xr = VEC.run(lambda e, n=n, t=t: e.scalar_tensor_tensor(
                        x[:, n, :], yb.ap[:, t * P:(t + 1) * P], deq[:, 0:1], x[:, n, :], ALU.mult, ALU.add), m,
                        x_ready[g])
                    end = [m, xr, ht]
                yb.free = [xr]
                x_ready[g] = [xr]

        def split3(dst, src, tmp, *after):
            hi, mid, lo = dst
            a, c = tmp
            VEC.chain(lambda e: e.tensor_copy(a, src), *after)
            VEC.chain(lambda e: e.tensor_copy(hi, a))
            VEC.chain(lambda e: e.tensor_tensor(c, src, a, ALU.subtract))
            VEC.chain(lambda e: e.tensor_copy(a, c))
            VEC.chain(lambda e: e.tensor_copy(mid, a))
            VEC.chain(lambda e: e.tensor_tensor(c, c, a, ALU.subtract))
            VEC.chain(lambda e: e.tensor_copy(a, c))
            return VEC.chain(lambda e: e.tensor_copy(lo, a))

        def attention8(work):
            H, HD, M = 8, 64, 2 * S
            KT4 = M // P
            HB = H * HD // P
            Wq = WB[:, 0:512]
            Wkv = WB[:, 512:1536]
            Wo = WB[:, 1536:2048].rearrange("p (k d) -> p k d", k=HB)
            colw = sb("colw", [P, 6], where=work)
            lno = sb("lno", [P, 2, D], where=work)
            sel = sb("sel3f", [24, 3 * 512], where=work)
            selb = sb("sel3b", [24, 512], BF16, where=work)
            selm = sb("selmb", [H, H, P], BF16, where=work)
            blk2 = sb("blk2", [P, 2], where=work)
            mki = sb("mki3", [P, TILES], U8, where=work)
            mri = sb("mri3", [1, TILES * P], U8, where=work)
            negc = sb("negc3", [P, TILES], where=work)
            negr = sb("negr3", [1, TILES * P], BF16, where=work)
            win = load_group("att8", [(WB[:, 0:2048], ins["l3_w"]), (colw[:, :], ins["l3_cols"]),
                                      (lno[:, :, :], ins["l3_lno"]), (sel[:, :], ins["c_sel3"]),
                                      (blk2[:, :], ins["c_blk2"]), (mki[:, :], ins["bmask_cols"]),
                                      (mri[0:1, :], ins["bmask_row"])], *region_free["B"])
            VEC.run(lambda e: e.tensor_copy(selb[:, :], sel[:, 0:512]), win)
            VEC.run(lambda e: e.tensor_copy(selm[:, :, :], sel[0:H, 512:1536].rearrange("p (h s) -> p h s", h=H)))
            VEC.run(lambda e: e.tensor_scalar(negc[:, :], mki[:, :], 0.0, 1e30 * -1.0, ALU.is_equal, ALU.mult))
            VEC.run(lambda e: e.tensor_scalar(negr[0:1, :], mri[0:1, :], 0.0, 1e30 * -1.0, ALU.is_equal, ALU.mult))
            qk = sb("qkscale", [P, 1], where=work)
            c_ready = VEC.run(lambda e: e.tensor_scalar(qk[:, :], colw[:, 4:5], colw[:, 5:6], 8.0, ALU.mult, ALU.mult))

            lnt = sb("lnt", [P, GT, D], where=work)
            kvT = sb("kvT", [P, M], where=work)
            sq = sb("sq3", [P, M], where=work)
            raw = sb("raw3", [P, HB, M + S], where=work)
            rawb = sb("raw3b", [P, HB, M + S], BF16, where=work)
            parts = sb("parts3", [P, 6, 24], where=work)
            tA = sb("tA3", [P, 48], BF16, where=work)
            tB = sb("tB3", [P, 48], where=work)
            rT = sb("rT3", [24, 6 * P], BF16, where=work)
            V = sb("V3", [P, KT4, H, HD + 1], where=work)
            nmx = sb("nmx3", [P, 2, H], where=work)
            nmT = sb("nmT3", [H, S], BF16, where=work)
            probs = Ring([sb(f"pr3_{i}", [P, KT4, S], where=work)[:, :, :] for i in range(2)])
            rs = sb("rs3", [P, 4], where=work)
            att = sb("att3", [P, 2, H * HD], where=work)
            attT = sb("attT3", [P, HB, P], where=work)
            yln = sb("yln", [P, 1, D], where=work)
            v1 = VEC.run(lambda e: e.memset(V[:, :, :, HD:HD + 1], 1.0))
            end = []
            for g in range(GROUPS):
                norm_x(g, *end)
                for u in range(2):
                    bt = 2 * g + u
                    a = normalise(ctxt[:, 2 * bt:2 * bt + 2, :], lnt[:, 0:2, :], 2, ctx_in, *end)
                    t1 = turn(lnt[:, 0:2, :], kvT[:, 0:S], 2, a, [win] + end, colw[:, 0:1], colw[:, 1:2])
                    a = normalise(xn[:, 2 * bt:2 * bt + 2, :], lnt[:, 2:4, :], 2, VEC.last())
                    t2 = turn(lnt[:, 2:4, :], kvT[:, S:M], 2, a, [win] + end, colw[:, 2:3], colw[:, 3:4])
                    nb = accs.take()
                    first = True
                    for k in range(HB):
                        for side in range(2):
                            n0, n = (0, M) if side == 0 else (M, S)
                            src = kvT[:, 0:M] if side == 0 else kvT[:, S:M]
                            wgt = Wkv[:, k * P:(k + 1) * P] if side == 0 else Wq[:, k * P:(k + 1) * P]
                            b = banks.take()
                            m = mm(b.ap[:, 0:n], wgt, src, True, True, b.free, t1, t2, win, tell=True)
                            s2 = SCA.run(lambda e, b=b, n=n: e.activation(sq[:, 0:n], b.ap[:, 0:n], ACT.Square), m,
                                         PE.last(), *end)
                            rw = VEC.run(lambda e, b=b, n=n, n0=n0, k=k: e.tensor_copy(raw[:, k, n0:n0 + n],
                                                                                       b.ap[:, 0:n]), m, s2, *end)
                            b.free = [s2, rw]
                            for i in range(n // P):
                                tl = (0 if side == 0 else KT4) + i
                                m = mm(nb.ap[:, tl * 8 + 2 * k:tl * 8 + 2 * k + 2], sq[:, i * P:(i + 1) * P],
                                       blk2[:, :], first, True, nb.free, s2, tell=(i == n // P - 1))
                                first = False
                    VEC.chain(lambda e: e.tensor_scalar(rsq_v[:, 0:48], nb.ap[:, 0:48], 1e-24, None, ALU.max), m)
                    nb.free = [VEC.last()]
                    rsqrt(48)
                    pv = lambda j: parts[:, :, 8 * j:8 * j + 8]
                    as6 = lambda z: z.rearrange("p (t h) -> p t h", t=6)
                    pr = split3((pv(0), pv(1), pv(2)), as6(rsq_y[:, 0:48]), (as6(tA[:, :]), as6(tB[:, :])), *end)
                    b, b2 = banks.take(), banks.take()
                    for i in range(6):
                        dst = (b if i < 4 else b2).ap[0:24, (i % 4) * P:(i % 4 + 1) * P]
                        m = transpose(dst, parts[:, i, :], ident[:, :], b.free, b2.free, pr, tell=(i == 5))
                    SCA.run(lambda e, b=b: e.activation(rT[:, 0:512], b.ap[0:24, :], ACT.Copy), m, *end)
                    rt = SCA.run(lambda e, b2=b2: e.activation(rT[:, 512:768], b2.ap[0:24, 0:256], ACT.Copy))
                    b.free = b2.free = [rt]
                    for k in range(HB):
                        for side in range(2):
                            n0, n = (0, M) if side == 0 else (M, S)
                            b = banks.take()
                            m = mm(b.ap[:, 0:n], selb[:, k * P:(k + 1) * P], rT[:, n0:n0 + n], True, True, b.free, rt,
                                   c_ready, tell=True)
                            z = raw[:, k, n0:n0 + n]
                            if side == 0:
                                kr = VEC.run(lambda e, z=z, b=b, n=n: e.tensor_tensor(z, b.ap[:, 0:n], z, ALU.mult),
                                             m, rw)
                            else:
                                kr = VEC.run(lambda e, z=z, b=b, n=n: e.scalar_tensor_tensor(
                                    z, b.ap[:, 0:n], qk[:, 0:1], z, ALU.mult, ALU.mult), m, rw)
                            b.free = [kr]
                        kb = POOL.run(lambda e, k=k: e.tensor_copy(rawb[:, k, :], raw[:, k, :]), kr, *end)
                    for i in range(KT4):
                        b = banks.take()
                        m = mm(b.ap, kvT[:, i * P:(i + 1) * P], Wkv[:, 512:1024], True, True, b.free, t1, t2,
                               tell=True)
                        vr = SCA.run(lambda e, b=b, i=i: e.activation(
                            V[:, i, :, 0:HD], b.ap.rearrange("p (h e) -> p h e", e=HD), ACT.Copy), m, v1, *end)
                        b.free = [vr]
                    for h in range(H):
                        r = slice(64 * (h % 2), 64 * (h % 2) + 64)
                        for i in range(2):
                            b = banks.take()
                            mm(b.ap, rawb[r, h // 2, M + i * P:M + (i + 1) * P], rawb[r, h // 2, 0:M], True, False,
                               b.free, kb)
                            m = mm(b.ap[:, 0:S], onesb[0:1, 0:P], negr[0:1, bt * S:(bt + 1) * S], False, True,
                                   c_ready, tell=True)
                            mr = VEC.run(lambda e, b=b, i=i, h=h: e.tensor_reduce(nmx[:, i, h:h + 1], b.ap, AX.X,
                                                                                  ALU.max, negate=True), m, *end)
                            b.free = [mr]
                    b = banks.take()
                    for i in range(2):
                        t = transpose(b.ap[0:H, i * P:(i + 1) * P], nmx[:, i, :], ident[:, :], b.free, mr,
                                      tell=(i == 1))
                    nt = SCA.run(lambda e, b=b: e.activation(nmT[:, :], b.ap[0:H, 0:S], ACT.Copy), t, *end)
                    b.free = [nt]
                    for hq in range(2):
                        av_banks = [accs.take(), accs.take()]
                        for hh in range(4):
                            h = 4 * hq + hh
                            r = slice(64 * (h % 2), 64 * (h % 2) + 64)
                            p = probs.take()
                            for half in range(2):
                                b = banks.take()
                                for j in range(2):
                                    kt = 2 * half + j
                                    o = b.ap[:, j * S:(j + 1) * S]
                                    mm(o, raw[r, h // 2, kt * P:(kt + 1) * P], raw[r, h // 2, M:M + S], True, False,
                                       b.free, kr)
                                    m = mm(o, selm[:, h, :], nmT[:, :], False, True, nt, tell=(j == 1))
                                if half == 0:
                                    for j in range(2):
                                        er = SCA.run(lambda e, p=p, b=b, j=j: e.activation(
                                            p.ap[:, j, :], b.ap[:, j * S:(j + 1) * S], ACT.Exp,
                                            bias=negc[:, 2 * bt + j:2 * bt + j + 1]), m, p.free, c_ready)
                                else:
                                    er = SCA.run(lambda e, p=p, b=b: e.activation(
                                        p.ap[:, 2:4, :], b.ap.rearrange("p (j s) -> p j s", j=2), ACT.Exp), m,
                                        p.free)
                                b.free = [er]
                            for i in range(2):
                                for kt in range(KT4):
                                    av = mm(av_banks[i].ap[:, hh * 65:(hh + 1) * 65],
                                            p.ap[:, kt, i * P:(i + 1) * P], V[:, kt, h, :], kt == 0, kt == KT4 - 1,
                                            av_banks[i].free, er, vr, tell=True)
                            p.free = [av]
                        for i in range(2):
                            o = av_banks[i].ap[:, 0:260].rearrange("p (h e) -> p h e", e=65)
                            VEC.chain(lambda e, o=o: e.reciprocal(rs[:, :], o[:, :, HD]), av, *end)
                            ar = VEC.chain(lambda e, o=o, i=i, hq=hq: e.tensor_tensor(
                                att[:, i, hq * 256:(hq + 1) * 256].rearrange("p (h e) -> p h e", e=HD),
                                o[:, :, 0:HD], rs[:, :].unsqueeze(2).to_broadcast([P, 4, HD]), ALU.mult))
                            av_banks[i].free = [ar]
                    for i in range(2):
                        n = 2 * bt + i
                        tt = turn(att[:, i, :].rearrange("p (k d) -> p k d", k=HB),
                                  attT[:, :, :].rearrange("p k d -> p (k d)"), HB, ar, [PE.last()])
                        b = banks.take()
                        for k in range(HB):
                            m = mm(b.ap[:, 0:P], attT[:, k, :], Wo[:, k, :], k == 0, k == HB - 1, b.free, tt,
                                   tell=(k == HB - 1))
                        y = normalise(b.ap[:, 0:P].unsqueeze(1), yln[:, :, :], 1, m)
                        b.free = [y]
                        VEC.chain(lambda e: e.tensor_tensor(yln[:, 0, :], yln[:, 0, :], lno[:, 0, :], ALU.mult))
                        VEC.chain(lambda e: e.tensor_tensor(yln[:, 0, :], yln[:, 0, :], lno[:, 1, :], ALU.add))
                        xr = VEC.chain(lambda e, n=n: e.tensor_tensor(x[:, n, :], x[:, n, :], yln[:, 0, :], ALU.add),
                                       x_ready[g])
                    end = [m, xr, tt, er, kb, mr]
                x_ready[g] = [xr]
            region_free["B"] = [PE.last()]

        def moe_small(work):
            E, NP_ = 32, 32
            wg, wu = WA[:, 0:4096], WA[:, 4096:8192]
            wd = WA[:, 8192:12288].rearrange("p (e d) -> p e d", d=D)
            wr = sb("wr3", [P, 2 * E], where=work)
            self_ = sb("sel96f", [96, 16 * P], where=work)
            selb = sb("sel96b", [96, 16, P], BF16, where=work)
            win = load_group("moe3", [(wr[:, :], ins["r3_w"]), (self_[:, :], ins["c_sel96"]), (wg, ins["e3_g"]),
                                      (wu, ins["e3_u"]), (WA[:, 8192:12288], ins["e3_d"])], *region_free["A"])
            sr = VEC.run(lambda e: e.tensor_copy(selb[:, :, :], self_[:, :].rearrange("p (a b) -> p a b", a=16)), win)
            coef = sb("coef3", [P, GT, E], where=work)
            tmp = (sb("lg3", [P, GT, E], where=work)[:, :, :], sb("top3", [P, GT, 8], where=work),
                   sb("ex3", [P, GT, E], where=work)[:, :, :], sb("ss3", [P, GT], where=work)[:, :])
            parts = sb("parts5", [P, GT, 3 * E], where=work)
            tA = sb("tA5", [P, GT, E], BF16, where=work)
            tB = sb("tB5", [P, GT, E], where=work)
            cT = [sb(f"cT5_{r}", [3 * E, GN], BF16, where=work) for r in range(2)]
            sg = Ring([sb(f"sg3_{i}", [P, GN], where=work)[:, :] for i in range(3)])
            hh = Ring([sb(f"h3_{i}", [P, GN], where=work)[:, :] for i in range(3)])
            end = []
            for g in range(GROUPS):
                _, xT = norm_x(g)
                cts = []
                for r in range(2):
                    c = router(g, E, wr[:, r * E:(r + 1) * E], None, "half", coef[:, :, :], tmp, win, xT)
                    pr = split3(tuple(parts[:, :, j * E:(j + 1) * E] for j in range(3)), coef[:, :, :],
                                (tA[:, :, :], tB[:, :, :]), c, *([PE.last()] if r else end))
                    b = banks.take()
                    for t in range(GT):
                        m = transpose(b.ap[0:3 * E, t * P:(t + 1) * P], parts[:, t, :], ident[:, :], b.free, pr,
                                      tell=(t == GT - 1))
                    ct = SCA.run(lambda e, b=b, r=r: e.activation(cT[r][:, :], b.ap[0:3 * E, :], ACT.Copy), m, *end)
                    b.free = [ct]
                    cts.append(ct)
                yb = accs.take()
                for p in range(NP_):
                    r = p // 16
                    bg, bu, bc = banks.take(), banks.take(), banks.take()
                    m1 = mm(bg.ap, wg[:, p * P:(p + 1) * P], xnT[:, g * GN:(g + 1) * GN], True, True, bg.free, xT,
                            win, tell=True)
                    m2 = mm(bu.ap, wu[:, p * P:(p + 1) * P], xnT[:, g * GN:(g + 1) * GN], True, True, bu.free,
                            tell=True)
                    m3 = mm(bc.ap, selb[:, p % 16, :], cT[r][:, :], True, True, bc.free, cts[r], sr, tell=True)
                    s, h = sg.take(), hh.take()
                    a = SCA.run(lambda e, s=s, bg=bg: e.activation(s.ap, bg.ap, ACT.Silu), m1, s.free)
                    bg.free = [a]
                    v = VEC.run(lambda e, s=s, bu=bu: e.tensor_tensor(s.ap, bu.ap, s.ap, ALU.mult), m2, a)
                    bu.free = [v]
                    hd = VEC.run(lambda e, s=s, bc=bc, h=h: e.tensor_tensor(h.ap, bc.ap, s.ap, ALU.mult), m3, v,
                                 h.free)
                    bc.free = s.free = [hd]
                    for t in range(GT):
                        m = mm(yb.ap[:, t * P:(t + 1) * P], h.ap[:, t * P:(t + 1) * P], wd[:, p, :],
                               p == 0 and t == 0, p == NP_ - 1, yb.free, hd, tell=(t == GT - 1))
                    h.free = [m]
                add_to_x(g, yb, m)
                end = [m]
            region_free["A"] = [PE.last()]

        stages = {"L0x": retention, "L0f": moe_gelu, "L1x": bidaf, "L1f": moe_swiglu, "L2x": attention16,
                  "L2f": bitnet, "L3x": attention8, "L3f": moe_small}
        for name in LAYERS:
            with ExitStack() as work:
                fence()
                stages[name](work)
        fence()
        stored = sem("stored")
        SYNC.wait(*[t for g in range(GROUPS) for t in x_ready[g]])
        SYNC.eng.dma_start(out.rearrange("b (u p) d -> p (b u) d", p=P), x[:, :, :]).then_inc(stored, 16)
        SYNC.eng.wait_ge(stored, 16)


def constants():
    c = {}
    c["c_ident"] = np.eye(P, dtype=np.float32)
    H, HD = 16, 8
    half = HD // 2
    pair = np.repeat(np.arange(half), 2)
    base = (np.arange(0, HD, 2) + 0.4 * HD) / (1.4 * HD)
    power = (np.arange(-(S // 2), S // 2)) / 512.0
    scale = base[None, :] ** power[:, None]
    ang = (np.arange(S, dtype=np.float32)[:, None]
           * (1.0 / 10000.0 ** (np.arange(half, dtype=np.float32) / half)).astype(np.float32)[None, :]).astype(np.float64)
    gam = (1.0 - np.exp(np.linspace(np.log(1 / 32.0), np.log(1 / 512.0), H)).astype(np.float32)).astype(np.float64)
    mid = np.arange(S) - S // 2
    sign = np.where(np.arange(HD) % 2 == 0, -1.0, 1.0)
    tab = np.zeros((P, 4, S))
    for h in range(H):
        for e in range(HD):
            p = h * HD + e
            for side, (sc, dec) in enumerate(((scale[:, pair[e]], gam[h] ** mid), (1 / scale[:, pair[e]], gam[h] ** -mid))):
                tab[p, 2 * side] = np.cos(ang[:, pair[e]]) * sc * dec
                tab[p, 2 * side + 1] = np.sin(ang[:, pair[e]]) * sc * dec * sign[e]
    c["c_xpos"] = tab.astype(np.float32)
    m = np.zeros((P, 4 + P + 512), np.float32)
    p = np.arange(P)
    m[:, 0:4] = (p[:, None] // HD) % 4 == np.arange(4)[None, :]
    m[:, 4:4 + P] = p[:, None] // HD == p[None, :] // HD
    m[:, 4 + P:] = np.tile(p[None, :] >= p[:, None], (1, 4))
    c["c_retmask"] = m
    c["c_sel16"] = np.tile(np.repeat(np.eye(32, 4, dtype=np.float32), P, axis=1), (4, 1))
    sel3 = np.zeros((24, 1536), np.float32)
    sel3[:, 0:512] = np.tile(np.repeat(np.eye(8, dtype=np.float32), 64, axis=1), (3, 1))
    sel3[0:8, 512:1536] = np.repeat(np.eye(8, dtype=np.float32), P, axis=1)
    c["c_sel3"] = sel3
    c["c_blk2"] = (p[:, None] // 64 == np.arange(2)[None, :]).astype(np.float32)
    c["c_sel96"] = np.tile(np.repeat(np.eye(32, dtype=np.float32), 64, axis=1), (3, 1))
    return c


def layout(i):
    n = {k: np.asarray(v) for k, v in i.items()}
    f = dict(constants())
    f["x"], f["ctx_1024"] = n["x"], n["ctx_1024"]
    f["ctxT"] = n["ctx_1024"].reshape(B * S, D).T
    heads = lambda w: w.transpose(1, 0, 2).reshape(D, D)
    swap = np.arange(D) ^ 1
    wq, wk, wv = (heads(n["L0_xattn_W_" + c]) for c in "QKV")
    f["w_ret"] = np.stack([wq, wq[:, swap], wk, wk[:, swap], wv, n["L0_xattn_g_w"].T, n["L0_xattn_out_w"].T], axis=1)
    f["rows_ret"] = np.stack([n["L0_xattn_g_b"], n["L0_xattn_out_b"]])[None]
    f["r0_w"], f["r0_b"] = n["L0_ffn_router_w"].T, n["L0_ffn_router_b"][None]
    f["e0_w1"] = n["L0_ffn_w1"].transpose(2, 0, 1).reshape(D, -1)
    f["e0_b1"] = n["L0_ffn_b1"].reshape(8, 4, P).transpose(2, 0, 1).reshape(P, 32)
    f["e0_w2"] = n["L0_ffn_w2"].reshape(8, D, 4, P).transpose(3, 0, 2, 1).reshape(P, -1)
    f["e0_b2"] = n["L0_ffn_b2"]
    f["l1_W"] = n["L1_xattn_W_l"].reshape(D, 4, D).transpose(2, 1, 0)
    f["l1_cols"] = np.stack([n["L1_xattn_w_cq"], n["L1_xattn_w_q"], n["L1_xattn_w_c"]], axis=1)
    f["l1_bias"] = np.broadcast_to(np.stack([n["L1_xattn_b_c"], n["L1_xattn_b_q"], n["L1_xattn_b_cq"]])[None], (P, 3))
    f["l1_row"] = n["L1_xattn_b_l"][None]
    f["r1_w"] = n["L1_ffn_Wr"]
    for a, b in (("g", "Wg"), ("u", "Wu")):
        f["e1_" + a] = np.concatenate([n["L1_ffn_" + b], n["L1_ffn_" + b + "_s"][None]]).transpose(1, 0, 2).reshape(D, -1)
    wd = np.concatenate([n["L1_ffn_Wd"], n["L1_ffn_Wd_s"][None]])
    f["e1_d"] = wd.reshape(8, 4, P, D).transpose(2, 0, 1, 3).reshape(P, -1)
    f["l2_w"] = np.stack([n["L2_xattn_W" + c].T for c in "qkvo"], axis=1)
    f["l2_cols"] = np.stack([n["L2_xattn_bq"], n["L2_xattn_bk"]], axis=1)
    f["l2_rows"] = np.stack([n["L2_xattn_bv"], n["L2_xattn_bo"]])[None]
    f["mask_row"] = np.broadcast_to(n["mask_BxS2_ik0"].reshape(1, -1), (P, B * S))
    f["mask_cols"] = n["mask_BxS2_ik0"].reshape(TILES, P).T
    f["b_w"] = np.stack([n["L2_ffn_w1"].T, n["L2_ffn_w2"].reshape(D, 4, P).transpose(2, 1, 0).reshape(P, -1)], axis=1)
    f["b_conv"] = np.concatenate([n["L2_ffn_conv_w"].reshape(4, P, 3), n["L2_ffn_conv_b"].reshape(4, P, 1)],
                                 axis=2).transpose(1, 0, 2)
    f["l3_w"] = np.concatenate([n["L3_xattn_Wq"], n["L3_xattn_Wkv"],
                                n["L3_xattn_Wo"].reshape(4, P, D).transpose(1, 0, 2).reshape(P, -1)], axis=1)
    two = lambda v: np.tile(v, 2)
    f["l3_cols"] = np.stack([n["L3_xattn_ln_x_w"], n["L3_xattn_ln_x_b"], n["L3_xattn_ln_l_w"], n["L3_xattn_ln_l_b"],
                             two(n["L3_xattn_q_scale"]), two(n["L3_xattn_k_scale"])], axis=1)
    f["l3_lno"] = np.broadcast_to(np.stack([n["L3_xattn_ln_o_w"], n["L3_xattn_ln_o_b"]])[None], (P, 2, D))
    keep = n["mask_BxS2_bk0"]
    f["bmask_row"], f["bmask_cols"] = keep.reshape(1, -1), keep.reshape(TILES, P).T
    f["r3_w"] = np.concatenate([n["L3_ffn_router_w0"], n["L3_ffn_router_w1"]], axis=1)
    for a, b in (("g", "wg"), ("u", "wu")):
        f["e3_" + a] = np.concatenate([n[f"L3_ffn_{b}{r}"] for r in range(2)]).transpose(1, 0, 2).reshape(D, -1)
    f["e3_d"] = np.concatenate([n[f"L3_ffn_wd{r}"] for r in range(2)]).reshape(32, P, D).transpose(1, 0, 2).reshape(P, -1)
    return {k: np.ascontiguousarray(v) for k, v in f.items()}


def kernel(**inputs):
    import concourse.bacc as bacc
    from concourse.bass_utils import run_bass_kernel_spmd

    arrays = layout(inputs)
    nc = bacc.Bacc("TRN2", target_bir_lowering=False, num_devices=1)
    aps = {k: nc.dram_tensor(k + "_dram", a.shape, mybir.dt.from_np(a.dtype), kind="ExternalInput").ap()
           for k, a in arrays.items()}
    out = nc.dram_tensor("out_dram", (B, S, D), F32, kind="ExternalOutput").ap()
    build(nc, aps, out)
    r = run_bass_kernel_spmd(nc, [{k + "_dram": a for k, a in arrays.items()}], core_ids=[0])
    return r.results[0]["out_dram"]
```

```python
from contextlib import ExitStack

import numpy as np
import concourse.bass as bass
from concourse import mybir

F32, BF16, I32, U8 = mybir.dt.float32, mybir.dt.bfloat16, mybir.dt.int32, mybir.dt.uint8
ALU = mybir.AluOpType
ACT = mybir.ActivationFunctionType
AX = mybir.AxisListType

P = 128
B, S, D = 8, 256, 128
TILES = B * S // P
GROUPS = 4
GT = TILES // GROUPS
GN = GT * P
EPS = 1e-5
ROUND = 1.5 * 2.0 ** 23
NEG = -1e9
LAYERS = ("L0x", "L0f", "L1x", "L1f", "L2x", "L2f", "L3x", "L3f")


class Queue:

    def __init__(self, eng, sem):
        self.eng, self.sem, self.done, self.waited = eng, sem, 0, {}

    def wait(self, *tickets):
        for t in tickets:
            if t is None:
                continue
            if isinstance(t, list):
                self.wait(*t)
                continue
            sem, count = t
            if self.waited.get(sem.name, 0) < count:
                self.waited[sem.name] = count
                self.eng.wait_ge(sem, count)

    def run(self, issue, *after):
        self.wait(*after)
        self.done += 1
        issue(self.eng).then_inc(self.sem, 1)
        return (self.sem, self.done)

    def chain(self, issue, *after):
        return self.run(issue, self.last(), *after)

    def quiet(self, issue, *after):
        self.wait(*after)
        issue(self.eng)

    def last(self):
        return (self.sem, self.done) if self.done else None


class Buffer:

    def __init__(self, ap):
        self.ap, self.held, self.tickets = ap, False, []

    @property
    def free(self):
        return self.tickets

    @free.setter
    def free(self, tickets):
        self.tickets, self.held = tickets, False


class Ring:
    def __init__(self, aps):
        self.buffers, self.at = [Buffer(a) for a in aps], 0

    def take(self):
        for _ in self.buffers:
            b = self.buffers[self.at % len(self.buffers)]
            self.at += 1
            if not b.held:
                b.held = True
                return b
        raise AssertionError("every buffer of the ring is held")


class Arena:

    def __init__(self, ap, words):
        self.slab, self.words, self.at, self.users = ap, words, 0, []

    def enter(self):
        self.at = 0
        return self.users

    def cut(self, shape, dt=F32):
        n = int(np.prod(shape[1:]))
        words = n if dt in (F32, I32) else (n + 1) // 2 if dt == BF16 else (n + 3) // 4
        words += words % 2
        v = self.slab[0:shape[0], self.at:self.at + words]
        self.at += words
        assert self.at <= self.words, (self.at, self.words)
        if dt != F32:
            v = v.bitcast(dt)
        v = v[:, 0:n]
        if len(shape) == 3:
            v = v.rearrange("p (a b) -> p a b", a=shape[1])
        if len(shape) == 4:
            v = v.rearrange("p (a b c) -> p a b c", a=shape[1], b=shape[2])
        return v


def build(nc, ins, out):
    ctx = ExitStack()
    with ctx:
        def sem(name):
            return ctx.enter_context(nc.semaphore(name))

        PE, VEC, SCA, POOL = (Queue(eng, sem(n)) for eng, n in (
            (nc.tensor, "pe_done"), (nc.vector, "vec_done"), (nc.scalar, "sca_done"), (nc.gpsimd, "pool_done")))
        SYNC = Queue(nc.sync, None)

        def sb(name, shape, dt=F32):
            t = ctx.enter_context(nc.sbuf_tensor(name, shape, dt))
            return t[tuple(slice(None) for _ in shape)]

        def load_group(name, pairs, *after):
            s = sem("in_" + name)
            SYNC.wait(*after)
            for dst, src in pairs:
                SYNC.eng.dma_start(dst, src).then_inc(s, 16)
            return (s, 16 * len(pairs))

        x = sb("x", [P, TILES, D])
        xn = sb("xn", [P, TILES, D])
        xnT = sb("xnT", [P, TILES * P])
        ctxt = sb("ctxt", [P, TILES, D])
        ctxT = sb("ctxT", [P, TILES * P])
        ident = sb("ident", [P, P])
        identb = sb("identb", [P, P], BF16)
        ones = sb("ones", [P, P])
        row0 = sb("row0", [P, P], BF16)
        stats = sb("stats", [P, GT, 6])
        meanvar = sb("meanvar", [P, GT, 2])
        rsq_v = sb("rsq_v", [P, 64])
        rsq_i = sb("rsq_i", [P, 64], I32)
        rsq_y = sb("rsq_y", [P, 64])
        rsq_t = sb("rsq_t", [P, 64])
        psum = [ctx.enter_context(nc.psum_tensor(f"bank{i}", [P, 512], F32)) for i in range(8)]
        banks = Ring([b[:, :] for b in psum[0:6]])
        accs = Ring([b[:, :] for b in psum[6:8]])

        SIZES = {"A": 12288, "B": 12288, "C": 7500, "E": 3900, "W": 5500}
        slab = {k: Arena(sb("slab" + k, [P, n]), n) for k, n in SIZES.items()}
        keep = slab["W"].cut

        x_v = ins["x"].rearrange("b (u p) d -> p (b u) d", p=P)
        c_v = ins["ctx_1024"].rearrange("b (u p) d -> p (b u) d", p=P)
        x_in = load_group("x", [(x, x_v)])
        const_in = load_group("const", [(ident, ins["c_ident"])])
        ctx_in = load_group("ctx", [(ctxT, ins["ctxT"]), (ctxt, c_v)])
        ones_set = VEC.run(lambda e: e.memset(ones, 1.0))
        VEC.run(lambda e: e.memset(row0, 0.0))
        row0_set = VEC.chain(lambda e: e.memset(row0[0:1, :], 1.0))
        identb_set = VEC.run(lambda e: e.tensor_copy(identb, ident), const_in)
        PE.wait(const_in, ones_set, row0_set, identb_set)
        x_ready = [[x_in] for _ in range(TILES)]
        xn_free = [[] for _ in range(TILES)]

        def mm(dst, lhsT, rhs, start, stop, *after, tell=False):
            f = lambda e: e.matmul(dst, lhsT, rhs, start=start, stop=stop, skip_group_check=True)
            return PE.run(f, *after) if tell else PE.quiet(f, *after)

        def transpose(dst, src, idt, *after, tell=False):
            f = lambda e: e.transpose(dst, src, idt)
            return PE.run(f, *after) if tell else PE.quiet(f, *after)

        def rsqrt(n, *after):
            v, i, y, t = rsq_v[:, 0:n], rsq_i[:, 0:n], rsq_y[:, 0:n], rsq_t[:, 0:n]
            VEC.chain(lambda e: e.tensor_scalar(i, v.bitcast(I32), 1, None, ALU.logical_shift_right), *after)
            VEC.chain(lambda e: e.tensor_scalar(y.bitcast(I32), i, -1.0, float(0x5F3759DF), ALU.mult, ALU.add))
            for _ in range(3):
                VEC.chain(lambda e: e.tensor_tensor(t, y, y, ALU.mult))
                VEC.chain(lambda e: e.tensor_tensor(t, t, v, ALU.mult))
                VEC.chain(lambda e: e.tensor_scalar(t, t, -0.5, 1.5, ALU.mult, ALU.add))
                VEC.chain(lambda e: e.tensor_tensor(y, y, t, ALU.mult))
            return VEC.last()

        def normalise(src, dst, n, *after):
            VEC.wait(*after)
            VEC.wait(VEC.last())
            for k in range(n):
                VEC.run(lambda e: e.bn_stats(stats[:, k, :], src[:, k, :]))
            VEC.wait(VEC.last())
            for k in range(n):
                VEC.run(lambda e: e.bn_aggr(meanvar[:, k, :], stats[:, k, :]))
            VEC.chain(lambda e: e.tensor_scalar(rsq_v[:, 0:n], meanvar[:, 0:n, 1], EPS, None, ALU.add))
            rsqrt(n)
            VEC.wait(VEC.last())
            for k in range(n):
                done = VEC.run(lambda e: e.tensor_scalar(dst[:, k, :], src[:, k, :], meanvar[:, k, 0:1],
                                                         rsq_y[:, k:k + 1], ALU.subtract, ALU.mult))
            return done

        def turn(src, dst, n, ready, dst_free=(), scale=None, bias=None):
            b = banks.take()
            for k in range(n):
                t = transpose(b.ap[:, k * P:(k + 1) * P], src[:, k, :], ident, b.free, ready, tell=(k == n - 1))
            if scale is None:
                done = SCA.run(lambda e: e.activation(dst, b.ap[:, 0:n * P], ACT.Copy), t, *dst_free)
            else:
                done = SCA.run(lambda e: e.activation(dst, b.ap[:, 0:n * P], ACT.Identity, scale=scale, bias=bias),
                               t, *dst_free)
            b.free = [done]
            return done

        def norm_x(t0, n):
            ts = slice(t0, t0 + n)
            free = [f for k in range(t0, t0 + n) for f in xn_free[k]]
            done = normalise(x[:, ts, :], xn[:, ts, :], n, *(x_ready[ts] + free))
            return done, turn(xn[:, ts, :], xnT[:, t0 * P:(t0 + n) * P], n, done, free)

        def x_written(t0, n, ticket):
            for k in range(t0, t0 + n):
                x_ready[k] = [ticket]

        def xn_read(t0, n):
            for k in range(t0, t0 + n):
                xn_free[k] = all_last()

        def add_to_x(t0, n, bank, ready):
            t = VEC.run(lambda e: e.tensor_tensor(x[:, t0:t0 + n, :],
                                                  bank.ap[:, 0:n * P].rearrange("p (t d) -> p t d", t=n),
                                                  x[:, t0:t0 + n, :], ALU.add), ready, *x_ready[t0:t0 + n])
            bank.free = [t]
            x_written(t0, n, t)

        def project_tokens(bank, n, lhs_of, weights, bias_row, ready, *after):
            for t in range(n):
                o = bank.ap[:, t * P:(t + 1) * P]
                if bias_row is not None:
                    mm(o, ones[0:1, :], bias_row, True, False, bank.free, ready, *after)
                for k, w in enumerate(weights):
                    done = mm(o, lhs_of(t, k), w, bias_row is None and k == 0, k == len(weights) - 1,
                              bank.free, ready, *after, tell=(k == len(weights) - 1))
            return done

        def all_last():
            return [q.last() for q in (PE, VEC, SCA, POOL)]

        def enter(*names):
            return [t for k in names for t in slab[k].enter()]

        def leave(*names):
            for k in names:
                slab[k].users = all_last()

        def head_front(t):
            return slice(t * P, (t + 1) * P)

        def retention():
            H, HD = 16, 8
            cut, cute, cutc = slab["B"].cut, slab["E"].cut, slab["C"].cut
            w = cut([P, 7, P])
            rows = cut([1, 2, P])
            tab = cut([P, 4, S])
            masks = cut([P, 16 + P + 512])
            win = load_group("ret", [(w, ins["w_ret"]), (rows[0:1], ins["rows_ret"]),
                                     (tab, ins["c_xpos"]), (masks, ins["c_retmask"])])
            head16, blockdiag, causal = masks[:, 0:16], masks[:, 16:16 + P], masks[:, 16 + P:]
            PITCH = GT * P + HD
            VM = cut([P, H * PITCH])
            VMw = VM.rearrange("p (h r) -> p h r", r=PITCH)[:, :, 0:GT * P].rearrange(
                "p h (t d) -> p h t d", t=GT)[:, :, :, 0:HD]
            VMr = lambda h, t: VM[:, (h * GT + t) * P:(h * GT + t + 1) * P]
            masked = Ring([cute([P, 4, S]), cutc([P, 4, S])])
            probs = Ring([cute([P, 512]) for _ in range(3)])
            QT, KT = cutc([P, GN]), cutc([P, GN])
            rot = cutc([P, 2, GN])
            Ktok, state, V = cutc([P, 2, P]), cutc([P, 2, P]), cutc([P, 2, P])
            mu = cutc([P, 64])
            cen, sq, gate = cutc([P, 512]), cutc([P, 512]), cutc([P, 512])
            yT = sq
            zeroed = POOL.run(lambda e: e.memset(VM, 0.0))
            front_end, tail_end = [], []
            yield "loaded"
            heads = lambda a: a.rearrange("p (h e) -> p h e", e=HD)
            wide = lambda a: a.unsqueeze(2).to_broadcast([P, 64, HD])
            def unit(g):
                nonlocal front_end, tail_end
                _, xT = norm_x(g * GT, GT)
                yield
                cols = slice(g * GN, (g + 1) * GN)

                def rotated(dst, k, src, t0, ready):
                    made = []
                    VEC.wait(VEC.last())
                    for j in range(2):
                        b = banks.take()
                        m = mm(b.ap, w[:, k + j, :], src[:, cols], True, True, b.free, ready, win, tell=True)
                        v = VEC.run(lambda e: e.tensor_tensor(
                            rot[:, j, :].rearrange("p (b s) -> p b s", b=2), b.ap.rearrange("p (b s) -> p b s", b=2),
                            tab[:, t0 + j:t0 + j + 1, :].to_broadcast([P, 2, S]), ALU.mult), m, win, *front_end)
                        b.free = [v]
                        made.append(v)
                    return VEC.chain(lambda e: e.tensor_tensor(dst, rot[:, 0, :], rot[:, 1, :], ALU.add), made)

                q_ready = rotated(QT, 0, xnT, 0, xT)
                k_ready = rotated(KT, 2, ctxT, 2, ctx_in)
                b = banks.take()
                v_mm = project_tokens(b, GT, lambda t, k: ctxT[:, head_front(g * GT + t)], [w[:, 4, :]], None, win,
                                      ctx_in)
                v_ready = SCA.run(lambda e: e.activation(V, b.ap.rearrange("p (t c d) -> p t c d", t=2, c=2)[:, :, 0, :],
                                                         ACT.Copy), v_mm, *front_end)
                vm_ready = SCA.run(lambda e: e.activation(
                    VMw, b.ap.rearrange("p (t h e) -> p h t e", t=GT, e=HD), ACT.Copy), zeroed, *front_end)
                b.free = [vm_ready]
                yield
                b = banks.take()
                for u in range(2):
                    t = transpose(b.ap[:, u * P:(u + 1) * P], KT[:, 2 * u * P:(2 * u + 1) * P], ident,
                                  b.free, k_ready, tell=(u == 1))
                ktok = SCA.run(lambda e: e.activation(Ktok, b.ap[:, 0:2 * P].rearrange("p (t d) -> p t d", t=2),
                                                      ACT.Copy), t, *front_end)
                b.free = [ktok]
                b = banks.take()
                for u in range(2):
                    t = mm(b.ap[:, u * P:(u + 1) * P], Ktok[:, u, :], V[:, u, :], True, True, b.free, ktok,
                           v_ready, tell=(u == 1))
                st = VEC.run(lambda e: e.tensor_tensor(
                    state, b.ap[:, 0:2 * P].rearrange("p (t d) -> p t d", t=2),
                    blockdiag.unsqueeze(1).to_broadcast([P, 2, P]), ALU.mult), t, *front_end)
                b.free = [st]
                ret = accs.take()
                for u in range(2):
                    t = 2 * u + 1
                    mm(ret.ap[:, head_front(t)], QT[:, head_front(t)], state[:, u, :], u == 0, False, ret.free, st,
                       q_ready)
                late = []

                def product(p, pr, c, t):
                    for j in range(4):
                        av = mm(ret.ap[:, head_front(t)], p.ap[:, j * P:(j + 1) * P], VMr(4 * c + j, t), False, True,
                                pr, vm_ready, tell=(j == 3))
                    p.free = [av]
                    return av

                for u in range(2):
                    for c in range(4):
                        q = masked.take()
                        for j in range(4):
                            f = lambda e: e.tensor_scalar(q.ap[:, j, :], QT[:, u * S:(u + 1) * S],
                                                          head16[:, 4 * c + j:4 * c + j + 1], None, ALU.mult)
                            if j % 2:
                                qm = VEC.run(f, q_ready, q.free)
                            else:
                                qp = POOL.run(f, q_ready, q.free)
                        for i in range(2):
                            t = 2 * u + i
                            b = banks.take()
                            s_mm = mm(b.ap, KT[:, head_front(t)], q.ap[:, :, i * P:(i + 1) * P], True, True, b.free,
                                      qm, qp, k_ready, tell=True)
                            p = probs.take()
                            pr = VEC.run(lambda e: e.tensor_tensor(p.ap, b.ap, causal, ALU.mult), s_mm, p.free)
                            b.free = [pr]
                            late.append((p, pr, c, t))
                            if len(late) > 1:
                                product(*late.pop(0))
                        q.free = [s_mm]
                    yield
                while late:
                    av = product(*late.pop(0))
                front_end = all_last()
                yield "next"
                b = banks.take()
                g_mm = project_tokens(b, GT, lambda t, k: xnT[:, head_front(g * GT + t)], [w[:, 5, :]],
                                      rows[0:1, 0, :], xT, win)
                gate_ready = SCA.run(lambda e: e.activation(gate, b.ap, ACT.Silu), g_mm, *tail_end)
                b.free = [gate_ready]
                VEC.run(lambda e: e.reduce_sum(mu, heads(ret.ap), AX.X), av, VEC.last())
                VEC.chain(lambda e: e.tensor_scalar(mu, mu, 1.0 / HD, None, ALU.mult))
                c_ready = VEC.chain(lambda e: e.tensor_tensor(heads(cen), heads(ret.ap), wide(mu), ALU.subtract),
                                    *tail_end)
                ret.free = [c_ready]
                sq_ready = SCA.run(lambda e: e.activation(sq, cen, ACT.Square), c_ready, *tail_end)
                VEC.chain(lambda e: e.reduce_sum(rsq_v, heads(sq), AX.X), sq_ready)
                VEC.chain(lambda e: e.tensor_scalar(rsq_v, rsq_v, 1.0 / HD, EPS, ALU.mult, ALU.add))
                rsqrt(64)
                VEC.chain(lambda e: e.tensor_tensor(heads(cen), heads(cen), wide(rsq_y), ALU.mult))
                y_ready = VEC.chain(lambda e: e.tensor_tensor(cen, cen, gate, ALU.mult), gate_ready)
                yt = turn(cen.rearrange("p (t d) -> p t d", t=GT), yT, GT, y_ready)
                b = banks.take()
                o_mm = project_tokens(b, GT, lambda t, k: yT[:, head_front(t)], [w[:, 6, :]], rows[0:1, 1, :], yt)
                add_to_x(g * GT, GT, b, o_mm)
                xn_read(g * GT, GT)
                tail_end = all_last()
                yield

            for g in range(GROUPS):
                yield unit(g)

        def router(g, E, w_r, bias_row, kind, coef, tmp, ready, xT, *free):
            logits, top, ex, ssum = tmp
            b = banks.take()
            for t in range(GT):
                o = b.ap[:, t * P:(t + 1) * P]
                if bias_row is not None:
                    mm(o, ones[0:1, :], bias_row, True, False, b.free, xT, ready)
                m = mm(o, xnT[:, head_front(g * GT + t)], w_r, bias_row is None, True, b.free, xT, ready,
                       tell=(t == GT - 1))
            made = []
            for r in range(len(coef)):
                lg = VEC.chain(lambda e: e.tensor_copy(
                    logits, b.ap.rearrange("p (t e) -> p t e", t=GT)[:, :, r * E:(r + 1) * E]), m, *free)
                VEC.wait(lg)
                for t in range(GT):
                    VEC.run(lambda e: e.max(top[:, t, :], logits[:, t, :]))
                sub = VEC.chain(lambda e: e.tensor_tensor(ex, logits, top[:, :, 0:1].to_broadcast([P, GT, E]),
                                                          ALU.subtract))
                exd = SCA.run(lambda e: e.activation(ex, ex, ACT.Exp), sub)
                k = 0 if kind == "first" else 1
                VEC.chain(lambda e: e.tensor_tensor(logits, logits, top[:, :, k:k + 1].to_broadcast([P, GT, E]),
                                                    ALU.is_ge))
                if kind != "pair":
                    VEC.chain(lambda e: e.reduce_sum(ssum, ex, AX.X), exd)
                VEC.chain(lambda e: e.tensor_tensor(ex, ex, logits, ALU.mult), exd)
                if kind == "pair":
                    VEC.chain(lambda e: e.reduce_sum(ssum, ex, AX.X))
                VEC.chain(lambda e: e.reciprocal(ssum, ssum))
                if kind != "pair":
                    VEC.chain(lambda e: e.tensor_scalar(ssum, ssum, 2.0 if kind == "first" else 0.5, None, ALU.mult))
                made.append(VEC.chain(lambda e: e.tensor_tensor(
                    coef[r], ex, ssum.unsqueeze(2).to_broadcast([P, GT, E]), ALU.mult)))
            b.free = [made[-1]]
            return made

        def router_scratch(cut, E):
            return cut([P, GT, E]), cut([P, GT, 8]), cut([P, GT, E]), cut([P, GT])

        def lagged(blocks, up, down, lag, pause):
            pend = []
            for n, blk in enumerate(blocks):
                pend.append((blk, up(blk)))
                if len(pend) > lag:
                    down(*pend.pop(0))
                if n % pause == pause - 1:
                    yield
            for p in pend:
                down(*p)
            yield

        def moe_gelu():
            E, F = 8, 512
            FB = F // P
            w1 = slab["A"].cut([P, E * F])
            w2 = slab["A"].cut([P, E * FB, D])
            b1, b2, wr, br = keep([P, E * FB]), keep([E, D]), keep([P, P]), keep([1, P])
            win = load_group("moe0", [(wr, ins["r0_w"]), (br, ins["r0_b"]), (b1, ins["e0_b1"]), (b2, ins["e0_b2"]),
                                      (w1, ins["e0_w1"]), (w2.rearrange("p a d -> p (a d)"), ins["e0_w2"])])
            yield "loaded"
            free = enter("C")
            cut = slab["C"].cut
            coefs = [cut([P, GT, E]) for _ in range(2)]
            tmp = router_scratch(cut, E)
            coefT = cut([E, GN])
            hs = Ring([cut([P, GN]) for _ in range(6)])
            for k in hs.buffers:
                k.tickets = free
            b2_done = list(free)
            def unit(g):
                nonlocal b2_done
                coef = coefs[g % 2]
                _, xT = norm_x(g * GT, GT)
                yield
                c_ready, = router(g, E, wr, br, "pair", [coef], tmp, win, xT, *free)
                b = banks.take()
                for t in range(GT):
                    m = transpose(b.ap[0:E, t * P:(t + 1) * P], coef[:, t, :], ident, b.free, c_ready,
                                  tell=(t == GT - 1))
                ct = SCA.run(lambda e: e.activation(coefT, b.ap[0:E, :], ACT.Copy), m, *b2_done)
                b.free = [ct]
                yield
                b = banks.take()
                for t in range(GT):
                    m = mm(b.ap[:, head_front(t)], coefT[:, head_front(t)], b2, True, True, b.free, ct,
                           win, tell=(t == GT - 1))
                b2_done = [m]
                add_to_x(g * GT, GT, b, m)
                acc = {}

                def up(blk):
                    b, h = banks.take(), hs.take()
                    m = mm(b.ap, w1[:, blk * P:(blk + 1) * P], xnT[:, g * GN:(g + 1) * GN], True, True, b.free, xT,
                           win, tell=True)
                    done = SCA.run(lambda e: e.activation(h.ap, b.ap, ACT.Gelu, bias=b1[:, blk:blk + 1]), m, h.free)
                    b.free = [done]
                    return h, done

                def down(blk, made):
                    h, done = made
                    ex, k = divmod(blk, FB)
                    if k == 0:
                        acc[0] = accs.take()
                    b = acc[0]
                    for t in range(GT):
                        m = mm(b.ap[:, head_front(t)], h.ap[:, head_front(t)], w2[:, blk, :], k == 0 and t == 0,
                               k == FB - 1, b.free, done, tell=(t == GT - 1))
                    h.free = [m]
                    if k == FB - 1:
                        for t in range(GT):
                            n = g * GT + t
                            v = VEC.run(lambda e: e.scalar_tensor_tensor(
                                x[:, n, :], b.ap[:, head_front(t)], coef[:, t, ex:ex + 1], x[:, n, :], ALU.mult,
                                ALU.add), m, c_ready, x_ready[n])
                            x_ready[n] = [v]
                        b.free = [v]

                for n, y in enumerate(lagged(range(E * FB), up, down, 2, FB)):
                    yield "next" if n == E - 3 else None
                xn_read(g * GT, GT)

            for g in range(GROUPS):
                yield unit(g)

        def bidaf():
            Wl, cols, bias3, row = keep([P, 4, D]), keep([P, 3]), keep([P, 3]), keep([1, D])
            win = load_group("bidaf", [(Wl, ins["l1_W"]), (cols, ins["l1_cols"]), (bias3, ins["l1_bias"]),
                                       (row, ins["l1_row"])])
            yield "loaded"
            free = enter("E")
            cut = slab["E"].cut
            sets = [dict(cw=cut([P, S]), attn=cut([P, 2, S]), aT=cut([P, 2, S]), c2q=cut([P, 2, S]),
                         mx=cut([P, 4]), nm=cut([P, 2]), sm=cut([P, 2]), rs=cut([P, 2]), mtop=cut([1, 2]),
                         eb=cut([P, 2]), rb=cut([P, 2]), q2c=cut([P, 2]), W14=cut([P, D]), end=list(free))
                    for _ in range(2)]
            bsum = keep([P, 2])
            VEC.run(lambda e: e.reduce_sum(bsum[:, 0:1], bias3, AX.X), win)
            def unit(bt):
                z = sets[bt % 2]
                end = z["end"]
                cw, attn, aT, c2q, mx, nm, sm, rs, mtop, eb, rb, q2c, W14 = (
                    z[k] for k in ("cw", "attn", "aT", "c2q", "mx", "nm", "sm", "rs", "mtop", "eb", "rb", "q2c",
                                   "W14"))
                xnr, xT = norm_x(2 * bt, 2)
                yield
                tok = slice(bt * S, (bt + 1) * S)
                tile = lambda i: slice(bt * S + i * P, bt * S + (i + 1) * P)
                cwr = VEC.run(lambda e: e.tensor_scalar(cw, xnT[:, tok], cols[:, 0:1], cols[:, 1:2],
                                                        ALU.mult, ALU.add), xT, win, *end)
                b = banks.take()
                for i in range(2):
                    s_mm = mm(b.ap[:, i * S:(i + 1) * S], cw[:, i * P:(i + 1) * P], ctxT[:, tok], True, True,
                              b.free, cwr, ctx_in, tell=(i == 1))
                bc = banks.take()
                for i in range(2):
                    c_mm = mm(bc.ap[:, i:i + 1], xnT[:, tile(i)], cols[:, 2:3], True, True, bc.free, xT, win,
                              tell=(i == 1))
                yield
                VEC.wait(VEC.last())
                VEC.run(lambda e: e.reduce_max(mx[:, 0:2], b.ap.rearrange("p (i s) -> p i s", i=2), AX.X), s_mm)
                nmr = VEC.chain(lambda e: e.tensor_scalar(nm, mx[:, 0:2], -1.0, None, ALU.mult))
                mr = VEC.chain(lambda e: e.scalar_tensor_tensor(mx[:, 2:4], bc.ap[:, 0:2], bsum[:, 0:1],
                                                                mx[:, 0:2], ALU.add, ALU.add), c_mm)
                bc.free = [mr]
                for i in range(2):
                    ex = SCA.run(lambda e: e.activation(attn[:, i, :], b.ap[:, i * S:(i + 1) * S], ACT.Exp,
                                                        bias=nm[:, i:i + 1], accum_out=sm[:, i:i + 1]), nmr, *end)
                b.free = [ex, mr]
                b = banks.take()
                for i in range(2):
                    t = mm(b.ap[0:1, i * P:(i + 1) * P], mx[:, 2 + i:3 + i], ident, True, True, b.free, mr,
                           tell=(i == 1))
                yield
                VEC.chain(lambda e: e.reciprocal(rs, sm), ex)
                VEC.wait(VEC.last())
                for i in range(2):
                    ar = VEC.run(lambda e: e.tensor_scalar(attn[:, i, :], attn[:, i, :], rs[:, i:i + 1],
                                                           None, ALU.mult))
                VEC.run(lambda e: e.reduce_max(mtop[0:1, 0:1], b.ap[0:1, 0:S], AX.X), t, *end)
                mt = VEC.chain(lambda e: e.tensor_scalar(mtop[0:1, 0:1], mtop[0:1, 0:1], -1.0, None, ALU.mult))
                b.free = [mt]
                b = banks.take()
                for i in range(2):
                    for j in range(2):
                        t = transpose(b.ap[:, j * S + i * P:j * S + (i + 1) * P], attn[:, i, j * P:(j + 1) * P],
                                      ident, b.free, ar, tell=(i + j == 2))
                at = SCA.run(lambda e: e.activation(aT, b.ap.rearrange("p (j s) -> p j s", j=2), ACT.Copy), t, *end)
                b.free = [at]
                b = banks.take()
                t = mm(b.ap[:, 0:1], ones[0:1, :], mtop[0:1, 0:1], True, True, b.free, mt, tell=True)
                nb = VEC.run(lambda e: e.tensor_copy(q2c[:, 0:1], b.ap[:, 0:1]), t, *end)
                b.free = [nb]
                er = SCA.run(lambda e: e.activation(eb, mx[:, 2:4], ACT.Exp, bias=q2c[:, 0:1]), nb, *end)
                yield
                b = banks.take()
                for j in range(2):
                    t = mm(b.ap[:, 0:S], ctxt[:, 2 * bt + j, :], aT[:, j, :], j == 0, j == 1, b.free, at, ctx_in,
                           tell=(j == 1))
                c1 = SCA.run(lambda e: e.activation(c2q[:, 0, :], b.ap[:, 0:S], ACT.Copy), t, *end)
                c2 = VEC.run(lambda e: e.tensor_tensor(c2q[:, 1, :], c2q[:, 0, :], xnT[:, tok], ALU.mult), c1)
                b.free = [c1]
                b = banks.take()
                for i in range(2):
                    mm(b.ap[:, 0:1], xn[:, 2 * bt + i, :], eb[:, i:i + 1], i == 0, i == 1, b.free, er, xnr)
                for i in range(2):
                    t = mm(b.ap[:, 1:2], ones, eb[:, i:i + 1], i == 0, i == 1, tell=(i == 1))
                VEC.run(lambda e: e.reciprocal(rb[:, 0:1], b.ap[:, 1:2]), t)
                q2 = VEC.chain(lambda e: e.tensor_scalar(q2c[:, 1:2], b.ap[:, 0:1], rb[:, 0:1], None, ALU.mult))
                b.free = [q2]
                w14 = VEC.chain(lambda e: e.scalar_tensor_tensor(W14, Wl[:, 3, :], q2c[:, 1:2], Wl[:, 0, :],
                                                                 ALU.mult, ALU.add))
                yield "next"
                b = banks.take()
                for i in range(2):
                    o = b.ap[:, head_front(i)]
                    mm(o, ones[0:1, :], row[0:1, :], True, False, b.free, w14, c2)
                    mm(o, xnT[:, tile(i)], W14, False, False)
                    mm(o, c2q[:, 0, head_front(i)], Wl[:, 1, :], False, False)
                    t = mm(o, c2q[:, 1, head_front(i)], Wl[:, 2, :], False, True, tell=(i == 1))
                add_to_x(2 * bt, 2, b, t)
                z["end"] = [t, er, w14, c1]
                xn_read(2 * bt, 2)
                yield

            for bt in range(B):
                yield unit(bt)

        def moe_swiglu():
            E, F = 8, 512
            FB = F // P
            free_b = enter("B")
            cut = slab["B"].cut
            wg, wu, wd = cut([P, E * F]), cut([P, E * F]), cut([P, E * FB, D])
            wr = keep([P, P])
            win = load_group("moe1", [(wr, ins["r1_w"]), (wg, ins["e1_g"]), (wu, ins["e1_u"]),
                                      (wd.rearrange("p a d -> p (a d)"), ins["e1_d"])], *free_b)
            yield "loaded"
            free = enter("C")
            cut = slab["C"].cut
            coefs = [cut([P, GT, E]) for _ in range(2)]
            tmp = router_scratch(cut, E)
            sg = Ring([cut([P, GN]) for _ in range(4)])
            hs = Ring([cut([P, GN]) for _ in range(6)])
            for k in hs.buffers + sg.buffers:
                k.tickets = free
            def unit(g):
                coef = coefs[g % 2]
                _, xT = norm_x(g * GT, GT)
                yield
                c_ready, = router(g, E, wr, None, "first", [coef], tmp, win, xT, *free)
                yield
                acc = {}

                def up(blk):
                    bg, bu, s, h = banks.take(), banks.take(), sg.take(), hs.take()
                    c = slice(blk * P, (blk + 1) * P)
                    m1 = mm(bg.ap, wg[:, c], xnT[:, g * GN:(g + 1) * GN], True, True, bg.free, xT, win, tell=True)
                    m2 = mm(bu.ap, wu[:, c], xnT[:, g * GN:(g + 1) * GN], True, True, bu.free, tell=True)
                    a = SCA.run(lambda e: e.activation(s.ap, bg.ap, ACT.Silu), m1, s.free)
                    bg.free = [a]
                    done = VEC.run(lambda e: e.tensor_tensor(h.ap, bu.ap, s.ap, ALU.mult), m2, a, h.free)
                    bu.free = s.free = [done]
                    return h, done

                def down(blk, made):
                    h, done = made
                    ex, k = divmod(blk, FB)
                    if k == 0:
                        acc[0] = accs.take()
                    b = acc[0]
                    for t in range(GT):
                        m = mm(b.ap[:, head_front(t)], h.ap[:, head_front(t)], wd[:, blk, :], k == 0 and t == 0,
                               k == FB - 1, b.free, done, tell=(t == GT - 1))
                    h.free = [m]
                    if k == FB - 1 and ex == E - 1:
                        add_to_x(g * GT, GT, b, m)
                    elif k == FB - 1:
                        for t in range(GT):
                            n = g * GT + t
                            v = VEC.run(lambda e: e.scalar_tensor_tensor(
                                x[:, n, :], b.ap[:, head_front(t)], coef[:, t, ex:ex + 1], x[:, n, :], ALU.mult,
                                ALU.add), m, c_ready, x_ready[n])
                            x_ready[n] = [v]
                        b.free = [v]

                for n, y in enumerate(lagged(range(E * FB), up, down, 1, FB)):
                    yield "next" if n == E - 3 else None
                xn_read(g * GT, GT)

            for g in range(GROUPS):
                yield unit(g)

        def attention16():
            H, HD = 16, 8
            w, bcols, rows = keep([P, 3, P]), keep([P, 2]), keep([1, 2, P])
            wo = keep([P, P])
            head16 = keep([P, 16])
            free = enter("A", "E")
            cut = slab["A"].cut
            sel = slab["E"].cut([P, H, P], BF16)
            mki = cut([P, TILES], I32)
            mri = cut([P, TILES * P], I32)
            keepr = cut([P, TILES * P])
            win = load_group("att16", [(w, ins["l2_w"]), (bcols, ins["l2_cols"]), (rows, ins["l2_rows"]),
                                       (wo, ins["l2_wo"]), (head16, ins["c_retmask"][:, 0:16]),
                                       (sel.bitcast(mybir.dt.uint16), ins["c_sel16"]),
                                       (mki, ins["mask_cols"]), (mri, ins["mask_row"])], *free)
            yield "loaded"
            flag = cut([P, 2, B])
            negc = cut([P, TILES])
            negr = cut([P, TILES * P], BF16)
            VEC.run(lambda e: e.tensor_scalar(keepr, mri, 0.0, None, ALU.not_equal), win)
            VEC.chain(lambda e: e.reduce_max(flag[:, 0, :], keepr.rearrange("p (b s) -> p b s", b=B), AX.X))
            VEC.chain(lambda e: e.tensor_scalar(flag[:, 1, :], flag[:, 0, :], float(HD) ** -0.5, None, ALU.mult))
            VEC.run(lambda e: e.tensor_scalar(negc, mki, 0.0, NEG, ALU.is_equal, ALU.mult))
            VEC.chain(lambda e: e.tensor_tensor(
                negc.rearrange("p (b u) -> p b u", b=B), negc.rearrange("p (b u) -> p b u", b=B),
                flag[:, 0, :].unsqueeze(2).to_broadcast([P, B, 2]), ALU.mult))
            VEC.run(lambda e: e.tensor_scalar(keepr, keepr, -NEG, NEG, ALU.mult, ALU.add))
            mask_ready = VEC.chain(lambda e: e.tensor_tensor(
                negr.rearrange("p (b s) -> p b s", b=B), keepr.rearrange("p (b s) -> p b s", b=B),
                flag[:, 0, :].unsqueeze(2).to_broadcast([P, B, S]), ALU.mult))
            slab["A"].at = TILES
            qms = Ring([cut([P, 2, S]) for _ in range(4)])
            kms = Ring([cut([P, 2, S], BF16) for _ in range(4)])
            assert slab["A"].at <= TILES + 2 * TILES * P
            for k in qms.buffers + kms.buffers:
                k.tickets = [mask_ready]
            slab["A"].at = TILES + 2 * TILES * P + 2 * B + TILES + TILES * P // 2
            sets = [dict(QT=cut([P, S]), KT=cut([P, S]), QTb=cut([P, S], BF16), V=cut([P, 2, H, 32]),
                         nmx=cut([P, 2, P]), nmT=cut([P, S], BF16), end=[]) for _ in range(2)]
            ce = slab["E"].cut
            probs = Ring([(ce if k < 5 else cut)([P, 512]) for k in range(8)])
            OT = cut([P, 4, S])
            att, attT = cut([P, 2, P]), ce([P, 2 * P])
            rs = cut([P, 2, H])
            for z in sets:
                VEC.run(lambda e: e.memset(z["nmx"], 0.0))
                VEC.run(lambda e: e.memset(z["V"], 0.0))
                v1 = VEC.chain(lambda e: e.memset(z["V"][:, :, :, HD:HD + 1], 1.0))
            for k in probs.buffers:
                k.tickets = free
            o_free, att_free = [], []
            def unit(bt):
                nonlocal o_free, att_free
                z = sets[bt % 2]
                end = z["end"]
                QT, KT, QTb, V, nmx, nmT = (z[k] for k in ("QT", "KT", "QTb", "V", "nmx", "nmT"))
                _, xT = norm_x(2 * bt, 2)
                yield
                tok = slice(bt * S, (bt + 1) * S)
                b = banks.take()
                qm = mm(b.ap[:, 0:S], w[:, 0, :], xnT[:, tok], True, True, b.free, xT, win, tell=True)
                qr = VEC.run(lambda e: e.tensor_scalar(QT, b.ap[:, 0:S], bcols[:, 0:1], flag[:, 1, bt:bt + 1],
                                                       ALU.add, ALU.mult), qm, *end)
                b.free = [qr]
                b = banks.take()
                km = mm(b.ap[:, 0:S], w[:, 1, :], ctxT[:, tok], True, True, b.free, ctx_in, win, tell=True)
                kr = SCA.run(lambda e: e.activation(KT, b.ap[:, 0:S], ACT.Identity, bias=bcols[:, 1:2]), km, *end)
                b.free = [kr]
                qb = POOL.run(lambda e: e.tensor_copy(QTb, QT), qr, *end)
                b = banks.take()
                for i in range(2):
                    o = b.ap[:, head_front(i)]
                    mm(o, ones[0:1, :], rows[0:1, 0, :], True, False, b.free, win)
                    vm = mm(o, ctxT[:, bt * S + i * P:bt * S + (i + 1) * P], w[:, 2, :], False, True, tell=(i == 1))
                vr = SCA.run(lambda e: e.activation(
                    V[:, :, :, 0:HD], b.ap[:, 0:S].rearrange("p (u h e) -> p u h e", u=2, e=HD), ACT.Copy), vm,
                    v1, *end)
                b.free = [vr]
                yield
                for hp in range(H // 2):
                    k = kms.take()
                    for j in range(2):
                        kb = POOL.run(lambda e: e.tensor_scalar(
                            k.ap[:, j, :], KT, head16[:, 2 * hp + j:2 * hp + j + 1], None, ALU.mult), kr, k.free)
                    for i in range(2):
                        b = banks.take()
                        mm(b.ap, QTb[:, i * P:(i + 1) * P], k.ap, True, False, b.free, qb, kb)
                        m = mm(b.ap.rearrange("p (h s) -> p h s", h=2), row0,
                               negr[:, tok].unsqueeze(1).to_broadcast([P, 2, S]), False, True, mask_ready, tell=True)
                        mr = VEC.run(lambda e: e.tensor_reduce(
                            nmx[:, i, 2 * hp:2 * hp + 2], b.ap.rearrange("p (h s) -> p h s", h=2), AX.X, ALU.max,
                            negate=True), m, *end)
                        b.free = [mr]
                    k.free = [m]
                    if hp % 2:
                        yield
                b = banks.take()
                for i in range(2):
                    t = transpose(b.ap[:, head_front(i)], nmx[:, i, :], ident, b.free, mr, tell=(i == 1))
                nt = SCA.run(lambda e: e.activation(nmT, b.ap[:, 0:S], ACT.Copy), t, *end)
                b.free = [nt]
                yield "next"
                late = []

                def product(c, ps):
                    ob = accs.take()
                    for kt in range(2):
                        for j in range(4):
                            p, er = ps[j // 2][kt]
                            hh = j % 2
                            av = mm(ob.ap[32 * j:32 * j + 32, 0:S], V[:, kt, 4 * c + j, :],
                                    p.ap[:, hh * S:(hh + 1) * S], kt == 0, kt == 1, ob.free, er, vr, tell=(j == 3))
                    for pair in ps:
                        for p, _ in pair:
                            p.free = [av]
                    oc = SCA.run(lambda e: e.activation(OT[:, c, :], ob.ap[:, 0:S], ACT.Copy), av, *o_free)
                    ob.free = [oc]
                    return oc

                for hp in range(H // 2):
                    q = qms.take()
                    for j in range(2):
                        qmr = VEC.run(lambda e: e.tensor_scalar(
                            q.ap[:, j, :], QT, head16[:, 2 * hp + j:2 * hp + j + 1], None, ALU.mult), qr, q.free)
                    ps = []
                    for kt in range(2):
                        b = banks.take()
                        mm(b.ap, KT[:, kt * P:(kt + 1) * P], q.ap, True, False, b.free, kr, qmr)
                        for hh in range(2):
                            m = mm(b.ap[:, hh * S:(hh + 1) * S], sel[:, 2 * hp + hh, :], nmT, False, True, nt,
                                   tell=(hh == 1))
                        p = probs.take()
                        er = SCA.run(lambda e: e.activation(p.ap, b.ap, ACT.Exp,
                                                            bias=negc[:, 2 * bt + kt:2 * bt + kt + 1]), m, p.free,
                                     mask_ready)
                        b.free = [er]
                        ps.append((p, er))
                    q.free = [m]
                    if hp % 2 == 0:
                        late.append((hp // 2, [ps]))
                    else:
                        late[-1][1].append(ps)
                        yield
                    if hp % 2 == 0 and len(late) > 1:
                        product(*late.pop(0))
                oc = product(*late.pop(0))
                for i in range(2):
                    b = banks.take()
                    for c in range(4):
                        m = transpose(b.ap[:, head_front(c)], OT[:, c, i * P:(i + 1) * P], ident, b.free, oc,
                                      tell=(c == 3))
                    o = b.ap.rearrange("p (c j e) -> p (c j) e", c=4, e=32)
                    VEC.chain(lambda e: e.reciprocal(rs[:, i, :], o[:, :, HD]), m)
                    ar = VEC.chain(lambda e: e.tensor_tensor(
                        att[:, i, :].rearrange("p (h e) -> p h e", e=HD), o[:, :, 0:HD],
                        rs[:, i, :].unsqueeze(2).to_broadcast([P, H, HD]), ALU.mult), *att_free)
                    b.free = [ar]
                o_free = [m]
                tt = turn(att, attT, 2, ar, att_free)
                b = banks.take()
                t = project_tokens(b, 2, lambda k, _: attT[:, head_front(k)], [wo], rows[0:1, 1, :], tt)
                att_free = [t, tt]
                add_to_x(2 * bt, 2, b, t)
                z["end"] = [t, er, kb, qmr]
                xn_read(2 * bt, 2)
                yield

            for bt in range(B):
                yield unit(bt)

        def bitnet():
            F = 512
            FB = F // P
            UT, UN = 2, 2 * P
            wf = keep([P, 2, F])
            cv = keep([P, FB, 4])
            win = load_group("bit", [(wf, ins["b_w"]), (cv, ins["b_conv"])])
            yield "loaded"
            free = enter("C")
            cut = slab["C"].cut
            wq = cut([P, 2, F], BF16)
            asum, wmean, wsc = cut([P, 2]), cut([P, 2]), cut([P, 2])
            VEC.run(lambda e: e.tensor_reduce(asum, wf, AX.X, ALU.add, apply_absolute_value=True), win, *free)
            b = banks.take()
            t = mm(b.ap[:, 0:2], ones, asum, True, True, b.free, VEC.last(), tell=True)
            VEC.run(lambda e: e.tensor_scalar(wmean, b.ap[:, 0:2], 1.0 / (F * D), EPS, ALU.mult, ALU.max), t)
            b.free = [VEC.last()]
            VEC.chain(lambda e: e.reciprocal(wsc, wmean))
            VEC.wait(VEC.last())
            for k in range(2):
                VEC.run(lambda e: e.tensor_scalar(wf[:, k, :], wf[:, k, :], wsc[:, k:k + 1], ROUND, ALU.mult,
                                                  ALU.add))
            VEC.chain(lambda e: e.tensor_scalar(wf, wf, ROUND, 1.0, ALU.subtract, ALU.min))
            wr = VEC.chain(lambda e: e.tensor_scalar(wq, wf, -1.0, None, ALU.max))
            amax, qs, deq = cut([P, UT]), cut([P, UT]), cut([P, UT])
            sets = [dict(rnd=cut([P, UT, D]), xiT=cut([P, UN], BF16), dq=cut([P, UN]), hT=cut([P, UN]),
                         sT=cut([P, FB, UN]), end=list(free)) for _ in range(2)]
            diag = cut([P, UT, P])
            amax2, qs2, deq2 = cut([P, 2]), cut([P, 2]), cut([P, 2])
            hrs = Ring([cut([P, F])])
            his = Ring([cut([P, F], BF16) for _ in range(2)])
            hiTs = Ring([cut([P, F], BF16) for _ in range(2)])

            def scales(a, q, d, k, *after):
                VEC.chain(lambda e: e.tensor_scalar(a, a, EPS, None, ALU.max), *after)
                VEC.chain(lambda e: e.reciprocal(q, a))
                VEC.chain(lambda e: e.tensor_scalar(q, q, 127.0, None, ALU.mult))
                return VEC.chain(lambda e: e.tensor_scalar(d, a, 1.0 / 127.0, wmean[:, k:k + 1], ALU.mult, ALU.mult))

            diag_free = list(free)
            def unit(bt):
                nonlocal diag_free
                z = sets[bt % 2]
                end = z["end"]
                rnd, xiT, dq, hT, sT = (z[k] for k in ("rnd", "xiT", "dq", "hT", "sT"))
                xnr, xT = norm_x(UT * bt, UT)
                xg = xn[:, UT * bt:UT * (bt + 1), :]
                VEC.chain(lambda e: e.tensor_reduce(amax, xg, AX.X, ALU.max, apply_absolute_value=True), *end)
                scales(amax, qs, deq, 0)
                VEC.wait(VEC.last())
                VEC.wait(*diag_free)
                for t in range(UT):
                    VEC.run(lambda e: e.tensor_scalar(rnd[:, t, :], xg[:, t, :], qs[:, t:t + 1], ROUND, ALU.mult,
                                                      ALU.add))
                    VEC.run(lambda e: e.tensor_scalar(diag[:, t, :], ident, deq[:, t:t + 1], None, ALU.mult))
                xi = VEC.chain(lambda e: e.tensor_scalar(rnd, rnd, ROUND, None, ALU.subtract))
                yield
                xt = turn(rnd, xiT, UT, xi, end)
                b = banks.take()
                for t in range(UT):
                    m = mm(b.ap[:, t * P:(t + 1) * P], ones, diag[:, t, :], True, True, b.free, xi,
                           tell=(t == UT - 1))
                diag_free = [m]
                dr = SCA.run(lambda e: e.activation(dq, b.ap[:, 0:UN], ACT.Copy), m, *end)
                b.free = [dr]
                yield
                hr_done = list(end)
                for k in range(FB):
                    b = banks.take()
                    m = mm(b.ap[:, 0:UN], wq[:, 0, k * P:(k + 1) * P], xiT, True, True, b.free, xt, wr, tell=True)
                    h = VEC.run(lambda e: e.tensor_tensor(hT, b.ap[:, 0:UN], dq, ALU.mult), m, dr, *hr_done)
                    b.free = [h]
                    c = SCA.run(lambda e: e.activation(sT[:, k, :], hT, ACT.Identity, scale=cv[:, k, 1:2],
                                                       bias=cv[:, k, 3:4]), h, win, *end)
                    v = VEC.run(lambda e: e.scalar_tensor_tensor(
                        sT[:, k, 1:S], hT[:, 0:S - 1], cv[:, k, 0:1], sT[:, k, 1:S], ALU.mult, ALU.add), c)
                    v = VEC.chain(lambda e: e.scalar_tensor_tensor(
                        sT[:, k, 0:S - 1], hT[:, 1:S], cv[:, k, 2:3], sT[:, k, 0:S - 1], ALU.mult, ALU.add))
                    hr_done = [v]
                    sr = SCA.run(lambda e: e.activation(sT[:, k, :], sT[:, k, :], ACT.Silu), v)
                    yield
                yield "next"
                yb = accs.take()
                for t in range(UT):
                    b = banks.take()
                    for k in range(FB):
                        m = transpose(b.ap[:, k * P:(k + 1) * P], sT[:, k, t * P:(t + 1) * P], ident, b.free,
                                      sr, tell=(k == FB - 1))
                    a2, q2, d2 = amax2[:, t:t + 1], qs2[:, t:t + 1], deq2[:, t:t + 1]
                    VEC.chain(lambda e: e.tensor_reduce(a2, b.ap, AX.X, ALU.max, apply_absolute_value=True), m)
                    scales(a2, q2, d2, 1)
                    hr, hi, hiT = hrs.take(), his.take(), hiTs.take()
                    r = VEC.chain(lambda e: e.tensor_scalar(hr.ap, b.ap, q2, ROUND, ALU.mult, ALU.add), hr.free)
                    b.free = [r]
                    r = VEC.chain(lambda e: e.tensor_scalar(hi.ap, hr.ap, ROUND, None, ALU.subtract), hi.free)
                    hr.free = [r]
                    yield
                    b = banks.take()
                    bb = b.ap.bitcast(BF16)
                    for k in range(FB):
                        m = transpose(bb[:, k * P:(k + 1) * P], hi.ap[:, k * P:(k + 1) * P], identb, b.free, r,
                                      tell=(k == FB - 1))
                    hi.free = [m]
                    ht = SCA.run(lambda e: e.activation(hiT.ap, bb[:, 0:F], ACT.Copy), m, hiT.free)
                    b.free = [ht]
                    for k in range(FB):
                        m = mm(yb.ap[:, t * P:(t + 1) * P], hiT.ap[:, k * P:(k + 1) * P],
                               wq[:, 1, k * P:(k + 1) * P], k == 0, k == FB - 1, yb.free, ht, tell=(k == FB - 1))
                    hiT.free = [m]
                    n = bt * UT + t
                    xr = VEC.run(lambda e: e.scalar_tensor_tensor(
                        x[:, n, :], yb.ap[:, t * P:(t + 1) * P], d2, x[:, n, :], ALU.mult, ALU.add), m, x_ready[n],
                        VEC.last())
                    x_ready[n] = [xr]
                yb.free = [xr]
                z["end"] = [m, xr, ht]
                xn_read(bt * UT, UT)
                yield

            for bt in range(B):
                yield unit(bt)

        def split3(dst, src, tmp, *after):
            hi, mid, lo = dst
            a, c = tmp
            VEC.chain(lambda e: e.tensor_copy(a, src), *after)
            VEC.chain(lambda e: e.tensor_copy(hi, a))
            VEC.chain(lambda e: e.tensor_tensor(c, src, a, ALU.subtract))
            VEC.chain(lambda e: e.tensor_copy(a, c))
            VEC.chain(lambda e: e.tensor_copy(mid, a))
            VEC.chain(lambda e: e.tensor_tensor(c, c, a, ALU.subtract))
            VEC.chain(lambda e: e.tensor_copy(a, c))
            return VEC.chain(lambda e: e.tensor_copy(lo, a))

        def attention8():
            H, HD, M = 8, 64, 2 * S
            KT4 = M // P
            HB = H * HD // P
            free = enter("B", "E", "C")
            cut, ce, cc = slab["B"].cut, slab["E"].cut, slab["C"].cut
            W = cut([P, 2048])
            Wq, Wkv = W[:, 0:512], W[:, 512:1536]
            Wo = W[:, 1536:2048].rearrange("p (k d) -> p k d", k=HB)
            colw, lno = keep([P, 6]), keep([P, 2, D])
            par2 = keep([P, 2])
            selb = keep([P, 512], BF16)
            selm = keep([P, H, P], BF16)
            blk8 = ce([P, P + 8])
            mki = keep([P, TILES], U8)
            sets = [dict(K=c1([P, HB, M]), Q=c2([P, HB, 2, S]), V=c3([P, KT4, H * (HD + 1) + HD]), end=[])
                    for c1, c2, c3 in ((cut, cut, cut), (cut, cc, cc))]
            mri = sets[1]["Q"].rearrange("p a b c -> p (a b c)")[:, 0:TILES * P // 4].bitcast(U8)
            win = load_group("att8", [(W, ins["l3_w"]), (colw, ins["l3_cols"]), (lno, ins["l3_lno"]),
                                      (par2, ins["c_par2"]), (selb.bitcast(mybir.dt.uint16), ins["c_sel24"]),
                                      (selm.bitcast(mybir.dt.uint16), ins["c_sel16"][:, 0:H, :]),
                                      (blk8, ins["c_blk8"]), (mki, ins["bmask_cols"]), (mri, ins["bmask_row"])],
                             *free)
            yield "loaded"
            negc = ce([P, TILES])
            negr = cut([P, TILES * P], BF16)
            VEC.run(lambda e: e.tensor_scalar(negc, mki, 0.0, -1e30, ALU.is_equal, ALU.mult), win)
            nr = VEC.run(lambda e: e.tensor_scalar(negr, mri, 0.0, -1e30, ALU.is_equal, ALU.mult), win)
            sets[1]["end"] = [nr]
            qk2 = ce([P, 2])
            VEC.run(lambda e: e.tensor_scalar(qk2, par2, colw[:, 4:5], colw[:, 5:6], ALU.mult, ALU.mult))
            c_ready = VEC.chain(lambda e: e.tensor_scalar(qk2, qk2, 8.0, None, ALU.mult))
            lnt = ce([P, 2, D])
            kvT = ce([P, M])
            sqs = Ring([ce([P, M])])
            qraw = ce([P, HB, S])
            parts = ce([P, 6, 24])
            tA, tB = ce([P, 48], BF16), ce([P, 48])
            rT = cc([24, 6 * P], BF16)
            nmx, nmT = cut([P, 2, P]), ce([P, S], BF16)
            probs = Ring([cc([P, KT4, S]) for _ in range(2)])
            rs = ce([P, 4])
            att, attT, yln = cc([P, H * HD]), ce([P, HB, P]), ce([P, 1, D])
            VEC.run(lambda e: e.memset(nmx, 0.0))
            for z in sets:
                VEC.wait(*z["end"])
                v1 = VEC.run(lambda e: e.memset(z["V"], 1.0))
            upper = lambda a, n: a.bitcast(BF16).rearrange("p (n two) -> p n two", two=2)[:, :, 1]
            kv_free, lnt_free, q_free, nm_free, att_free, r_free = [], [], [], [], [], []

            def unit(bt):
                nonlocal kv_free, lnt_free, q_free, nm_free, att_free, r_free
                z = sets[bt % 2]
                K, Q, V, end = z["K"], z["Q"], z["V"], z["end"]
                Vh = V[:, :, 0:H * (HD + 1)].rearrange("p k (h e) -> p k h e", e=HD + 1)
                norm_x(2 * bt, 2)
                a = normalise(ctxt[:, 2 * bt:2 * bt + 2, :], lnt, 2, ctx_in, *lnt_free)
                t1 = turn(lnt, kvT[:, 0:S], 2, a, [win] + kv_free, colw[:, 0:1], colw[:, 1:2])
                yield
                a = normalise(xn[:, 2 * bt:2 * bt + 2, :], lnt, 2, VEC.last(), t1)
                t2 = turn(lnt, kvT[:, S:M], 2, a, [win] + kv_free, colw[:, 2:3], colw[:, 3:4])
                lnt_free = [t2]
                yield
                nb, nb2 = banks.take(), banks.take()
                for k in range(HB):
                    for side in range(2):
                        n = M if side == 0 else S
                        src = kvT if side == 0 else kvT[:, S:M]
                        wgt = Wkv[:, k * P:(k + 1) * P] if side == 0 else Wq[:, k * P:(k + 1) * P]
                        dst = K[:, k, :] if side == 0 else qraw[:, k, :]
                        b, sq = banks.take(), sqs.take()
                        m = mm(b.ap[:, 0:n], wgt, src, True, True, b.free, t1, t2, win, tell=True)
                        s2 = SCA.run(lambda e: e.activation(sq.ap[:, 0:n], b.ap[:, 0:n], ACT.Square), m, sq.free)
                        rw = VEC.run(lambda e: e.tensor_copy(dst, b.ap[:, 0:n]), m, s2, *(end if side == 0 else q_free))
                        b.free = [s2, rw]
                        for i in range(n // P):
                            to = (nb if side == 0 else nb2)
                            m = mm(to.ap[:, i * P:(i + 1) * P], sq.ap[:, i * P:(i + 1) * P],
                                   blk8[:, 8 - 2 * k:8 - 2 * k + P], k == 0 and i == 0, k == HB - 1, to.free, s2,
                                   tell=(i == n // P - 1))
                        sq.free = [m]
                    yield
                VEC.chain(lambda e: e.tensor_scalar(
                    rsq_v[:, 0:32].rearrange("p (t h) -> p t h", t=4),
                    nb.ap.rearrange("p (t h) -> p t h", t=4)[:, :, 0:8], 1e-24, None, ALU.max), m)
                VEC.run(lambda e: e.tensor_scalar(
                    rsq_v[:, 32:48].rearrange("p (t h) -> p t h", t=2),
                    nb2.ap[:, 0:2 * P].rearrange("p (t h) -> p t h", t=2)[:, :, 0:8], 1e-24, None, ALU.max))
                nb.free = [VEC.last()]
                nb2.free = [VEC.last()]
                rsqrt(48)
                pv = lambda j: parts[:, :, 8 * j:8 * j + 8]
                as6 = lambda z: z.rearrange("p (t h) -> p t h", t=6)
                pr = split3((pv(0), pv(1), pv(2)), as6(rsq_y[:, 0:48]), (as6(tA), as6(tB)), *r_free)
                for i in range(KT4):
                    b = banks.take()
                    m = mm(b.ap, kvT[:, i * P:(i + 1) * P], Wkv[:, 512:1024], True, True, b.free, t1, t2, tell=True)
                    vr = SCA.run(lambda e: e.activation(
                        Vh[:, i, :, 0:HD], b.ap.rearrange("p (h e) -> p h e", e=HD), ACT.Copy), m, v1, *end)
                    b.free = [vr]
                kv_free = [m]
                yield
                b, b2 = banks.take(), banks.take()
                for i in range(6):
                    dst = (b if i < 4 else b2).ap[0:24, (i % 4) * P:(i % 4 + 1) * P]
                    m = transpose(dst, parts[:, i, :], ident, b.free, b2.free, pr, tell=(i == 5))
                SCA.run(lambda e: e.activation(rT[:, 0:512], b.ap[0:24, :], ACT.Copy), m, *r_free)
                rt = SCA.run(lambda e: e.activation(rT[:, 512:768], b2.ap[0:24, 0:256], ACT.Copy))
                b.free = [rt]
                b2.free = [rt]
                yield
                for k in range(HB):
                    b = banks.take()
                    m = mm(b.ap, selb[0:24, k * P:(k + 1) * P], rT[:, 0:M], True, True, b.free, rt, c_ready, tell=True)
                    kr = VEC.run(lambda e: e.tensor_tensor(K[:, k, :], b.ap, K[:, k, :], ALU.mult), m, rw)
                    b.free = [kr]
                    b = banks.take()
                    m = mm(b.ap[:, 0:S], selb[0:24, k * P:(k + 1) * P], rT[:, M:M + S], True, True, b.free, rt,
                           tell=True)
                    for j in range(2):
                        qr = VEC.run(lambda e: e.scalar_tensor_tensor(
                            Q[:, k, j, :], b.ap[:, 0:S], qk2[:, j:j + 1], qraw[:, k, :], ALU.mult, ALU.mult), m, rw,
                            *end)
                    b.free = [qr]
                r_free, q_free = [m], [qr]
                yield
                for h in range(H):
                    for i in range(2):
                        b = banks.take()
                        mm(b.ap, upper(Q[:, h // 2, h % 2, i * P:(i + 1) * P], P), upper(K[:, h // 2, :], M),
                           True, False, b.free, kr, qr)
                        m = mm(b.ap[:, 0:S], row0, negr[:, bt * S:(bt + 1) * S], False, True, nr, tell=True)
                        mr = VEC.run(lambda e: e.tensor_reduce(nmx[:, i, h:h + 1], b.ap, AX.X,
                                                               ALU.max, negate=True), m, *nm_free)
                        b.free = [mr]
                    if h % 2:
                        yield
                b = banks.take()
                for i in range(2):
                    t = transpose(b.ap[:, i * P:(i + 1) * P], nmx[:, i, :], ident, b.free, mr, tell=(i == 1))
                yield "next"
                nt = SCA.run(lambda e: e.activation(nmT, b.ap[:, 0:S], ACT.Copy), t, *nm_free)
                b.free = [nt]
                nm_free = [t]
                obs = [[accs.take(), banks.take()]]
                late = []

                def product(h, p, er):
                    for i in range(2):
                        o = obs[-1][i]
                        for kt in range(KT4):
                            av = mm(o.ap[:, (h % 4) * P:(h % 4 + 1) * P], p.ap[:, kt, i * P:(i + 1) * P],
                                    V[:, kt, h * (HD + 1):h * (HD + 1) + P], kt == 0, kt == KT4 - 1,
                                    o.free, er, vr, tell=(kt == KT4 - 1))
                    p.free = [av]
                    if h == 3:
                        obs.append([accs.take(), banks.take()])
                    return av

                for h in range(H):
                    p = probs.take()
                    for half in range(2):
                        b = banks.take()
                        for j in range(2):
                            kt = 2 * half + j
                            o = b.ap[:, j * S:(j + 1) * S]
                            mm(o, K[:, h // 2, kt * P:(kt + 1) * P], Q[:, h // 2, h % 2, :], True, False,
                               b.free, kr, qr)
                            m = mm(o, selm[:, h, :], nmT, False, True, nt, tell=(j == 1))
                        if half == 0:
                            for j in range(2):
                                er = SCA.run(lambda e: e.activation(
                                    p.ap[:, j, :], b.ap[:, j * S:(j + 1) * S], ACT.Exp,
                                    bias=negc[:, 2 * bt + j:2 * bt + j + 1]), m, p.free, c_ready)
                        else:
                            er = SCA.run(lambda e: e.activation(
                                p.ap[:, 2:4, :], b.ap.rearrange("p (j s) -> p j s", j=2), ACT.Exp), m, p.free)
                        b.free = [er]
                    late.append((h, p, er))
                    if len(late) > 1:
                        av = product(*late.pop(0))
                    if h % 2:
                        yield
                av = product(*late.pop(0))
                nm_free = nm_free + [m]
                for i in range(2):
                    n = 2 * bt + i
                    for hq in range(2):
                        ob = obs[hq][i]
                        o = ob.ap.rearrange("p (h e) -> p h e", e=P)
                        VEC.chain(lambda e: e.reciprocal(rs, o[:, :, HD]), av)
                        ar = VEC.chain(lambda e: e.tensor_tensor(
                            att[:, hq * 256:(hq + 1) * 256].rearrange("p (h e) -> p h e", e=HD), o[:, :, 0:HD],
                            rs.unsqueeze(2).to_broadcast([P, 4, HD]), ALU.mult), *att_free)
                        ob.free = [ar]
                    tt = turn(att.rearrange("p (k d) -> p k d", k=HB), attT.rearrange("p k d -> p (k d)"), HB, ar,
                              [PE.last()])
                    b = banks.take()
                    for k in range(HB):
                        m = mm(b.ap[:, 0:P], attT[:, k, :], Wo[:, k, :], k == 0, k == HB - 1, b.free, tt,
                               tell=(k == HB - 1))
                    att_free = [m, tt]
                    y = normalise(b.ap[:, 0:P].unsqueeze(1), yln, 1, m)
                    b.free = [y]
                    VEC.chain(lambda e: e.tensor_tensor(yln[:, 0, :], yln[:, 0, :], lno[:, 0, :], ALU.mult))
                    VEC.chain(lambda e: e.tensor_tensor(yln[:, 0, :], yln[:, 0, :], lno[:, 1, :], ALU.add))
                    x_ready[n] = [VEC.chain(lambda e: e.tensor_tensor(x[:, n, :], x[:, n, :], yln[:, 0, :], ALU.add),
                                            x_ready[n])]
                z["end"] = [PE.last(), VEC.last(), er]
                xn_read(2 * bt, 2)
                yield

            for bt in range(B):
                yield unit(bt)

        def moe_small():
            E, PAIRS = 32, 32
            free_a = enter("A")
            cut = slab["A"].cut
            wg, wu, wd = cut([P, 4096]), cut([P, 4096]), cut([P, PAIRS, D])
            wr = keep([P, P])
            selb = keep([P, 16, P], BF16)
            win = load_group("moe3", [(wr, ins["r3_w"]), (selb.rearrange("p a b -> p (a b)").bitcast(
                mybir.dt.uint16), ins["c_sel96"]), (wg, ins["e3_g"]), (wu, ins["e3_u"]),
                (wd.rearrange("p a d -> p (a d)"), ins["e3_d"])], *free_a)
            yield "loaded"
            free = enter("C")
            cut = slab["C"].cut
            coef = [cut([P, GT, E]) for _ in range(2)]
            tmp = router_scratch(cut, E)
            parts = cut([P, GT, 3 * E])
            tA, tB = cut([P, GT, E], BF16), cut([P, GT, E])
            cTs = [[cut([3 * E, GN], BF16) for r in range(2)] for _ in range(2)]
            sg = Ring([cut([P, GN]) for _ in range(3)])
            hs = Ring([cut([P, GN]) for _ in range(4)])
            for k in hs.buffers + sg.buffers:
                k.tickets = free
            ct_free = [list(free), list(free)]
            VEC.wait(*free)

            def unit(g):
                cT = cTs[g % 2]
                _, xT = norm_x(g * GT, GT)
                yield
                cr = router(g, E, wr, None, "half", coef, tmp, win, xT)
                yield
                cts = []
                for r in range(2):
                    pr = split3(tuple(parts[:, :, j * E:(j + 1) * E] for j in range(3)), coef[r], (tA, tB), cr[r],
                                PE.last())
                    b = banks.take()
                    for t in range(GT):
                        m = transpose(b.ap[0:3 * E, t * P:(t + 1) * P], parts[:, t, :], ident, b.free, pr,
                                      tell=(t == GT - 1))
                    ct = SCA.run(lambda e: e.activation(cT[r], b.ap[0:3 * E, :], ACT.Copy), m, *ct_free[g % 2])
                    b.free = [ct]
                    cts.append(ct)
                    yield
                acc = {}

                def up(p):
                    if p == 0:
                        acc[0] = accs.take()
                    r = p // 16
                    bg, bu, bc = banks.take(), banks.take(), banks.take()
                    m1 = mm(bg.ap, wg[:, p * P:(p + 1) * P], xnT[:, g * GN:(g + 1) * GN], True, True, bg.free, xT,
                            win, tell=True)
                    m2 = mm(bu.ap, wu[:, p * P:(p + 1) * P], xnT[:, g * GN:(g + 1) * GN], True, True, bu.free,
                            tell=True)
                    m3 = mm(bc.ap, selb[0:3 * E, p % 16, :], cT[r], True, True, bc.free, cts[r], tell=True)
                    s, h = sg.take(), hs.take()
                    a = SCA.run(lambda e: e.activation(s.ap, bg.ap, ACT.Silu), m1, s.free)
                    bg.free = [a]
                    v = VEC.run(lambda e: e.tensor_tensor(s.ap, bu.ap, s.ap, ALU.mult), m2, a)
                    bu.free = [v]
                    hd = VEC.run(lambda e: e.tensor_tensor(h.ap, bc.ap, s.ap, ALU.mult), m3, v, h.free)
                    bc.free = [hd]
                    s.free = [hd]
                    return h, hd

                def down(p, made):
                    h, hd = made
                    b = acc[0]
                    for t in range(GT):
                        m = mm(b.ap[:, head_front(t)], h.ap[:, head_front(t)], wd[:, p, :], p == 0 and t == 0,
                               p == PAIRS - 1, b.free, hd, tell=(t == GT - 1))
                    h.free = [m]
                    if p == PAIRS - 1:
                        add_to_x(g * GT, GT, b, m)

                for n, y in enumerate(lagged(range(PAIRS), up, down, 1, 4)):
                    yield "next" if n == 5 else None
                ct_free[g % 2] = [PE.last()]
                xn_read(g * GT, GT)

            for g in range(GROUPS):
                yield unit(g)

        stages = {"L0x": (retention, "BEC"), "L0f": (moe_gelu, "AC"), "L1x": (bidaf, "E"),
                  "L1f": (moe_swiglu, "BC"), "L2x": (attention16, "AE"), "L2f": (bitnet, "C"),
                  "L3x": (attention8, "BEC"), "L3f": (moe_small, "AC")}

        def run_all(order):
            gens = [stages[name][0]() for name in order]
            uses = [set(stages[name][1]) for name in order]
            state = dict(layer=0, started=0, asked=-1)
            open_units = {n: 0 for n in range(len(order))}
            exhausted = [False] * len(order)
            left = [False] * len(order)
            active = []

            def ask(n):
                if n < len(order) and n > state["asked"]:
                    assert next(gens[n]) == "loaded"
                    state["asked"] = n

            def start():
                n = state["layer"]
                if n == len(order):
                    return False
                if any(uses[n] & uses[k] and not left[k] for k in range(n)):
                    return False
                ask(n)
                u = next(gens[n], None)
                if u is None:
                    exhausted[n] = True
                    settle(n)
                    state["layer"], state["started"] = n + 1, 0
                    return start()
                state["started"] += 1
                open_units[n] += 1
                active.append([u, n, False])
                if state["started"] == 2 and n + 1 < len(order) and not any(
                        uses[n + 1] & uses[k] and not left[k] for k in range(n)):
                    if order[n + 1] != "L3x":
                        ask(n + 1)
                return True

            def settle(n):
                if exhausted[n] and open_units[n] == 0 and not left[n]:
                    leave(*stages[order[n]][1])
                    left[n] = True

            start()
            while active:
                for entry in list(active):
                    if entry[2] and entry is not active[0]:
                        continue
                    v = next(entry[0], "end")
                    if v == "end":
                        active.remove(entry)
                        open_units[entry[1]] -= 1
                        settle(entry[1])
                    elif v == "next":
                        entry[2] = True
                    if len(active) < 2 and (not active or active[0][2]):
                        start()

        run_all(LAYERS)
        stored = sem("stored")
        SYNC.wait(*[t for k in range(TILES) for t in x_ready[k]])
        SYNC.eng.dma_start(out.rearrange("b (u p) d -> p (b u) d", p=P), x).then_inc(stored, 16)
        SYNC.eng.wait_ge(stored, 16)


def constants():
    c = {}
    c["c_ident"] = np.eye(P, dtype=np.float32)
    H, HD = 16, 8
    half = HD // 2
    pair = np.repeat(np.arange(half), 2)
    base = (np.arange(0, HD, 2) + 0.4 * HD) / (1.4 * HD)
    power = (np.arange(-(S // 2), S // 2)) / 512.0
    scale = base[None, :] ** power[:, None]
    ang = (np.arange(S, dtype=np.float32)[:, None]
           * (1.0 / 10000.0 ** (np.arange(half, dtype=np.float32) / half)).astype(np.float32)[None, :]).astype(np.float64)
    gam = (1.0 - np.exp(np.linspace(np.log(1 / 32.0), np.log(1 / 512.0), H)).astype(np.float32)).astype(np.float64)
    mid = np.arange(S) - S // 2
    sign = np.where(np.arange(HD) % 2 == 0, -1.0, 1.0)
    tab = np.zeros((P, 4, S))
    for h in range(H):
        for e in range(HD):
            p = h * HD + e
            for side, (sc, dec) in enumerate(((scale[:, pair[e]], gam[h] ** mid), (1 / scale[:, pair[e]], gam[h] ** -mid))):
                tab[p, 2 * side] = np.cos(ang[:, pair[e]]) * sc * dec
                tab[p, 2 * side + 1] = np.sin(ang[:, pair[e]]) * sc * dec * sign[e]
    c["c_xpos"] = tab.astype(np.float32)
    m = np.zeros((P, 16 + P + 512), np.float32)
    p = np.arange(P)
    m[:, 0:16] = p[:, None] // HD == np.arange(16)[None, :]
    m[:, 16:16 + P] = p[:, None] // HD == p[None, :] // HD
    m[:, 16 + P:] = np.tile(p[None, :] >= p[:, None], (1, 4))
    c["c_retmask"] = m
    one = np.uint16(0x3F80)
    c["c_sel16"] = (p[:, None, None] == np.arange(16)[None, :, None]) * np.full((1, 1, P), one)
    c["c_sel24"] = ((p[:, None] % 8 == np.arange(512)[None, :] // 64) & (p[:, None] < 24)) * one
    c["c_par2"] = (p[:, None] // 64 == np.arange(2)[None, :]).astype(np.float32)
    c["c_blk8"] = (p[:, None] // 64 + 8 == np.arange(P + 8)[None, :]).astype(np.float32)
    c["c_sel96"] = ((p[:, None] % 32 == np.arange(2048)[None, :] // 64) & (p[:, None] < 96)) * one
    return c


def layout(i):
    n = {k: np.asarray(v) for k, v in i.items()}
    f = dict(constants())
    f["x"], f["ctx_1024"] = n["x"], n["ctx_1024"]
    f["ctxT"] = n["ctx_1024"].reshape(B * S, D).T
    heads = lambda w: w.transpose(1, 0, 2).reshape(D, D)
    swap = np.arange(D) ^ 1
    wq, wk, wv = (heads(n["L0_xattn_W_" + c]) for c in "QKV")
    f["w_ret"] = np.stack([wq, wq[:, swap], wk, wk[:, swap], wv, n["L0_xattn_g_w"].T, n["L0_xattn_out_w"].T], axis=1)
    f["rows_ret"] = np.stack([n["L0_xattn_g_b"], n["L0_xattn_out_b"]])[None]
    wide = lambda w: np.concatenate([w, np.zeros((w.shape[0], P - w.shape[1]), w.dtype)], axis=1)
    f["r0_w"], f["r0_b"] = wide(n["L0_ffn_router_w"].T), wide(n["L0_ffn_router_b"][None])
    f["e0_w1"] = n["L0_ffn_w1"].transpose(2, 0, 1).reshape(D, -1)
    f["e0_b1"] = n["L0_ffn_b1"].reshape(8, 4, P).transpose(2, 0, 1).reshape(P, 32)
    f["e0_w2"] = n["L0_ffn_w2"].reshape(8, D, 4, P).transpose(3, 0, 2, 1).reshape(P, -1)
    f["e0_b2"] = n["L0_ffn_b2"]
    f["l1_W"] = n["L1_xattn_W_l"].reshape(D, 4, D).transpose(2, 1, 0)
    f["l1_cols"] = np.stack([n["L1_xattn_w_cq"], n["L1_xattn_w_q"], n["L1_xattn_w_c"]], axis=1)
    f["l1_bias"] = np.broadcast_to(np.stack([n["L1_xattn_b_c"], n["L1_xattn_b_q"], n["L1_xattn_b_cq"]])[None], (P, 3))
    f["l1_row"] = n["L1_xattn_b_l"][None]
    f["r1_w"] = wide(n["L1_ffn_Wr"])
    for a, b in (("g", "Wg"), ("u", "Wu")):
        f["e1_" + a] = np.concatenate([n["L1_ffn_" + b], n["L1_ffn_" + b + "_s"][None]]).transpose(1, 0, 2).reshape(D, -1)
    wd = np.concatenate([n["L1_ffn_Wd"], n["L1_ffn_Wd_s"][None]])
    f["e1_d"] = wd.reshape(8, 4, P, D).transpose(2, 0, 1, 3).reshape(P, -1)
    f["l2_w"] = np.stack([n["L2_xattn_W" + c].T for c in "qkv"], axis=1)
    f["l2_wo"] = n["L2_xattn_Wo"].T
    f["l2_cols"] = np.stack([n["L2_xattn_bq"], n["L2_xattn_bk"]], axis=1)
    f["l2_rows"] = np.stack([n["L2_xattn_bv"], n["L2_xattn_bo"]])[None]
    f["mask_row"] = np.broadcast_to(n["mask_BxS2_ik0"].reshape(1, -1), (P, B * S))
    f["mask_cols"] = n["mask_BxS2_ik0"].reshape(TILES, P).T
    f["b_w"] = np.stack([n["L2_ffn_w1"].T, n["L2_ffn_w2"].reshape(D, 4, P).transpose(2, 1, 0).reshape(P, -1)], axis=1)
    f["b_conv"] = np.concatenate([n["L2_ffn_conv_w"].reshape(4, P, 3), n["L2_ffn_conv_b"].reshape(4, P, 1)],
                                 axis=2).transpose(1, 0, 2)
    f["l3_w"] = np.concatenate([n["L3_xattn_Wq"], n["L3_xattn_Wkv"],
                                n["L3_xattn_Wo"].reshape(4, P, D).transpose(1, 0, 2).reshape(P, -1)], axis=1)
    two = lambda v: np.tile(v, 2)
    f["l3_cols"] = np.stack([n["L3_xattn_ln_x_w"], n["L3_xattn_ln_x_b"], n["L3_xattn_ln_l_w"], n["L3_xattn_ln_l_b"],
                             two(n["L3_xattn_q_scale"]), two(n["L3_xattn_k_scale"])], axis=1)
    f["l3_lno"] = np.broadcast_to(np.stack([n["L3_xattn_ln_o_w"], n["L3_xattn_ln_o_b"]])[None], (P, 2, D))
    keep = n["mask_BxS2_bk0"]
    f["bmask_row"], f["bmask_cols"] = np.broadcast_to(keep.reshape(1, -1), (P, B * S)), keep.reshape(TILES, P).T
    f["r3_w"] = wide(np.concatenate([n["L3_ffn_router_w0"], n["L3_ffn_router_w1"]], axis=1))
    for a, b in (("g", "wg"), ("u", "wu")):
        f["e3_" + a] = np.concatenate([n[f"L3_ffn_{b}{r}"] for r in range(2)]).transpose(1, 0, 2).reshape(D, -1)
    f["e3_d"] = np.concatenate([n[f"L3_ffn_wd{r}"] for r in range(2)]).reshape(32, P, D).transpose(1, 0, 2).reshape(P, -1)
    return {k: np.ascontiguousarray(v) for k, v in f.items()}


def kernel(**inputs):
    import concourse.bacc as bacc
    from concourse.bass_utils import run_bass_kernel_spmd

    arrays = layout(inputs)
    nc = bacc.Bacc("TRN2", target_bir_lowering=False, num_devices=1)
    aps = {k: nc.dram_tensor(k + "_dram", a.shape, mybir.dt.from_np(a.dtype), kind="ExternalInput").ap()
           for k, a in arrays.items()}
    out = nc.dram_tensor("out_dram", (B, S, D), F32, kind="ExternalOutput").ap()
    build(nc, aps, out)
    r = run_bass_kernel_spmd(nc, [{k + "_dram": a for k, a in arrays.items()}], core_ids=[0])
    return r.results[0]["out_dram"]
```

```python
from contextlib import ExitStack

import numpy as np
import concourse.bass as bass
from concourse import mybir

F32, BF16, I32, U8 = mybir.dt.float32, mybir.dt.bfloat16, mybir.dt.int32, mybir.dt.uint8
R32 = mybir.dt.float32r
ALU = mybir.AluOpType
ACT = mybir.ActivationFunctionType
AX = mybir.AxisListType

P = 128
B, S, D = 8, 256, 128
TILES = B * S // P
GROUPS = 4
GT = TILES // GROUPS
GN = GT * P
EPS = 1e-5
ROUND = 1.5 * 2.0 ** 23
NEG = -1e9
LAYERS = ("L0x", "L0f", "L1x", "L1f", "L2x", "L2f", "L3x", "L3f")


class Queue:

    def __init__(self, eng, sem):
        self.eng, self.sem, self.done, self.waited = eng, sem, 0, {}

    def wait(self, *tickets):
        for t in tickets:
            if t is None:
                continue
            if isinstance(t, list):
                self.wait(*t)
                continue
            sem, count = t
            if self.waited.get(sem.name, 0) < count:
                self.waited[sem.name] = count
                self.eng.wait_ge(sem, count)

    def run(self, issue, *after):
        self.wait(*after)
        self.done += 1
        issue(self.eng).then_inc(self.sem, 1)
        return (self.sem, self.done)

    def chain(self, issue, *after):
        return self.run(issue, self.last(), *after)

    def quiet(self, issue, *after):
        self.wait(*after)
        issue(self.eng)

    def last(self):
        return (self.sem, self.done) if self.done else None


class Buffer:

    def __init__(self, ap):
        self.ap, self.held, self.tickets = ap, False, []

    @property
    def free(self):
        return self.tickets

    @free.setter
    def free(self, tickets):
        self.tickets, self.held = tickets, False


class Ring:
    def __init__(self, aps):
        self.buffers, self.at = [Buffer(a) for a in aps], 0

    def take(self):
        for _ in self.buffers:
            b = self.buffers[self.at % len(self.buffers)]
            self.at += 1
            if not b.held:
                b.held = True
                return b
        raise AssertionError("every buffer of the ring is held")


class Arena:

    def __init__(self, ap, words, split_view):
        self.slab, self.split_view, self.words, self.at, self.users = ap, split_view, words, 0, []

    def enter(self):
        self.at = 0
        return self.users

    def cut(self, shape, dt=F32):
        n = int(np.prod(shape[1:]))
        words = n if dt in (F32, I32, R32) else (n + 1) // 2 if dt == BF16 else (n + 3) // 4
        words += words % 2
        v = (self.split_view if dt == R32 else self.slab)[0:shape[0], self.at:self.at + words]
        self.at += words
        assert self.at <= self.words, (self.at, self.words)
        if dt not in (F32, R32):
            v = v.bitcast(dt)
        v = v[:, 0:n]
        if len(shape) == 3:
            v = v.rearrange("p (a b) -> p a b", a=shape[1])
        if len(shape) == 4:
            v = v.rearrange("p (a b c) -> p a b c", a=shape[1], b=shape[2])
        return v


def build(nc, ins, out):
    ctx = ExitStack()
    with ctx:
        def sem(name):
            return ctx.enter_context(nc.semaphore(name))

        PE, VEC, SCA, POOL = (Queue(eng, sem(n)) for eng, n in (
            (nc.tensor, "pe_done"), (nc.vector, "vec_done"), (nc.scalar, "sca_done"), (nc.gpsimd, "pool_done")))
        SYNC = Queue(nc.sync, None)

        def sb(name, shape, dt=F32):
            t = ctx.enter_context(nc.sbuf_tensor(name, shape, dt))
            return t[tuple(slice(None) for _ in shape)]

        def load_group(name, pairs, *after):
            s = sem("in_" + name)
            SYNC.wait(*after)
            for dst, src in pairs:
                SYNC.eng.dma_start(dst, src).then_inc(s, 16)
            return (s, 16 * len(pairs))

        x = sb("x", [P, TILES, D])
        xn = sb("xn", [P, TILES, D])
        xnT = sb("xnT", [P, TILES * P])
        ctxt = sb("ctxt", [P, TILES, D])
        ctxT = sb("ctxT", [P, TILES * P])
        ident = sb("ident", [P, P])
        identb = sb("identb", [P, P], BF16)
        ones = sb("ones", [P, P])
        stats = sb("stats", [P, GT, 6])
        meanvar = sb("meanvar", [P, GT, 2])
        rsq_v = sb("rsq_v", [P, 64])
        rsq_i = sb("rsq_i", [P, 64], I32)
        rsq_y = sb("rsq_y", [P, 64])
        rsq_t = sb("rsq_t", [P, 64])
        psum = [ctx.enter_context(nc.psum_tensor(f"bank{i}", [P, 512], F32)) for i in range(8)]
        banks = Ring([b[:, :] for b in psum])

        SIZES = {"A": 12288, "B": 12288, "C": 4384, "D": 3072, "E": 3880, "G": 4072, "W": 2328}
        slab = {}
        for k, n in SIZES.items():
            with nc.sbuf_tensor("split" + k, [P, n], R32) as t:
                split_view = t[:, :]
            slab[k] = Arena(sb("slab" + k, [P, n]), n, split_view)
        keep, keep3 = slab["G"].cut, slab["W"].cut

        x_v = ins["x"].rearrange("b (u p) d -> p (b u) d", p=P)
        c_v = ins["ctx_1024"].rearrange("b (u p) d -> p (b u) d", p=P)
        const_in = load_group("const", [(ident, ins["c_ident"])])
        x_in, ctx_in = [], []
        for g in range(GROUPS):
            x_in += [load_group(f"x{g}", [(x[:, g * GT:(g + 1) * GT, :], x_v[:, g * GT:(g + 1) * GT, :])])] * GT
            ctx_in.append(load_group(f"ctx{g}", [(ctxT[:, g * GN:(g + 1) * GN], ins["ctxT"][:, g * GN:(g + 1) * GN])]))
        ones_set = VEC.run(lambda e: e.memset(ones, 1.0))
        identb_set = VEC.run(lambda e: e.tensor_copy(identb, ident), const_in)
        PE.wait(const_in, ones_set, identb_set)
        ctxt_in = []
        x_ready = [[t] for t in x_in]
        xn_free = [[] for _ in range(TILES)]

        def mm(dst, lhsT, rhs, start, stop, *after, tell=False):
            f = lambda e: e.matmul(dst, lhsT, rhs, start=start, stop=stop, skip_group_check=True)
            return PE.run(f, *after) if tell else PE.quiet(f, *after)

        def transpose(dst, src, idt, *after, tell=False):
            f = lambda e: e.transpose(dst, src, idt)
            return PE.run(f, *after) if tell else PE.quiet(f, *after)

        def rsqrt(n, *after):
            v, i, y, t = rsq_v[:, 0:n], rsq_i[:, 0:n], rsq_y[:, 0:n], rsq_t[:, 0:n]
            VEC.chain(lambda e: e.tensor_scalar(i, v.bitcast(I32), 1, None, ALU.logical_shift_right), *after)
            VEC.chain(lambda e: e.tensor_scalar(y.bitcast(I32), i, -1.0, float(0x5F3759DF), ALU.mult, ALU.add))
            for _ in range(3):
                VEC.chain(lambda e: e.tensor_tensor(t, y, y, ALU.mult))
                VEC.chain(lambda e: e.tensor_tensor(t, t, v, ALU.mult))
                VEC.chain(lambda e: e.tensor_scalar(t, t, -0.5, 1.5, ALU.mult, ALU.add))
                VEC.chain(lambda e: e.tensor_tensor(y, y, t, ALU.mult))
            return VEC.last()

        def normalise(src, dst, n, *after):
            VEC.wait(*after)
            VEC.wait(VEC.last())
            for k in range(n):
                VEC.run(lambda e: e.bn_stats(stats[:, k, :], src[:, k, :]))
            VEC.wait(VEC.last())
            for k in range(n):
                VEC.run(lambda e: e.bn_aggr(meanvar[:, k, :], stats[:, k, :]))
            VEC.chain(lambda e: e.tensor_scalar(rsq_v[:, 0:n], meanvar[:, 0:n, 1], EPS, None, ALU.add))
            rsqrt(n)
            VEC.wait(VEC.last())
            for k in range(n):
                done = VEC.run(lambda e: e.tensor_scalar(dst[:, k, :], src[:, k, :], meanvar[:, k, 0:1],
                                                         rsq_y[:, k:k + 1], ALU.subtract, ALU.mult))
            return done

        def turn(src, dst, n, ready, dst_free=(), scale=None, bias=None):
            b = banks.take()
            for k in range(n):
                t = transpose(b.ap[:, k * P:(k + 1) * P], src[:, k, :], ident, b.free, ready, tell=(k == n - 1))
            if scale is None:
                done = SCA.run(lambda e: e.activation(dst, b.ap[:, 0:n * P], ACT.Copy), t, *dst_free)
            else:
                done = SCA.run(lambda e: e.activation(dst, b.ap[:, 0:n * P], ACT.Identity, scale=scale, bias=bias),
                               t, *dst_free)
            b.free = [done]
            return done

        def norm_x(t0, n):
            ts = slice(t0, t0 + n)
            free = [f for k in range(t0, t0 + n) for f in xn_free[k]]
            done = normalise(x[:, ts, :], xn[:, ts, :], n, *(x_ready[ts] + free))
            for _ in range(3 if n == GT else 2):
                yield
            return done, turn(xn[:, ts, :], xnT[:, t0 * P:(t0 + n) * P], n, done, free)

        def x_written(t0, n, ticket):
            for k in range(t0, t0 + n):
                x_ready[k] = [ticket]

        def xn_read(t0, n):
            for k in range(t0, t0 + n):
                xn_free[k] = all_last()

        def add_to_x(t0, n, bank, ready):
            t = VEC.run(lambda e: e.tensor_tensor(x[:, t0:t0 + n, :],
                                                  bank.ap[:, 0:n * P].rearrange("p (t d) -> p t d", t=n),
                                                  x[:, t0:t0 + n, :], ALU.add), ready, *x_ready[t0:t0 + n])
            bank.free = [t]
            x_written(t0, n, t)

        def split_x(g, xs, xT, *free):
            src = xnT[:, g * GN:(g + 1) * GN]
            VEC.run(lambda e: e.tensor_copy(xs[0], src), xT, *free)
            return VEC.chain(lambda e: e.tensor_tensor(xs[1], src, xs[0].bitcast(F32), ALU.subtract))

        def split_w(ws, src, ready):
            h = POOL.run(lambda e: e.tensor_copy(ws.ap[:, 0], src), ready, ws.free)
            return ws, POOL.run(lambda e: e.tensor_tensor(ws.ap[:, 1], src, ws.ap[:, 0].bitcast(F32), ALU.subtract), h)

        def mm_split(dst, w_hi, w_lo, xs, *after):
            mm(dst, w_hi, xs[0], True, False, *after)
            mm(dst, w_lo, xs[0], False, False)
            return mm(dst, w_hi, xs[1], False, True, tell=True)

        def project_tokens(bank, n, lhs_of, weights, bias_row, ready, *after):
            for t in range(n):
                o = bank.ap[:, t * P:(t + 1) * P]
                if bias_row is not None:
                    mm(o, ones[0:1, :], bias_row, True, False, bank.free, ready, *after)
                for k, w in enumerate(weights):
                    done = mm(o, lhs_of(t, k), w, bias_row is None and k == 0, k == len(weights) - 1,
                              bank.free, ready, *after, tell=(k == len(weights) - 1))
            return done

        def all_last():
            return [q.last() for q in (PE, VEC, SCA, POOL)]

        def enter(*names):
            return [t for k in names for t in slab[k].enter()]

        def leave(*names):
            for k in names:
                slab[k].users = all_last()

        def pick_row(k):
            return identb[:, k:k + 1].to_broadcast([P, P])

        def tile_cols(t):
            return slice(t * P, (t + 1) * P)

        def retention():
            H, HD = 16, 8
            cut, cute, cutc = slab["B"].cut, slab["E"].cut, slab["C"].cut
            w = cut([P, 7, P])
            rows = cut([1, 2, P])
            tab = cut([P, 4, S])
            masks = cut([P, 16 + P + 512])
            win = load_group("ret", [(w, ins["w_ret"]), (rows[0:1], ins["rows_ret"]),
                                     (tab, ins["c_xpos"]), (masks, ins["c_retmask"])])
            head16, blockdiag, causal = masks[:, 0:16], masks[:, 16:16 + P], masks[:, 16 + P:]
            PITCH = GT * P + HD
            VM = cut([P, H * PITCH])
            VMw = VM.rearrange("p (h r) -> p h r", r=PITCH)[:, :, 0:GT * P].rearrange(
                "p h (t d) -> p h t d", t=GT)[:, :, :, 0:HD]
            VMr = lambda h, t: VM[:, (h * GT + t) * P:(h * GT + t + 1) * P]
            masked = Ring([cute([P, 4, S]), cutc([P, 4, S])])
            probs = Ring([cute([P, 512]) for _ in range(3)] + [slab["W"].cut([P, 512])])
            QT, KT = cutc([P, GN]), cutc([P, GN])
            rot = cutc([P, 2, GN])
            Ktok, state, V = cute([P, 2, P]), cute([P, 2, P]), cutc([P, 2, P])
            mu = cut([P, 64])
            cen, sq, gate = cutc([P, 512]), cutc([P, 512]), cute([P, 512])
            yT = sq
            zeroed = POOL.run(lambda e: e.memset(VM, 0.0))
            front_end, tail_end = [], []
            yield "loaded"
            heads = lambda a: a.rearrange("p (h e) -> p h e", e=HD)
            wide = lambda a: a.unsqueeze(2).to_broadcast([P, 64, HD])
            def unit(g):
                nonlocal front_end, tail_end
                cols = slice(g * GN, (g + 1) * GN)

                def rotated(dst, k, src, t0, ready):
                    made = []
                    VEC.wait(VEC.last())
                    for j in range(2):
                        b = banks.take()
                        m = mm(b.ap, w[:, k + j, :], src[:, cols], True, True, b.free, ready, win, tell=True)
                        v = VEC.run(lambda e: e.tensor_tensor(
                            rot[:, j, :].rearrange("p (b s) -> p b s", b=2), b.ap.rearrange("p (b s) -> p b s", b=2),
                            tab[:, t0 + j:t0 + j + 1, :].to_broadcast([P, 2, S]), ALU.mult), m, win, *front_end)
                        b.free = [v]
                        made.append(v)
                    return VEC.chain(lambda e: e.tensor_tensor(dst, rot[:, 0, :], rot[:, 1, :], ALU.add), made)

                k_ready = rotated(KT, 2, ctxT, 2, ctx_in[g])
                b = banks.take()
                v_mm = project_tokens(b, GT, lambda t, k: ctxT[:, tile_cols(g * GT + t)], [w[:, 4, :]], None, win,
                                      ctx_in[g])
                v_ready = SCA.run(lambda e: e.activation(V, b.ap.rearrange("p (t c d) -> p t c d", t=2, c=2)[:, :, 0, :],
                                                         ACT.Copy), v_mm, *front_end)
                vm_ready = SCA.run(lambda e: e.activation(
                    VMw, b.ap.rearrange("p (t h e) -> p h t e", t=GT, e=HD), ACT.Copy), zeroed, *front_end)
                b.free = [vm_ready]
                _, xT = yield from norm_x(g * GT, GT)
                b = banks.take()
                for u in range(2):
                    t = transpose(b.ap[:, u * P:(u + 1) * P], KT[:, 2 * u * P:(2 * u + 1) * P], ident,
                                  b.free, k_ready, tell=(u == 1))
                ktok = SCA.run(lambda e: e.activation(Ktok, b.ap[:, 0:2 * P].rearrange("p (t d) -> p t d", t=2),
                                                      ACT.Copy), t, *front_end)
                b.free = [ktok]
                yield
                q_ready = rotated(QT, 0, xnT, 0, xT)
                b = banks.take()
                for u in range(2):
                    t = mm(b.ap[:, u * P:(u + 1) * P], Ktok[:, u, :], V[:, u, :], True, True, b.free, ktok,
                           v_ready, tell=(u == 1))
                st = VEC.run(lambda e: e.tensor_tensor(
                    state, b.ap[:, 0:2 * P].rearrange("p (t d) -> p t d", t=2),
                    blockdiag.unsqueeze(1).to_broadcast([P, 2, P]), ALU.mult), t, *front_end)
                b.free = [st]
                ready_masks = []

                def mask_queries(u, c):
                    q = masked.take()
                    for j in range(4):
                        f = lambda e: e.tensor_scalar(q.ap[:, j, :], QT[:, u * S:(u + 1) * S],
                                                      head16[:, 4 * c + j:4 * c + j + 1], None, ALU.mult)
                        if j % 2:
                            qm = VEC.run(f, q_ready, q.free)
                        else:
                            qp = POOL.run(f, q_ready, q.free)
                    ready_masks.append((q, qm, qp))

                mask_queries(0, 0)
                yield
                ret = banks.take()
                for u in range(2):
                    t = 2 * u + 1
                    mm(ret.ap[:, tile_cols(t)], QT[:, tile_cols(t)], state[:, u, :], u == 0, False, ret.free, st,
                       q_ready)
                late = []

                def product(p, pr, c, t):
                    for j in range(4):
                        av = mm(ret.ap[:, tile_cols(t)], p.ap[:, j * P:(j + 1) * P], VMr(4 * c + j, t), False, True,
                                pr, vm_ready, tell=(j == 3))
                    p.free = [av]
                    return av

                for u in range(2):
                    for c in range(4):
                        q, qm, qp = ready_masks.pop(0)
                        if 4 * u + c < 7:
                            mask_queries(*divmod(4 * u + c + 1, 4))
                        for i in range(2):
                            t = 2 * u + i
                            b = banks.take()
                            s_mm = mm(b.ap, KT[:, tile_cols(t)], q.ap[:, :, i * P:(i + 1) * P], True, True, b.free,
                                      qm, qp, k_ready, tell=True)
                            p = probs.take()
                            pr = VEC.run(lambda e: e.tensor_tensor(p.ap, b.ap, causal, ALU.mult), s_mm, p.free)
                            b.free = [pr]
                            late.append((p, pr, c, t))
                            if len(late) > 2:
                                product(*late.pop(0))
                        q.free = [s_mm]
                        yield
                while late:
                    av = product(*late.pop(0))
                front_end = all_last()
                yield "next"
                b = banks.take()
                g_mm = project_tokens(b, GT, lambda t, k: xnT[:, tile_cols(g * GT + t)], [w[:, 5, :]],
                                      rows[0:1, 0, :], xT, win)
                gate_ready = SCA.run(lambda e: e.activation(gate, b.ap, ACT.Silu), g_mm, *tail_end)
                b.free = [gate_ready]
                VEC.run(lambda e: e.reduce_sum(mu, heads(ret.ap), AX.X), av, VEC.last())
                VEC.chain(lambda e: e.tensor_scalar(mu, mu, 1.0 / HD, None, ALU.mult))
                c_ready = VEC.chain(lambda e: e.tensor_tensor(heads(cen), heads(ret.ap), wide(mu), ALU.subtract),
                                    *tail_end)
                ret.free = [c_ready]
                sq_ready = SCA.run(lambda e: e.activation(sq, cen, ACT.Square), c_ready, *tail_end)
                VEC.chain(lambda e: e.reduce_sum(rsq_v, heads(sq), AX.X), sq_ready)
                VEC.chain(lambda e: e.tensor_scalar(rsq_v, rsq_v, 1.0 / HD, EPS, ALU.mult, ALU.add))
                rsqrt(64)
                VEC.chain(lambda e: e.tensor_tensor(heads(cen), heads(cen), wide(rsq_y), ALU.mult))
                y_ready = VEC.chain(lambda e: e.tensor_tensor(cen, cen, gate, ALU.mult), gate_ready)
                yield
                yield
                yt = turn(cen.rearrange("p (t d) -> p t d", t=GT), yT, GT, y_ready)
                yield
                b = banks.take()
                o_mm = project_tokens(b, GT, lambda t, k: yT[:, tile_cols(t)], [w[:, 6, :]], rows[0:1, 1, :], yt)
                add_to_x(g * GT, GT, b, o_mm)
                xn_read(g * GT, GT)
                tail_end = all_last()
                yield

            for g in range(GROUPS):
                yield unit(g)

        def router(g, E, w_r, bias_row, kind, coef, tmp, ready, xT, *free):
            logits, top, ex, ssum = tmp
            b = banks.take()
            for t in range(GT):
                o = b.ap[:, t * P:(t + 1) * P]
                if bias_row is not None:
                    mm(o, ones[0:1, :], bias_row, True, False, b.free, xT, ready)
                m = mm(o, xnT[:, tile_cols(g * GT + t)], w_r, bias_row is None, True, b.free, xT, ready,
                       tell=(t == GT - 1))
            made = []
            for r in range(len(coef)):
                lg = VEC.chain(lambda e: e.tensor_copy(
                    logits, b.ap.rearrange("p (t e) -> p t e", t=GT)[:, :, r * E:(r + 1) * E]), m, *free)
                VEC.wait(lg)
                for t in range(GT):
                    VEC.run(lambda e: e.max(top[:, t, :], logits[:, t, :]))
                sub = VEC.chain(lambda e: e.tensor_tensor(ex, logits, top[:, :, 0:1].to_broadcast([P, GT, E]),
                                                          ALU.subtract))
                exd = SCA.run(lambda e: e.activation(ex, ex, ACT.Exp), sub)
                k = 0 if kind == "first" else 1
                VEC.chain(lambda e: e.tensor_tensor(logits, logits, top[:, :, k:k + 1].to_broadcast([P, GT, E]),
                                                    ALU.is_ge))
                if kind != "pair":
                    VEC.chain(lambda e: e.reduce_sum(ssum, ex, AX.X), exd)
                VEC.chain(lambda e: e.tensor_tensor(ex, ex, logits, ALU.mult), exd)
                if kind == "pair":
                    VEC.chain(lambda e: e.reduce_sum(ssum, ex, AX.X))
                VEC.chain(lambda e: e.reciprocal(ssum, ssum))
                if kind != "pair":
                    VEC.chain(lambda e: e.tensor_scalar(ssum, ssum, 2.0 if kind == "first" else 0.5, None, ALU.mult))
                made.append(VEC.chain(lambda e: e.tensor_tensor(
                    coef[r], ex, ssum.unsqueeze(2).to_broadcast([P, GT, E]), ALU.mult)))
            b.free = [made[-1]]
            return made

        def router_scratch(cut, E):
            return cut([P, GT, E]), cut([P, GT, 8]), cut([P, GT, E]), cut([P, GT])

        def lagged(blocks, up, down, lag, pause):
            pend = []
            for n, blk in enumerate(blocks):
                pend.append((blk, up(blk)))
                if len(pend) > lag:
                    down(*pend.pop(0))
                if n % pause == pause - 1:
                    yield
            for p in pend:
                down(*p)
            yield

        def moe_gelu():
            E, F = 8, 512
            FB = F // P
            w1 = slab["A"].cut([P, E * F])
            w2 = slab["A"].cut([P, E * FB, D])
            b1, b2, wr, br = keep([P, E * FB]), keep([E, D]), keep([P, P]), keep([1, P])
            win = load_group("moe0", [(wr, ins["r0_w"]), (br, ins["r0_b"]), (b1, ins["e0_b1"]), (b2, ins["e0_b2"]),
                                      (w1, ins["e0_w1"]), (w2.rearrange("p a d -> p (a d)"), ins["e0_w2"])])
            yield "loaded"
            free = enter("D")
            cut = slab["D"].cut
            coefs = [cut([P, GT, E]) for _ in range(2)]
            tmp = router_scratch(cut, E)
            coefTs = [cut([E, GN]) for _ in range(2)]
            hs = Ring([cut([P, GN]) for _ in range(3)])
            for k in hs.buffers:
                k.tickets = free
            b2_done = [list(free), list(free)]
            cut = slab["W"].cut
            xs = [cut([P, GN], R32) for _ in range(2)]
            wsplit = Ring([cut([P, 2, P], R32) for _ in range(3)])
            xs_free = []

            def unit(g):
                nonlocal xs_free
                coef, coefT = coefs[g % 2], coefTs[g % 2]
                _, xT = yield from norm_x(g * GT, GT)
                yield
                c_ready, = router(g, E, wr, br, "pair", [coef], tmp, win, xT, *free)
                yield
                yield
                b = banks.take()
                for t in range(GT):
                    m = transpose(b.ap[0:E, t * P:(t + 1) * P], coef[:, t, :], ident, b.free, c_ready,
                                  tell=(t == GT - 1))
                ct = SCA.run(lambda e: e.activation(coefT, b.ap[0:E, :], ACT.Copy), m, *b2_done[g % 2])
                b.free = [ct]
                yield
                acc = {}

                def up(blk):
                    b, h = banks.take(), hs.take()
                    if blk + 2 < E * FB:
                        weights.append(split_w(wsplit.take(), w1[:, (blk + 2) * P:(blk + 3) * P], win))
                    ws, wr = weights.pop(0)
                    m = mm_split(b.ap, ws.ap[:, 0, :], ws.ap[:, 1, :], xs, b.free, x_split, wr)
                    ws.free = [m]
                    done = SCA.run(lambda e: e.activation(h.ap, b.ap, ACT.Gelu, bias=b1[:, blk:blk + 1]), m, h.free)
                    b.free = [done]
                    return h, done

                def down(blk, made):
                    h, done = made
                    ex, k = divmod(blk, FB)
                    if k == 0:
                        acc[0] = banks.take()
                    b = acc[0]
                    for t in range(GT):
                        m = mm(b.ap[:, tile_cols(t)], h.ap[:, tile_cols(t)], w2[:, blk, :], k == 0 and t == 0,
                               k == FB - 1, b.free, done, tell=(t == GT - 1))
                    h.free = [m]
                    if k == FB - 1:
                        for t in range(GT):
                            n = g * GT + t
                            v = VEC.run(lambda e: e.scalar_tensor_tensor(
                                x[:, n, :], b.ap[:, tile_cols(t)], coef[:, t, ex:ex + 1], x[:, n, :], ALU.mult,
                                ALU.add), m, c_ready, x_ready[n])
                            x_ready[n] = [v]
                        b.free = [v]

                yield "next"
                x_split = split_x(g, xs, xT, *xs_free)
                weights = [split_w(wsplit.take(), w1[:, k * P:(k + 1) * P], win) for k in range(2)]
                b = banks.take()
                for t in range(GT):
                    m = mm(b.ap[:, tile_cols(t)], coefT[:, tile_cols(t)], b2, True, True, b.free, ct,
                           win, tell=(t == GT - 1))
                b2_done[g % 2] = [m]
                add_to_x(g * GT, GT, b, m)
                yield from lagged(range(E * FB), up, down, 2, 1)
                xs_free = [PE.last()]
                xn_read(g * GT, GT)

            for g in range(GROUPS):
                yield unit(g)

        def bidaf():
            Wl, cols, bias3, row = keep([P, 4, D]), keep([P, 3]), keep([P, 3]), keep([1, D])
            win = load_group("bidaf", [(Wl, ins["l1_W"]), (cols, ins["l1_cols"]), (bias3, ins["l1_bias"]),
                                       (row, ins["l1_row"])])
            yield "loaded"
            free = enter("E")
            cut = slab["E"].cut
            sets = [dict(cw=cut([P, S]), attn=cut([P, 2, S]), aT=cut([P, 2, S]), c2q=cut([P, 2, S]),
                         mx=cut([P, 4]), nm=cut([P, 2]), sm=cut([P, 2]), rs=cut([P, 2]), mtop=cut([1, 2]),
                         eb=cut([P, 2]), rb=cut([P, 2]), q2c=cut([P, 2]), W14=cut([P, D]), end=list(free))
                    for _ in range(2)]
            bsum = keep([P, 2])
            VEC.run(lambda e: e.reduce_sum(bsum[:, 0:1], bias3, AX.X), win)
            def unit(bt):
                z = sets[bt % 2]
                end = z["end"]
                cw, attn, aT, c2q, mx, nm, sm, rs, mtop, eb, rb, q2c, W14 = (
                    z[k] for k in ("cw", "attn", "aT", "c2q", "mx", "nm", "sm", "rs", "mtop", "eb", "rb", "q2c",
                                   "W14"))
                xnr, xT = yield from norm_x(2 * bt, 2)
                tok = slice(bt * S, (bt + 1) * S)
                tile = lambda i: slice(bt * S + i * P, bt * S + (i + 1) * P)
                cwr = VEC.run(lambda e: e.tensor_scalar(cw, xnT[:, tok], cols[:, 0:1], cols[:, 1:2],
                                                        ALU.mult, ALU.add), xT, win, *end)
                yield
                b = banks.take()
                for i in range(2):
                    s_mm = mm(b.ap[:, i * S:(i + 1) * S], cw[:, i * P:(i + 1) * P], ctxT[:, tok], True, True,
                              b.free, cwr, ctx_in, tell=(i == 1))
                bc = banks.take()
                for i in range(2):
                    c_mm = mm(bc.ap[:, i:i + 1], xnT[:, tile(i)], cols[:, 2:3], True, True, bc.free, xT, win,
                              tell=(i == 1))
                VEC.wait(VEC.last())
                VEC.run(lambda e: e.reduce_max(mx[:, 0:2], b.ap.rearrange("p (i s) -> p i s", i=2), AX.X), s_mm)
                nmr = VEC.chain(lambda e: e.tensor_scalar(nm, mx[:, 0:2], -1.0, None, ALU.mult))
                mr = VEC.chain(lambda e: e.scalar_tensor_tensor(mx[:, 2:4], bc.ap[:, 0:2], bsum[:, 0:1],
                                                                mx[:, 0:2], ALU.add, ALU.add), c_mm)
                bc.free = [mr]
                for i in range(2):
                    ex = SCA.run(lambda e: e.activation(attn[:, i, :], b.ap[:, i * S:(i + 1) * S], ACT.Exp,
                                                        bias=nm[:, i:i + 1], accum_out=sm[:, i:i + 1]), nmr, *end)
                b.free = [ex, mr]
                yield
                b = banks.take()
                for i in range(2):
                    t = mm(b.ap[0:1, i * P:(i + 1) * P], mx[:, 2 + i:3 + i], ident, True, True, b.free, mr,
                           tell=(i == 1))
                VEC.chain(lambda e: e.reciprocal(rs, sm), ex)
                VEC.wait(VEC.last())
                for i in range(2):
                    ar = VEC.run(lambda e: e.tensor_scalar(attn[:, i, :], attn[:, i, :], rs[:, i:i + 1],
                                                           None, ALU.mult))
                VEC.run(lambda e: e.reduce_max(mtop[0:1, 0:1], b.ap[0:1, 0:S], AX.X), t, *end)
                mt = VEC.chain(lambda e: e.tensor_scalar(mtop[0:1, 0:1], mtop[0:1, 0:1], -1.0, None, ALU.mult))
                b.free = [mt]
                yield "next"
                b = banks.take()
                for i in range(2):
                    for j in range(2):
                        t = transpose(b.ap[:, j * S + i * P:j * S + (i + 1) * P], attn[:, i, j * P:(j + 1) * P],
                                      ident, b.free, ar, tell=(i + j == 2))
                at = SCA.run(lambda e: e.activation(aT, b.ap.rearrange("p (j s) -> p j s", j=2), ACT.Copy), t, *end)
                b.free = [at]
                b = banks.take()
                t = mm(b.ap[:, 0:1], ones[0:1, :], mtop[0:1, 0:1], True, True, b.free, mt, tell=True)
                nb = VEC.run(lambda e: e.tensor_copy(q2c[:, 0:1], b.ap[:, 0:1]), t, *end)
                b.free = [nb]
                er = SCA.run(lambda e: e.activation(eb, mx[:, 2:4], ACT.Exp, bias=q2c[:, 0:1]), nb, *end)
                yield
                b = banks.take()
                for j in range(2):
                    t = mm(b.ap[:, 0:S], ctxt[:, 2 * bt + j, :], aT[:, j, :], j == 0, j == 1, b.free, at, ctxt_in,
                           tell=(j == 1))
                c1 = SCA.run(lambda e: e.activation(c2q[:, 0, :], b.ap[:, 0:S], ACT.Copy), t, *end)
                c2 = VEC.run(lambda e: e.tensor_tensor(c2q[:, 1, :], c2q[:, 0, :], xnT[:, tok], ALU.mult), c1)
                b.free = [c1]
                b = banks.take()
                for i in range(2):
                    mm(b.ap[:, 0:1], xn[:, 2 * bt + i, :], eb[:, i:i + 1], i == 0, i == 1, b.free, er, xnr)
                for i in range(2):
                    t = mm(b.ap[:, 1:2], ones, eb[:, i:i + 1], i == 0, i == 1, tell=(i == 1))
                VEC.run(lambda e: e.reciprocal(rb[:, 0:1], b.ap[:, 1:2]), t)
                q2 = VEC.chain(lambda e: e.tensor_scalar(q2c[:, 1:2], b.ap[:, 0:1], rb[:, 0:1], None, ALU.mult))
                b.free = [q2]
                w14 = VEC.chain(lambda e: e.scalar_tensor_tensor(W14, Wl[:, 3, :], q2c[:, 1:2], Wl[:, 0, :],
                                                                 ALU.mult, ALU.add))
                yield
                b = banks.take()
                for i in range(2):
                    o = b.ap[:, tile_cols(i)]
                    mm(o, ones[0:1, :], row[0:1, :], True, False, b.free, w14, c2)
                    mm(o, xnT[:, tile(i)], W14, False, False)
                    mm(o, c2q[:, 0, tile_cols(i)], Wl[:, 1, :], False, False)
                    t = mm(o, c2q[:, 1, tile_cols(i)], Wl[:, 2, :], False, True, tell=(i == 1))
                add_to_x(2 * bt, 2, b, t)
                z["end"] = [t, er, w14, c1]
                xn_read(2 * bt, 2)
                yield

            for bt in range(B):
                yield unit(bt)

        def moe_swiglu():
            E, F = 8, 512
            FB = F // P
            free_b = enter("B")
            cut = slab["B"].cut
            wgu, wd = cut([P, 2, E * F]), cut([P, E * FB, D])
            wr = keep([P, P])
            win = load_group("moe1", [(wr, ins["r1_w"]), (wgu[:, 0, :], ins["e1_g"]), (wgu[:, 1, :], ins["e1_u"]),
                                      (wd.rearrange("p a d -> p (a d)"), ins["e1_d"])], *free_b)
            yield "loaded"
            free = enter("C")
            cut = slab["C"].cut
            coefs = [cut([P, GT, E]) for _ in range(2)]
            tmp = router_scratch(cut, E)
            hs = Ring([cut([P, GN]) for _ in range(3)])
            xs = [cut([P, GN], R32) for _ in range(2)]
            wsplit = Ring([cut([P, 2, 2, P], R32) for _ in range(3)])
            for k in hs.buffers + wsplit.buffers:
                k.tickets = free
            xs_free = list(free)

            def unit(g):
                nonlocal xs_free
                coef = coefs[g % 2]
                _, xT = yield from norm_x(g * GT, GT)
                yield
                c_ready, = router(g, E, wr, None, "first", [coef], tmp, win, xT, *free)
                yield
                acc = {}

                def up(blk):
                    bg, bu, h = banks.take(), banks.take(), hs.take()
                    if blk + 2 < E * FB:
                        weights.append(split_w(wsplit.take(), wgu[:, :, (blk + 2) * P:(blk + 3) * P], win))
                    ws, wr = weights.pop(0)
                    m1 = mm_split(bg.ap, ws.ap[:, 0, 0, :], ws.ap[:, 1, 0, :], xs, bg.free, x_split, wr)
                    m2 = mm_split(bu.ap, ws.ap[:, 0, 1, :], ws.ap[:, 1, 1, :], xs, bu.free)
                    ws.free = [m2]
                    a = SCA.run(lambda e: e.activation(h.ap, bg.ap, ACT.Silu), m1, h.free)
                    bg.free = [a]
                    done = VEC.run(lambda e: e.tensor_tensor(h.ap, bu.ap, h.ap, ALU.mult), m2, a)
                    bu.free = [done]
                    return h, done

                def down(blk, made):
                    h, done = made
                    ex, k = divmod(blk, FB)
                    if k == 0:
                        acc[0] = banks.take()
                    b = acc[0]
                    for t in range(GT):
                        m = mm(b.ap[:, tile_cols(t)], h.ap[:, tile_cols(t)], wd[:, blk, :], k == 0 and t == 0,
                               k == FB - 1, b.free, done, tell=(t == GT - 1))
                    h.free = [m]
                    if k == FB - 1 and ex == E - 1:
                        add_to_x(g * GT, GT, b, m)
                    elif k == FB - 1:
                        for t in range(GT):
                            n = g * GT + t
                            v = VEC.run(lambda e: e.scalar_tensor_tensor(
                                x[:, n, :], b.ap[:, tile_cols(t)], coef[:, t, ex:ex + 1], x[:, n, :], ALU.mult,
                                ALU.add), m, c_ready, x_ready[n])
                            x_ready[n] = [v]
                        b.free = [v]

                yield "next"
                x_split = split_x(g, xs, xT, *xs_free)
                weights = [split_w(wsplit.take(), wgu[:, :, k * P:(k + 1) * P], win) for k in range(2)]
                yield from lagged(range(E * FB), up, down, 2, 1)
                xs_free = [PE.last()]
                xn_read(g * GT, GT)

            for g in range(GROUPS):
                yield unit(g)

        def attention16():
            H, HD = 16, 8
            w, bcols, rows = keep([P, 3, P]), keep([P, 2]), keep([1, 2, P])
            wo = keep([P, P])
            head16 = keep([P, 16])
            free = enter("A", "E")
            cut = slab["A"].cut
            mki = cut([P, TILES], I32)
            mri = cut([P, TILES * P], I32)
            keepr = cut([P, TILES * P])
            win = load_group("att16", [(w, ins["l2_w"]), (bcols, ins["l2_cols"]), (rows, ins["l2_rows"]),
                                       (wo, ins["l2_wo"]), (head16, ins["c_retmask"][:, 0:16]),
                                       (mki, ins["mask_cols"]), (mri, ins["mask_row"])], *free)
            yield "loaded"
            flag = cut([P, 2, B])
            negc = cut([P, TILES])
            negr = cut([P, TILES * P], BF16)
            VEC.run(lambda e: e.tensor_scalar(keepr, mri, 0.0, None, ALU.not_equal), win)
            VEC.chain(lambda e: e.reduce_max(flag[:, 0, :], keepr.rearrange("p (b s) -> p b s", b=B), AX.X))
            VEC.chain(lambda e: e.tensor_scalar(flag[:, 1, :], flag[:, 0, :], float(HD) ** -0.5, None, ALU.mult))
            VEC.run(lambda e: e.tensor_scalar(negc, mki, 0.0, NEG, ALU.is_equal, ALU.mult))
            VEC.chain(lambda e: e.tensor_tensor(
                negc.rearrange("p (b u) -> p b u", b=B), negc.rearrange("p (b u) -> p b u", b=B),
                flag[:, 0, :].unsqueeze(2).to_broadcast([P, B, 2]), ALU.mult))
            VEC.run(lambda e: e.tensor_scalar(keepr, keepr, -NEG, NEG, ALU.mult, ALU.add))
            mask_ready = VEC.chain(lambda e: e.tensor_tensor(
                negr.rearrange("p (b s) -> p b s", b=B), keepr.rearrange("p (b s) -> p b s", b=B),
                flag[:, 0, :].unsqueeze(2).to_broadcast([P, B, S]), ALU.mult))
            slab["A"].at = TILES
            qms = Ring([cut([P, 2, S]) for _ in range(4)])
            kms = Ring([cut([P, 2, S], BF16) for _ in range(4)])
            assert slab["A"].at <= TILES + 2 * TILES * P
            for k in qms.buffers + kms.buffers:
                k.tickets = [mask_ready]
            slab["A"].at = TILES + 2 * TILES * P + 2 * B + TILES + TILES * P // 2
            sets = [dict(QT=cut([P, S]), KT=cut([P, S]), QTb=cut([P, S], BF16), V=cut([P, 2, H, 32]),
                         nmx=cut([P, 2, P]), nmT=cut([P, S], BF16), end=[]) for _ in range(2)]
            ce = slab["E"].cut
            probs = Ring([(ce if k < 7 else cut)([P, 512]) for k in range(8)])
            OT = cut([P, 4, S])
            att, attT = cut([P, 2, P]), ce([P, 2 * P])
            rs = cut([P, 2, H])
            for z in sets:
                VEC.run(lambda e: e.memset(z["nmx"], 0.0))
                VEC.run(lambda e: e.memset(z["V"], 0.0))
                v1 = VEC.chain(lambda e: e.memset(z["V"][:, :, :, HD:HD + 1], 1.0))
            for k in probs.buffers:
                k.tickets = free
            o_free, att_free = [], []
            def unit(bt):
                nonlocal o_free, att_free
                z = sets[bt % 2]
                end = z["end"]
                QT, KT, QTb, V, nmx, nmT = (z[k] for k in ("QT", "KT", "QTb", "V", "nmx", "nmT"))
                tok = slice(bt * S, (bt + 1) * S)
                b = banks.take()
                km = mm(b.ap[:, 0:S], w[:, 1, :], ctxT[:, tok], True, True, b.free, ctx_in, win, tell=True)
                kr = SCA.run(lambda e: e.activation(KT, b.ap[:, 0:S], ACT.Identity, bias=bcols[:, 1:2]), km, *end)
                b.free = [kr]
                b = banks.take()
                for i in range(2):
                    o = b.ap[:, tile_cols(i)]
                    mm(o, ones[0:1, :], rows[0:1, 0, :], True, False, b.free, win)
                    vm = mm(o, ctxT[:, bt * S + i * P:bt * S + (i + 1) * P], w[:, 2, :], False, True, tell=(i == 1))
                vr = SCA.run(lambda e: e.activation(
                    V[:, :, :, 0:HD], b.ap[:, 0:S].rearrange("p (u h e) -> p u h e", u=2, e=HD), ACT.Copy), vm,
                    v1, *end)
                b.free = [vr]
                _, xT = yield from norm_x(2 * bt, 2)
                keys, queries = [], []

                def mask_keys(hp):
                    k = kms.take()
                    for j in range(2):
                        kb = POOL.run(lambda e: e.tensor_scalar(
                            k.ap[:, j, :], KT, head16[:, 2 * hp + j:2 * hp + j + 1], None, ALU.mult), kr, k.free)
                    keys.append((k, kb))

                def mask_queries(hp):
                    q = qms.take()
                    qmr = [VEC.run(lambda e: e.tensor_scalar(
                        q.ap[:, 0, :], QT, head16[:, 2 * hp:2 * hp + 1], None, ALU.mult), qr, q.free),
                        POOL.run(lambda e: e.tensor_scalar(
                            q.ap[:, 1, :], QT, head16[:, 2 * hp + 1:2 * hp + 2], None, ALU.mult), qr, q.free)]
                    queries.append((q, qmr))

                mask_keys(0)
                yield
                b = banks.take()
                qm = mm(b.ap[:, 0:S], w[:, 0, :], xnT[:, tok], True, True, b.free, xT, win, tell=True)
                qr = VEC.run(lambda e: e.tensor_scalar(QT, b.ap[:, 0:S], bcols[:, 0:1], flag[:, 1, bt:bt + 1],
                                                       ALU.add, ALU.mult), qm, *end)
                qb = SCA.run(lambda e: e.activation(QTb, QT, ACT.Copy), qr, *end)
                b.free = [qr]
                yield
                for hp in range(H // 2):
                    k, kb = keys.pop(0)
                    if hp < H // 2 - 1:
                        mask_keys(hp + 1)
                    for i in range(2):
                        b = banks.take()
                        mm(b.ap, QTb[:, i * P:(i + 1) * P], k.ap, True, False, b.free, qb, kb)
                        m = mm(b.ap.rearrange("p (h s) -> p h s", h=2), pick_row(0),
                               negr[:, tok].unsqueeze(1).to_broadcast([P, 2, S]), False, True, mask_ready, tell=True)
                        mr = VEC.run(lambda e: e.tensor_reduce(
                            nmx[:, i, 2 * hp:2 * hp + 2], b.ap.rearrange("p (h s) -> p h s", h=2), AX.X, ALU.max,
                            negate=True), m, *end)
                        b.free = [mr]
                    k.free = [m]
                    yield
                yield "next"
                b = banks.take()
                for i in range(2):
                    t = transpose(b.ap[:, tile_cols(i)], nmx[:, i, :], ident, b.free, mr, tell=(i == 1))
                nt = SCA.run(lambda e: e.activation(nmT, b.ap[:, 0:S], ACT.Copy), t, *end)
                b.free = [nt]
                mask_queries(0)
                mask_queries(1)
                yield
                late = []

                def product(c, ps):
                    ob = banks.take()
                    for kt in range(2):
                        for j in range(4):
                            p, er = ps[j // 2][kt]
                            hh = j % 2
                            av = mm(ob.ap[32 * j:32 * j + 32, 0:S], V[:, kt, 4 * c + j, :],
                                    p.ap[:, hh * S:(hh + 1) * S], kt == 0, kt == 1, ob.free, er, vr, tell=(j == 3))
                    for pair in ps:
                        for p, _ in pair:
                            p.free = [av]
                    oc = SCA.run(lambda e: e.activation(OT[:, c, :], ob.ap[:, 0:S], ACT.Copy), av, *o_free)
                    ob.free = [oc]
                    return oc

                for hp in range(H // 2):
                    q, qmr = queries.pop(0)
                    if hp < H // 2 - 2:
                        mask_queries(hp + 2)
                    ps = []
                    for kt in range(2):
                        b = banks.take()
                        mm(b.ap, KT[:, kt * P:(kt + 1) * P], q.ap, True, False, b.free, kr, qmr)
                        for hh in range(2):
                            m = mm(b.ap[:, hh * S:(hh + 1) * S], pick_row(2 * hp + hh), nmT, False, True, nt,
                                   tell=(hh == 1))
                        p = probs.take()
                        er = SCA.run(lambda e: e.activation(p.ap, b.ap, ACT.Exp,
                                                            bias=negc[:, 2 * bt + kt:2 * bt + kt + 1]), m, p.free,
                                     mask_ready)
                        b.free = [er]
                        ps.append((p, er))
                    q.free = [m]
                    if hp % 2 == 0:
                        late.append((hp // 2, [ps]))
                    else:
                        late[-1][1].append(ps)
                        if len(late) > 1:
                            product(*late.pop(0))
                    yield
                oc = product(*late.pop(0))
                yield
                for i in range(2):
                    b = banks.take()
                    for c in range(4):
                        m = transpose(b.ap[:, tile_cols(c)], OT[:, c, i * P:(i + 1) * P], ident, b.free, oc,
                                      tell=(c == 3))
                    o = b.ap.rearrange("p (c j e) -> p (c j) e", c=4, e=32)
                    VEC.chain(lambda e: e.reciprocal(rs[:, i, :], o[:, :, HD]), m)
                    ar = VEC.chain(lambda e: e.tensor_tensor(
                        att[:, i, :].rearrange("p (h e) -> p h e", e=HD), o[:, :, 0:HD],
                        rs[:, i, :].unsqueeze(2).to_broadcast([P, H, HD]), ALU.mult), *att_free)
                    b.free = [ar]
                o_free = [m]
                yield
                yield
                tt = turn(att, attT, 2, ar, att_free)
                yield
                yield
                b = banks.take()
                t = project_tokens(b, 2, lambda k, _: attT[:, tile_cols(k)], [wo], rows[0:1, 1, :], tt)
                att_free = [t, tt]
                add_to_x(2 * bt, 2, b, t)
                z["end"] = [t, er, kb, qmr]
                xn_read(2 * bt, 2)
                yield

            for bt in range(B):
                yield unit(bt)

        def bitnet():
            F = 512
            FB = F // P
            UT, UN = 2, 2 * P
            wf = keep([P, 2, F])
            cv = keep([P, FB, 4])
            win = load_group("bit", [(wf, ins["b_w"]), (cv, ins["b_conv"])])
            yield "loaded"
            free = enter("C", "D")
            cut, cutd = slab["C"].cut, slab["D"].cut
            wq = cut([P, 2, F], BF16)
            asum, wmean, wsc = cut([P, 2]), cut([P, 2]), cut([P, 2])
            VEC.run(lambda e: e.tensor_reduce(asum, wf, AX.X, ALU.add, apply_absolute_value=True), win, *free)
            b = banks.take()
            t = mm(b.ap[:, 0:2], ones, asum, True, True, b.free, VEC.last(), tell=True)
            VEC.run(lambda e: e.tensor_scalar(wmean, b.ap[:, 0:2], 1.0 / (F * D), EPS, ALU.mult, ALU.max), t)
            b.free = [VEC.last()]
            VEC.chain(lambda e: e.reciprocal(wsc, wmean))
            VEC.wait(VEC.last())
            for k in range(2):
                VEC.run(lambda e: e.tensor_scalar(wf[:, k, :], wf[:, k, :], wsc[:, k:k + 1], ROUND, ALU.mult,
                                                  ALU.add))
            VEC.chain(lambda e: e.tensor_scalar(wf, wf, ROUND, 1.0, ALU.subtract, ALU.min))
            wr = VEC.chain(lambda e: e.tensor_scalar(wq, wf, -1.0, None, ALU.max))
            amax, qs, deq = cut([P, UT]), cut([P, UT]), cut([P, UT])
            sets = [dict(rnd=c([P, UT, D]), xiT=c([P, UN], BF16), dq=c([P, UN]), hT=c([P, UN]),
                         sT=c([P, FB, UN]), end=list(free)) for c in (cut, cutd)]
            diag = cut([P, UT, P])
            amax2, qs2, deq2 = cut([P, 2]), cut([P, 2]), cut([P, 2])
            hrs = Ring([cut([P, F])])
            his = Ring([cutd([P, F], BF16) for _ in range(2)])
            hiTs = Ring([cutd([P, F], BF16) for _ in range(2)])

            def scales(a, q, d, k, *after):
                VEC.chain(lambda e: e.tensor_scalar(a, a, EPS, None, ALU.max), *after)
                VEC.chain(lambda e: e.reciprocal(q, a))
                VEC.chain(lambda e: e.tensor_scalar(q, q, 127.0, None, ALU.mult))
                return VEC.chain(lambda e: e.tensor_scalar(d, a, 1.0 / 127.0, wmean[:, k:k + 1], ALU.mult, ALU.mult))

            diag_free = list(free)
            def unit(bt):
                nonlocal diag_free
                z = sets[bt % 2]
                end = z["end"]
                rnd, xiT, dq, hT, sT = (z[k] for k in ("rnd", "xiT", "dq", "hT", "sT"))
                xnr, xT = yield from norm_x(UT * bt, UT)
                xg = xn[:, UT * bt:UT * (bt + 1), :]
                VEC.chain(lambda e: e.tensor_reduce(amax, xg, AX.X, ALU.max, apply_absolute_value=True), *end)
                scales(amax, qs, deq, 0)
                VEC.wait(VEC.last())
                VEC.wait(*diag_free)
                for t in range(UT):
                    VEC.run(lambda e: e.tensor_scalar(rnd[:, t, :], xg[:, t, :], qs[:, t:t + 1], ROUND, ALU.mult,
                                                      ALU.add))
                    VEC.run(lambda e: e.tensor_scalar(diag[:, t, :], ident, deq[:, t:t + 1], None, ALU.mult))
                xi = VEC.chain(lambda e: e.tensor_scalar(rnd, rnd, ROUND, None, ALU.subtract))
                yield
                yield
                xt = turn(rnd, xiT, UT, xi, end)
                b = banks.take()
                for t in range(UT):
                    m = mm(b.ap[:, t * P:(t + 1) * P], ones, diag[:, t, :], True, True, b.free, xi,
                           tell=(t == UT - 1))
                diag_free = [m]
                dr = SCA.run(lambda e: e.activation(dq, b.ap[:, 0:UN], ACT.Copy), m, *end)
                b.free = [dr]
                yield
                hr_done = list(end)
                for k in range(FB):
                    b = banks.take()
                    m = mm(b.ap[:, 0:UN], wq[:, 0, k * P:(k + 1) * P], xiT, True, True, b.free, xt, wr, tell=True)
                    h = VEC.run(lambda e: e.tensor_tensor(hT, b.ap[:, 0:UN], dq, ALU.mult), m, dr, *hr_done)
                    b.free = [h]
                    c = SCA.run(lambda e: e.activation(sT[:, k, :], hT, ACT.Identity, scale=cv[:, k, 1:2],
                                                       bias=cv[:, k, 3:4]), h, win, *end)
                    v = VEC.run(lambda e: e.scalar_tensor_tensor(
                        sT[:, k, 1:S], hT[:, 0:S - 1], cv[:, k, 0:1], sT[:, k, 1:S], ALU.mult, ALU.add), c)
                    v = VEC.chain(lambda e: e.scalar_tensor_tensor(
                        sT[:, k, 0:S - 1], hT[:, 1:S], cv[:, k, 2:3], sT[:, k, 0:S - 1], ALU.mult, ALU.add))
                    hr_done = [v]
                    sr = SCA.run(lambda e: e.activation(sT[:, k, :], sT[:, k, :], ACT.Silu), v)
                    yield
                yield "next"
                yb = banks.take()
                for t in range(UT):
                    b = banks.take()
                    for k in range(FB):
                        m = transpose(b.ap[:, k * P:(k + 1) * P], sT[:, k, t * P:(t + 1) * P], ident, b.free,
                                      sr, tell=(k == FB - 1))
                    a2, q2, d2 = amax2[:, t:t + 1], qs2[:, t:t + 1], deq2[:, t:t + 1]
                    VEC.chain(lambda e: e.tensor_reduce(a2, b.ap, AX.X, ALU.max, apply_absolute_value=True), m)
                    scales(a2, q2, d2, 1)
                    hr, hi, hiT = hrs.take(), his.take(), hiTs.take()
                    r = VEC.chain(lambda e: e.tensor_scalar(hr.ap, b.ap, q2, ROUND, ALU.mult, ALU.add), hr.free)
                    b.free = [r]
                    r = VEC.chain(lambda e: e.tensor_scalar(hi.ap, hr.ap, ROUND, None, ALU.subtract), hi.free)
                    hr.free = [r]
                    yield
                    yield
                    b = banks.take()
                    bb = b.ap.bitcast(BF16)
                    for k in range(FB):
                        m = transpose(bb[:, k * P:(k + 1) * P], hi.ap[:, k * P:(k + 1) * P], identb, b.free, r,
                                      tell=(k == FB - 1))
                    hi.free = [m]
                    ht = SCA.run(lambda e: e.activation(hiT.ap, bb[:, 0:F], ACT.Copy), m, hiT.free)
                    b.free = [ht]
                    yield
                    for k in range(FB):
                        m = mm(yb.ap[:, t * P:(t + 1) * P], hiT.ap[:, k * P:(k + 1) * P],
                               wq[:, 1, k * P:(k + 1) * P], k == 0, k == FB - 1, yb.free, ht, tell=(k == FB - 1))
                    hiT.free = [m]
                    n = bt * UT + t
                    xr = VEC.run(lambda e: e.scalar_tensor_tensor(
                        x[:, n, :], yb.ap[:, t * P:(t + 1) * P], d2, x[:, n, :], ALU.mult, ALU.add), m, x_ready[n],
                        VEC.last())
                    x_ready[n] = [xr]
                yb.free = [xr]
                z["end"] = [m, xr, ht]
                xn_read(bt * UT, UT)
                yield

            for bt in range(B):
                yield unit(bt)

        def split3(dst, src, tmp, *after):
            hi, mid, lo = dst
            a, c = tmp
            VEC.chain(lambda e: e.tensor_copy(a, src), *after)
            VEC.chain(lambda e: e.tensor_copy(hi, a))
            VEC.chain(lambda e: e.tensor_tensor(c, src, a, ALU.subtract))
            VEC.chain(lambda e: e.tensor_copy(a, c))
            VEC.chain(lambda e: e.tensor_copy(mid, a))
            VEC.chain(lambda e: e.tensor_tensor(c, c, a, ALU.subtract))
            VEC.chain(lambda e: e.tensor_copy(a, c))
            return VEC.chain(lambda e: e.tensor_copy(lo, a))

        def attention8():
            H, HD, M = 8, 64, 2 * S
            KT4 = M // P
            HB = H * HD // P
            free = enter("B", "W")
            cut = slab["B"].cut
            W = cut([P, 2048])
            Wq, Wkv = W[:, 0:512], W[:, 512:1536]
            Wo = W[:, 1536:2048].rearrange("p (k d) -> p k d", k=HB)
            colw, lno = keep3([P, 6]), keep3([P, 2, D])
            par2 = keep3([P, 2])
            selb = keep3([P, 512], BF16)
            blk8 = keep3([P, P + 8])
            mki = keep3([P, TILES], U8)
            Ks = [cut([P, HB, M]) for _ in range(2)]
            mri = Ks[1].rearrange("p a b -> p (a b)")[:, 0:TILES * P // 4].bitcast(U8)
            win = load_group("att8", [(W, ins["l3_w"]), (colw, ins["l3_cols"]), (lno, ins["l3_lno"]),
                                      (par2, ins["c_par2"]), (selb.bitcast(mybir.dt.uint16), ins["c_sel24"]),
                                      (blk8, ins["c_blk8"]), (mki, ins["bmask_cols"]), (mri, ins["bmask_row"])],
                             *free)
            yield "loaded"
            free = enter("E")
            enter("C", "D")
            ce, cc, cd = slab["E"].cut, slab["C"].cut, slab["D"].cut
            sets = [dict(K=K, Q=c([P, HB, 2, S]), V=c([P, KT4, H * (HD + 1) + HD]), end=[])
                    for K, c in zip(Ks, (cut, cc))]
            VEC.wait(*free)
            negc = ce([P, TILES])
            negr = cut([P, TILES * P], BF16)
            VEC.run(lambda e: e.tensor_scalar(negc, mki, 0.0, -1e30, ALU.is_equal, ALU.mult), win)
            nr = VEC.run(lambda e: e.tensor_scalar(negr, mri, 0.0, -1e30, ALU.is_equal, ALU.mult), win)
            qk2 = ce([P, 2])
            VEC.run(lambda e: e.tensor_scalar(qk2, par2, colw[:, 4:5], colw[:, 5:6], ALU.mult, ALU.mult))
            c_ready = VEC.chain(lambda e: e.tensor_scalar(qk2, qk2, 8.0, None, ALU.mult))
            lnt = ce([P, 2, D])
            kvT = ce([P, M])
            qraw = ce([P, HB, S])
            parts = ce([P, 6, 24])
            tA, tB = ce([P, 48], BF16), ce([P, 48])
            rT = cut([24, 6 * P], BF16)
            nmx, nmT = cut([P, 2, P]), ce([P, S], BF16)
            halves = Ring([(cd if k < 4 else ce)([P, M]) for k in range(5)])
            rs = ce([P, 4])
            atts = [cd([P, H * HD]), ce([P, H * HD])]
            attT, yln = ce([P, HB, P]), ce([P, 1, D])
            VEC.run(lambda e: e.memset(nmx, 0.0))
            v1 = VEC.run(lambda e: e.memset(sets[0]["V"], 1.0))
            upper = lambda a, n: a.bitcast(BF16).rearrange("p (n two) -> p n two", two=2)[:, :, 1]
            kv_free, lnt_free, q_free, nm_free, att_free, r_free = (list(free) for _ in range(6))
            for k in halves.buffers[0:4]:
                k.held = True
            halves.buffers[4].tickets = free

            def second_part():
                nonlocal v1, att_free
                users = slab["C"].users + slab["D"].users
                for k in halves.buffers[0:4]:
                    k.free = users
                att_free = att_free + users
                v1 = VEC.run(lambda e: e.memset(sets[1]["V"], 1.0), *users)
                sets[1]["end"] = [nr] + users


            def unit(bt):
                nonlocal kv_free, lnt_free, q_free, nm_free, att_free, r_free
                z = sets[bt % 2]
                K, Q, V, end = z["K"], z["Q"], z["V"], z["end"]
                Vh = V[:, :, 0:H * (HD + 1)].rearrange("p k (h e) -> p k h e", e=HD + 1)
                yield from norm_x(2 * bt, 2)
                a = normalise(ctxt[:, 2 * bt:2 * bt + 2, :], lnt, 2, ctxt_in, *lnt_free)
                yield
                yield
                t1 = turn(lnt, kvT[:, 0:S], 2, a, [win] + kv_free, colw[:, 0:1], colw[:, 1:2])
                yield
                a = normalise(xn[:, 2 * bt:2 * bt + 2, :], lnt, 2, VEC.last(), t1)
                yield
                yield
                t2 = turn(lnt, kvT[:, S:M], 2, a, [win] + kv_free, colw[:, 2:3], colw[:, 3:4])
                lnt_free = [t2]
                yield
                nb, nb2 = banks.take(), banks.take()
                squares = []

                def add_squares(k, side, sq, s2):
                    to, n = (nb, KT4) if side == 0 else (nb2, 2)
                    for i in range(n):
                        m = mm(to.ap[:, i * P:(i + 1) * P], sq.ap[:, i * P:(i + 1) * P],
                               blk8[:, 8 - 2 * k:8 - 2 * k + P], k == 0 and i == 0, k == HB - 1, to.free, s2,
                               tell=(i == n - 1))
                    sq.free = [m]
                    return m

                for k in range(HB):
                    for side in range(2):
                        n = M if side == 0 else S
                        src = kvT if side == 0 else kvT[:, S:M]
                        wgt = Wkv[:, k * P:(k + 1) * P] if side == 0 else Wq[:, k * P:(k + 1) * P]
                        dst = K[:, k, :] if side == 0 else qraw[:, k, :]
                        if bt == 0 and squares:
                            add_squares(*squares.pop())
                        b, sq = banks.take(), halves.take()
                        m = mm(b.ap[:, 0:n], wgt, src, True, True, b.free, t1, t2, win, tell=True)
                        s2 = SCA.run(lambda e: e.activation(sq.ap[:, 0:n], b.ap[:, 0:n], ACT.Square), m, sq.free)
                        rw = VEC.run(lambda e: e.tensor_copy(dst, b.ap[:, 0:n]), m, s2, *(end if side == 0 else q_free))
                        b.free = [s2, rw]
                        if squares:
                            add_squares(*squares.pop())
                        squares.append((k, side, sq, s2))
                        yield
                m = add_squares(*squares.pop())
                VEC.chain(lambda e: e.tensor_scalar(
                    rsq_v[:, 0:32].rearrange("p (t h) -> p t h", t=4),
                    nb.ap.rearrange("p (t h) -> p t h", t=4)[:, :, 0:8], 1e-24, None, ALU.max), m)
                VEC.run(lambda e: e.tensor_scalar(
                    rsq_v[:, 32:48].rearrange("p (t h) -> p t h", t=2),
                    nb2.ap[:, 0:2 * P].rearrange("p (t h) -> p t h", t=2)[:, :, 0:8], 1e-24, None, ALU.max))
                nb.free = [VEC.last()]
                nb2.free = [VEC.last()]
                rsqrt(48)
                pv = lambda j: parts[:, :, 8 * j:8 * j + 8]
                as6 = lambda z: z.rearrange("p (t h) -> p t h", t=6)
                pr = split3((pv(0), pv(1), pv(2)), as6(rsq_y[:, 0:48]), (as6(tA), as6(tB)), *r_free)
                for i in range(KT4):
                    b = banks.take()
                    m = mm(b.ap, kvT[:, i * P:(i + 1) * P], Wkv[:, 512:1024], True, True, b.free, t1, t2, tell=True)
                    vr = SCA.run(lambda e: e.activation(
                        Vh[:, i, :, 0:HD], b.ap.rearrange("p (h e) -> p h e", e=HD), ACT.Copy), m, v1, *end)
                    b.free = [vr]
                kv_free = [m]
                yield
                b, b2 = banks.take(), banks.take()
                for i in range(6):
                    dst = (b if i < 4 else b2).ap[0:24, (i % 4) * P:(i % 4 + 1) * P]
                    m = transpose(dst, parts[:, i, :], ident, b.free, b2.free, pr, tell=(i == 5))
                SCA.run(lambda e: e.activation(rT[:, 0:512], b.ap[0:24, :], ACT.Copy), m, *r_free)
                rt = SCA.run(lambda e: e.activation(rT[:, 512:768], b2.ap[0:24, 0:256], ACT.Copy))
                b.free = [rt]
                b2.free = [rt]
                yield
                for k in range(HB):
                    b = banks.take()
                    m = mm(b.ap, selb[0:24, k * P:(k + 1) * P], rT[:, 0:M], True, True, b.free, rt, c_ready, tell=True)
                    kr = VEC.run(lambda e: e.tensor_tensor(K[:, k, :], b.ap, K[:, k, :], ALU.mult), m, rw)
                    b.free = [kr]
                    b = banks.take()
                    m = mm(b.ap[:, 0:S], selb[0:24, k * P:(k + 1) * P], rT[:, M:M + S], True, True, b.free, rt,
                           tell=True)
                    for j in range(2):
                        qr = VEC.run(lambda e: e.scalar_tensor_tensor(
                            Q[:, k, j, :], b.ap[:, 0:S], qk2[:, j:j + 1], qraw[:, k, :], ALU.mult, ALU.mult), m, rw,
                            *end)
                    b.free = [qr]
                r_free, q_free = [m], [qr]
                yield
                for h in range(H):
                    for i in range(2):
                        b = banks.take()
                        mm(b.ap, upper(Q[:, h // 2, h % 2, i * P:(i + 1) * P], P), upper(K[:, h // 2, :], M),
                           True, False, b.free, kr, qr)
                        m = mm(b.ap[:, 0:S], pick_row(0), negr[:, bt * S:(bt + 1) * S], False, True, nr, tell=True)
                        mr = VEC.run(lambda e: e.tensor_reduce(nmx[:, i, h:h + 1], b.ap, AX.X,
                                                               ALU.max, negate=True), m, *nm_free)
                        b.free = [mr]
                    if h % 2:
                        yield
                yield
                yield "next"
                if bt == 0:
                    second_part()
                b = banks.take()
                for i in range(2):
                    t = transpose(b.ap[:, i * P:(i + 1) * P], nmx[:, i, :], ident, b.free, mr, tell=(i == 1))
                nt = SCA.run(lambda e: e.activation(nmT, b.ap[:, 0:S], ACT.Copy), t, *nm_free)
                b.free = [nt]
                nm_free = [t]
                yield
                late = []
                obs = []

                def product(h, half, p, er):
                    nonlocal obs
                    if h % 4 == 0 and half == 0:
                        obs = [banks.take(), banks.take()]
                    for i in range(2):
                        for j in range(2):
                            av = mm(obs[i].ap[:, (h % 4) * P:(h % 4 + 1) * P], p.ap[:, j * S + i * P:j * S + (i + 1) * P],
                                    V[:, 2 * half + j, h * (HD + 1):h * (HD + 1) + P], half == 0 and j == 0,
                                    half == 1 and j == 1, obs[i].free, er, vr, tell=(j == 1))
                    p.free = [av]
                    if h % 4 == 3 and half == 1:
                        hq = h // 4
                        for i in range(2):
                            o = obs[i].ap.rearrange("p (h e) -> p h e", e=P)
                            VEC.chain(lambda e: e.reciprocal(rs, o[:, :, HD]), av)
                            ar = VEC.chain(lambda e: e.tensor_tensor(
                                atts[i][:, hq * 256:(hq + 1) * 256].rearrange("p (h e) -> p h e", e=HD),
                                o[:, :, 0:HD], rs.unsqueeze(2).to_broadcast([P, 4, HD]), ALU.mult), *att_free)
                            obs[i].free = [ar]
                        return ar

                for h in range(H):
                    for half in range(2):
                        b, p = banks.take(), halves.take()
                        for j in range(2):
                            kt = 2 * half + j
                            o = b.ap[:, j * S:(j + 1) * S]
                            mm(o, K[:, h // 2, kt * P:(kt + 1) * P], Q[:, h // 2, h % 2, :], True, False,
                               b.free, kr, qr)
                            m = mm(o, pick_row(h), nmT, False, True, nt, tell=(j == 1))
                        if half == 0:
                            for j in range(2):
                                er = SCA.run(lambda e: e.activation(
                                    p.ap[:, j * S:(j + 1) * S], b.ap[:, j * S:(j + 1) * S], ACT.Exp,
                                    bias=negc[:, 2 * bt + j:2 * bt + j + 1]), m, p.free, c_ready)
                        else:
                            er = SCA.run(lambda e: e.activation(p.ap, b.ap, ACT.Exp), m, p.free)
                        b.free = [er]
                        late.append((h, half, p, er))
                        if len(late) > 3:
                            product(*late.pop(0))
                        yield
                while late:
                    ar = product(*late.pop(0))
                nm_free = nm_free + [m]
                yield
                for i in range(2):
                    n = 2 * bt + i
                    tt = turn(atts[i].rearrange("p (k d) -> p k d", k=HB), attT.rearrange("p k d -> p (k d)"), HB, ar,
                              [PE.last()])
                    yield
                    yield
                    b = banks.take()
                    for k in range(HB):
                        m = mm(b.ap[:, 0:P], attT[:, k, :], Wo[:, k, :], k == 0, k == HB - 1, b.free, tt,
                               tell=(k == HB - 1))
                    y = normalise(b.ap[:, 0:P].unsqueeze(1), yln, 1, m)
                    b.free = [y]
                    VEC.chain(lambda e: e.tensor_tensor(yln[:, 0, :], yln[:, 0, :], lno[:, 0, :], ALU.mult))
                    VEC.chain(lambda e: e.tensor_tensor(yln[:, 0, :], yln[:, 0, :], lno[:, 1, :], ALU.add))
                    x_ready[n] = [VEC.chain(lambda e: e.tensor_tensor(x[:, n, :], x[:, n, :], yln[:, 0, :], ALU.add),
                                            x_ready[n])]
                    yield
                att_free = [m, tt]
                z["end"] = [PE.last(), VEC.last(), er]
                xn_read(2 * bt, 2)
                yield

            for bt in range(B):
                yield unit(bt)

        def moe_small():
            E, PAIRS = 32, 32
            free_a = enter("A")
            cut = slab["A"].cut
            wg, wu, wd = cut([P, 4096]), cut([P, 4096]), cut([P, PAIRS, D])
            wr = keep3([P, P])
            selb = keep3([P, 16, P], BF16)
            win = load_group("moe3", [(wr, ins["r3_w"]), (selb.rearrange("p a b -> p (a b)").bitcast(
                mybir.dt.uint16), ins["c_sel96"]), (wg, ins["e3_g"]), (wu, ins["e3_u"]),
                (wd.rearrange("p a d -> p (a d)"), ins["e3_d"])], *free_a)
            yield "loaded"
            free = enter("G")
            cut = slab["G"].cut
            coef = [cut([P, GT, E]) for _ in range(2)]
            tmp = router_scratch(cut, E)
            parts = cut([P, GT, 3 * E])
            tA, tB = cut([P, GT, E], BF16), tmp[2]
            cTs = [[cut([3 * E, GN], BF16) for r in range(2)] for _ in range(2)]
            hs = Ring([cut([P, GN]) for _ in range(3)])
            x_hi, x_lo = cut([P, GN], R32), slab["W"].cut([P, GN], R32)
            wsplit = Ring([slab["D"].cut([P, 2, P], R32) for _ in range(2)])
            for k in hs.buffers + wsplit.buffers:
                k.tickets = free + slab["D"].users
            xs_free = list(free)
            ct_free = [list(free), list(free)]
            VEC.wait(*free)

            def unit(g):
                nonlocal xs_free
                cT = cTs[g % 2]
                _, xT = yield from norm_x(g * GT, GT)
                yield
                cr = router(g, E, wr, None, "half", coef, tmp, win, xT)
                yield
                yield
                yield
                cts = []
                for r in range(2):
                    pr = split3(tuple(parts[:, :, j * E:(j + 1) * E] for j in range(3)), coef[r], (tA, tB), cr[r],
                                PE.last())
                    yield
                    yield
                    b = banks.take()
                    for t in range(GT):
                        m = transpose(b.ap[0:3 * E, t * P:(t + 1) * P], parts[:, t, :], ident, b.free, pr,
                                      tell=(t == GT - 1))
                    ct = SCA.run(lambda e: e.activation(cT[r], b.ap[0:3 * E, :], ACT.Copy), m, *ct_free[g % 2])
                    b.free = [ct]
                    cts.append(ct)
                    yield
                acc = {}

                def up(p):
                    if p == 0:
                        acc[0] = banks.take()
                    r = p // 16
                    bg, bu, bc = banks.take(), banks.take(), banks.take()
                    made = []
                    for b, w in ((bg, wg), (bu, wu)):
                        ws, ready = weights.pop(0)
                        m = mm_split(b.ap, ws.ap[:, 0, :], ws.ap[:, 1, :], (x_hi, x_lo), b.free, x_split, ready)
                        ws.free = [m]
                        if p + 1 < PAIRS:
                            weights.append(split_w(wsplit.take(), w[:, (p + 1) * P:(p + 2) * P], win))
                        made.append(m)
                    m1, m2 = made
                    m3 = mm(bc.ap, selb[0:3 * E, p % 16, :], cT[r], True, True, bc.free, cts[r], tell=True)
                    h = hs.take()
                    a = SCA.run(lambda e: e.activation(h.ap, bg.ap, ACT.Silu), m1, h.free)
                    bg.free = [a]
                    v = VEC.run(lambda e: e.tensor_tensor(h.ap, bu.ap, h.ap, ALU.mult), m2, a)
                    bu.free = [v]
                    hd = VEC.run(lambda e: e.tensor_tensor(h.ap, bc.ap, h.ap, ALU.mult), m3, v)
                    bc.free = [hd]
                    return h, hd

                def down(p, made):
                    h, hd = made
                    b = acc[0]
                    for t in range(GT):
                        m = mm(b.ap[:, tile_cols(t)], h.ap[:, tile_cols(t)], wd[:, p, :], p == 0 and t == 0,
                               p == PAIRS - 1, b.free, hd, tell=(t == GT - 1))
                    h.free = [m]
                    if p == PAIRS - 1:
                        add_to_x(g * GT, GT, b, m)

                yield "next"
                x_split = split_x(g, (x_hi, x_lo), xT, *xs_free)
                weights = [split_w(wsplit.take(), w[:, 0:P], win) for w in (wg, wu)]
                yield from lagged(range(PAIRS), up, down, 2, 1)
                ct_free[g % 2] = [PE.last()]
                xs_free = [PE.last()]
                xn_read(g * GT, GT)

            for g in range(GROUPS):
                yield unit(g)

        stages = {"L0x": (retention, 4, "B", "CE", 1), "L0f": (moe_gelu, 4, "A", "DW", 2),
                  "L1x": (bidaf, 8, "", "E", 1), "L1f": (moe_swiglu, 4, "B", "C", 1.5),
                  "L2x": (attention16, 8, "AE", "AE", 1), "L2f": (bitnet, 8, "", "CD", 1),
                  "L3x": (attention8, 8, "BW", "E", 1, "CD"), "L3f": (moe_small, 4, "A", "G", .75)}

        def run_all(order):
            gens, units, load, work, steps, more = zip(*((stages[name] + ("",))[0:6] for name in order))
            gens = [g() for g in gens]
            N = len(order)
            uses = [set(load[k] + work[k] + more[k]) | set("" if order[k][1] == "3" else "G") for k in range(N)]
            asked, left = [False] * N, [False] * N
            started, finished = [0] * N, [0] * N
            active = []

            def vacant(n, names):
                return not any(uses[k] & set(names) and not left[k] for k in range(n))

            def ask():
                for n in range(N):
                    if not asked[n]:
                        if not all(asked[:n]) or not vacant(n, load[n]):
                            return
                        assert next(gens[n]) == "loaded"
                        asked[n] = True
                        if not ctxt_in:
                            ctxt_in.append(load_group("ctxt", [(ctxt, c_v)]))

            def start():
                for n in reversed(range(N)):
                    mine = [a for a in active if a[1] == n]
                    if (asked[n] and started[n] < units[n] and len(mine) < 2
                            and vacant(n, work[n] + (more[n] if started[n] else ""))
                            and all(a[2] for a in mine)
                            and (n == 0 or finished[n - 1] * units[n] >= (started[n] + 1) * units[n - 1])):
                        active.append([next(gens[n]), n, False, 0.0])
                        started[n] += 1
                        return True
                return False

            ask()
            while start() or active:
                active.sort(key=lambda a: a[1])
                for entry in list(active):
                    unit, n, second, _ = entry
                    if second and entry is not next(a for a in active if a[1] == n):
                        continue
                    if second and not vacant(n, more[n]):
                        continue
                    entry[3] += steps[n]
                    while entry[3] >= 1:
                        entry[3] -= 1
                        v = next(unit, "end")
                        if v == "end":
                            active.remove(entry)
                            finished[n] += 1
                            if finished[n] == units[n]:
                                leave(*uses[n])
                                left[n] = True
                                ask()
                        elif v == "next":
                            entry[2] = True
                        if v:
                            break

        run_all(LAYERS)
        stored = sem("stored")
        out_v = out.rearrange("b (u p) d -> p (b u) d", p=P)
        for g in range(GROUPS):
            ts = slice(g * GT, (g + 1) * GT)
            SYNC.wait(*x_ready[ts])
            SYNC.eng.dma_start(out_v[:, ts, :], x[:, ts, :]).then_inc(stored, 16)
        SYNC.eng.wait_ge(stored, 16 * GROUPS)


def constants():
    c = {}
    c["c_ident"] = np.eye(P, dtype=np.float32)
    H, HD = 16, 8
    half = HD // 2
    pair = np.repeat(np.arange(half), 2)
    base = (np.arange(0, HD, 2) + 0.4 * HD) / (1.4 * HD)
    power = (np.arange(-(S // 2), S // 2)) / 512.0
    scale = base[None, :] ** power[:, None]
    ang = (np.arange(S, dtype=np.float32)[:, None]
           * (1.0 / 10000.0 ** (np.arange(half, dtype=np.float32) / half)).astype(np.float32)[None, :]).astype(np.float64)
    gam = (1.0 - np.exp(np.linspace(np.log(1 / 32.0), np.log(1 / 512.0), H)).astype(np.float32)).astype(np.float64)
    mid = np.arange(S) - S // 2
    sign = np.where(np.arange(HD) % 2 == 0, -1.0, 1.0)
    tab = np.zeros((P, 4, S))
    for h in range(H):
        for e in range(HD):
            p = h * HD + e
            for side, (sc, dec) in enumerate(((scale[:, pair[e]], gam[h] ** mid), (1 / scale[:, pair[e]], gam[h] ** -mid))):
                tab[p, 2 * side] = np.cos(ang[:, pair[e]]) * sc * dec
                tab[p, 2 * side + 1] = np.sin(ang[:, pair[e]]) * sc * dec * sign[e]
    c["c_xpos"] = tab.astype(np.float32)
    m = np.zeros((P, 16 + P + 512), np.float32)
    p = np.arange(P)
    m[:, 0:16] = p[:, None] // HD == np.arange(16)[None, :]
    m[:, 16:16 + P] = p[:, None] // HD == p[None, :] // HD
    m[:, 16 + P:] = np.tile(p[None, :] >= p[:, None], (1, 4))
    c["c_retmask"] = m
    one = np.uint16(0x3F80)
    c["c_sel24"] = ((p[:, None] % 8 == np.arange(512)[None, :] // 64) & (p[:, None] < 24)) * one
    c["c_par2"] = (p[:, None] // 64 == np.arange(2)[None, :]).astype(np.float32)
    c["c_blk8"] = (p[:, None] // 64 + 8 == np.arange(P + 8)[None, :]).astype(np.float32)
    c["c_sel96"] = ((p[:, None] % 32 == np.arange(2048)[None, :] // 64) & (p[:, None] < 96)) * one
    return c


def layout(i):
    n = {k: np.asarray(v) for k, v in i.items()}
    f = dict(constants())
    f["x"], f["ctx_1024"] = n["x"], n["ctx_1024"]
    f["ctxT"] = n["ctx_1024"].reshape(B * S, D).T
    heads = lambda w: w.transpose(1, 0, 2).reshape(D, D)
    swap = np.arange(D) ^ 1
    wq, wk, wv = (heads(n["L0_xattn_W_" + c]) for c in "QKV")
    f["w_ret"] = np.stack([wq, wq[:, swap], wk, wk[:, swap], wv, n["L0_xattn_g_w"].T, n["L0_xattn_out_w"].T], axis=1)
    f["rows_ret"] = np.stack([n["L0_xattn_g_b"], n["L0_xattn_out_b"]])[None]
    wide = lambda w: np.concatenate([w, np.zeros((w.shape[0], P - w.shape[1]), w.dtype)], axis=1)
    f["r0_w"], f["r0_b"] = wide(n["L0_ffn_router_w"].T), wide(n["L0_ffn_router_b"][None])
    f["e0_w1"] = n["L0_ffn_w1"].transpose(2, 0, 1).reshape(D, -1)
    f["e0_b1"] = n["L0_ffn_b1"].reshape(8, 4, P).transpose(2, 0, 1).reshape(P, 32)
    f["e0_w2"] = n["L0_ffn_w2"].reshape(8, D, 4, P).transpose(3, 0, 2, 1).reshape(P, -1)
    f["e0_b2"] = n["L0_ffn_b2"]
    f["l1_W"] = n["L1_xattn_W_l"].reshape(D, 4, D).transpose(2, 1, 0)
    f["l1_cols"] = np.stack([n["L1_xattn_w_cq"], n["L1_xattn_w_q"], n["L1_xattn_w_c"]], axis=1)
    f["l1_bias"] = np.broadcast_to(np.stack([n["L1_xattn_b_c"], n["L1_xattn_b_q"], n["L1_xattn_b_cq"]])[None], (P, 3))
    f["l1_row"] = n["L1_xattn_b_l"][None]
    f["r1_w"] = wide(n["L1_ffn_Wr"])
    for a, b in (("g", "Wg"), ("u", "Wu")):
        f["e1_" + a] = np.concatenate([n["L1_ffn_" + b], n["L1_ffn_" + b + "_s"][None]]).transpose(1, 0, 2).reshape(D, -1)
    wd = np.concatenate([n["L1_ffn_Wd"], n["L1_ffn_Wd_s"][None]])
    f["e1_d"] = wd.reshape(8, 4, P, D).transpose(2, 0, 1, 3).reshape(P, -1)
    f["l2_w"] = np.stack([n["L2_xattn_W" + c].T for c in "qkv"], axis=1)
    f["l2_wo"] = n["L2_xattn_Wo"].T
    f["l2_cols"] = np.stack([n["L2_xattn_bq"], n["L2_xattn_bk"]], axis=1)
    f["l2_rows"] = np.stack([n["L2_xattn_bv"], n["L2_xattn_bo"]])[None]
    f["mask_row"] = np.broadcast_to(n["mask_BxS2_ik0"].reshape(1, -1), (P, B * S))
    f["mask_cols"] = n["mask_BxS2_ik0"].reshape(TILES, P).T
    f["b_w"] = np.stack([n["L2_ffn_w1"].T, n["L2_ffn_w2"].reshape(D, 4, P).transpose(2, 1, 0).reshape(P, -1)], axis=1)
    f["b_conv"] = np.concatenate([n["L2_ffn_conv_w"].reshape(4, P, 3), n["L2_ffn_conv_b"].reshape(4, P, 1)],
                                 axis=2).transpose(1, 0, 2)
    f["l3_w"] = np.concatenate([n["L3_xattn_Wq"], n["L3_xattn_Wkv"],
                                n["L3_xattn_Wo"].reshape(4, P, D).transpose(1, 0, 2).reshape(P, -1)], axis=1)
    two = lambda v: np.tile(v, 2)
    f["l3_cols"] = np.stack([n["L3_xattn_ln_x_w"], n["L3_xattn_ln_x_b"], n["L3_xattn_ln_l_w"], n["L3_xattn_ln_l_b"],
                             two(n["L3_xattn_q_scale"]), two(n["L3_xattn_k_scale"])], axis=1)
    f["l3_lno"] = np.broadcast_to(np.stack([n["L3_xattn_ln_o_w"], n["L3_xattn_ln_o_b"]])[None], (P, 2, D))
    keep = n["mask_BxS2_bk0"]
    f["bmask_row"], f["bmask_cols"] = np.broadcast_to(keep.reshape(1, -1), (P, B * S)), keep.reshape(TILES, P).T
    f["r3_w"] = wide(np.concatenate([n["L3_ffn_router_w0"], n["L3_ffn_router_w1"]], axis=1))
    for a, b in (("g", "wg"), ("u", "wu")):
        f["e3_" + a] = np.concatenate([n[f"L3_ffn_{b}{r}"] for r in range(2)]).transpose(1, 0, 2).reshape(D, -1)
    f["e3_d"] = np.concatenate([n[f"L3_ffn_wd{r}"] for r in range(2)]).reshape(32, P, D).transpose(1, 0, 2).reshape(P, -1)
    return {k: np.ascontiguousarray(v) for k, v in f.items()}


def kernel(**inputs):
    import concourse.bacc as bacc
    from concourse.bass_utils import run_bass_kernel_spmd

    arrays = layout(inputs)
    nc = bacc.Bacc("TRN2", target_bir_lowering=False, num_devices=1)
    aps = {k: nc.dram_tensor(k + "_dram", a.shape, mybir.dt.from_np(a.dtype), kind="ExternalInput").ap()
           for k, a in arrays.items()}
    out = nc.dram_tensor("out_dram", (B, S, D), F32, kind="ExternalOutput").ap()
    build(nc, aps, out)
    r = run_bass_kernel_spmd(nc, [{k + "_dram": a for k, a in arrays.items()}], core_ids=[0])
    return r.results[0]["out_dram"]
```
